# Optimizing a Trainium2 kernel written in Bass

```python
import numpy as np
import jax
import jax.numpy as jnp

def _softmax(x, axis=-1):
    return jax.nn.softmax(x, axis=axis)

def _gelu(x):
    return jax.nn.gelu(x, approximate=True)

def _silu(x):
    return jax.nn.silu(x)

def _sigmoid(x):
    return jax.nn.sigmoid(x)

def _layernorm(x, axis=-1, eps=1e-05):
    m = jnp.mean(x, axis=axis, keepdims=True)
    v = jnp.var(x, axis=axis, keepdims=True)
    return (x - m) / jnp.sqrt(v + eps)

def _scatter_add(tgt, idx, src, axis=0):
    return tgt.at[idx].add(src)

def _segment_sum(src, seg, n):
    return jax.ops.segment_sum(src, seg, n)
kernel_name = 'mk_flamingo_gated_d2_seqx_r8_5d0f57'

def setup_inputs(seed: int=0):
    np.random.seed(seed)
    _w = jnp.asarray

    def _rec_inputs():
        import jax
        import jax.numpy as jnp
        _rk = jax.random.key(seed)
        x = 7.22e-05 + 1 * jax.random.normal(jax.random.fold_in(_rk, 1), (8, 256, 128), jnp.float32)
        _lenS = 256 - jax.random.randint(jax.random.fold_in(_rk, 7), (8,), 0, max(1, 256 // 4) + 1, jnp.int32)
        _lenS2 = 256 - jax.random.randint(jax.random.fold_in(_rk, 8), (8,), 0, max(1, 256 // 4) + 1, jnp.int32)
        _ctx_1024P = jax.random.normal(jax.random.fold_in(_rk, 11), (8, 16, 128), jnp.float32)
        _ctx_1024c = jax.random.dirichlet(jax.random.fold_in(_rk, 511), 0.3 * jnp.ones((16,), jnp.float32), (8, 256))
        _ctx_1024t = jnp.einsum('bsk,bkd->bsd', _ctx_1024c, _ctx_1024P)
        _ctx_1024t = _ctx_1024t * jax.lax.rsqrt(jnp.mean(jnp.square(_ctx_1024t)) + 1e-12) * 0.953939
        ctx_1024 = 4.13588e-05 + 0.999923 * (_ctx_1024t + 0.3 * jax.random.normal(jax.random.fold_in(_rk, 611), (8, 256, 128), jnp.float32))
        _g = jax.random.normal(jax.random.fold_in(_rk, 9001), (2, 2), jnp.float32)
        _g = jnp.sign(_g) * jnp.maximum(jnp.abs(_g), 1.0) + (_g == 0) * 1.0
        g_xattn = _g[0]
        g_ffn = _g[1]
        return (x, ctx_1024, g_xattn, g_ffn)
    x, ctx_1024, g_xattn, g_ffn = _rec_inputs()

    def _L0_xattn_setup():
        import jax, jax.numpy as jnp
        import numpy as np
        D_MODEL = 128
        NUM_HEADS = 16
        HEAD_DIM = D_MODEL // NUM_HEADS
        B, S = (4, 256)
        key = jax.random.key(seed)
        ks = jax.random.split(key, 6)
        scale = 1.0 / np.sqrt(D_MODEL)
        return {'q': jax.random.normal(ks[0], (B, S, D_MODEL), dtype=jnp.float32), 'k': jax.random.normal(ks[1], (B, S, D_MODEL), dtype=jnp.float32), 'v': jax.random.normal(ks[2], (B, S, D_MODEL), dtype=jnp.float32), 'Wq': jax.random.normal(ks[3], (D_MODEL, D_MODEL), dtype=jnp.float32) * scale, 'Wk': jax.random.normal(ks[4], (D_MODEL, D_MODEL), dtype=jnp.float32) * scale, 'Wv': jax.random.normal(ks[5], (D_MODEL, D_MODEL), dtype=jnp.float32) * scale}
    _L0_xattn_all = _L0_xattn_setup()
    _L0_xattn_in = {k: v for k, v in _L0_xattn_all.items() if k in ('Wq', 'Wk', 'Wv')}
    del _L0_xattn_all

    def _L0_ffn_setup():
        import jax, jax.numpy as jnp
        import numpy as np
        DIM = 128
        DEPTH = 2
        HEADS = 8
        DIM_HEAD = 64
        WINDOW = 64
        INNER = HEADS * DIM_HEAD
        HID = int(DIM * 4 * 2 / 3)
        B, N = (2, 1024)
        QK_SCALE = 8.0

        def shift_token(t):
            t1, t2 = jnp.split(t, 2, axis=-1)
            t2 = jnp.pad(t2, ((0, 0), (1, 0), (0, 0)))[:, :-1]
            return jnp.concatenate([t1, t2], axis=-1)

        def l2norm(t):
            return t / jnp.clip(jnp.linalg.norm(t, axis=-1, keepdims=True), 1e-12)

        def rotate_half(x):
            x1, x2 = jnp.split(x, 2, axis=-1)
            return jnp.concatenate([-x2, x1], axis=-1)

        def rotary_xpos(q, k):
            n = q.shape[-2]
            half_idx = jnp.arange(0, DIM_HEAD, 2, dtype=jnp.float32)
            inv_freq = 1.0 / 10000.0 ** (half_idx / DIM_HEAD)
            t = jnp.arange(n, dtype=jnp.float32)
            freqs = t[:, None] * inv_freq[None, :]
            freqs = jnp.concatenate([freqs, freqs], axis=-1)
            base = (half_idx + 0.4 * DIM_HEAD) / (1.4 * DIM_HEAD)
            power = (t - n // 2) / float(WINDOW // 2)
            scale = base[None, :] ** power[:, None]
            scale = jnp.concatenate([scale, scale], axis=-1)
            cos, sin = (jnp.cos(freqs), jnp.sin(freqs))
            q = q * cos * scale + rotate_half(q) * sin * scale
            k = k * cos / scale + rotate_half(k) * sin / scale
            return (q, k)

        def local_attention(q, k, v):
            b, h, n, d = q.shape
            w = n // WINDOW
            bq = q.reshape(b, h, w, WINDOW, d) * QK_SCALE
            bk = k.reshape(b, h, w, WINDOW, d)
            bv = v.reshape(b, h, w, WINDOW, d)

            def look_around(t):
                p = jnp.pad(t, ((0, 0), (0, 0), (1, 0), (0, 0), (0, 0)))
                return jnp.concatenate([p[:, :, :w], p[:, :, 1:]], axis=3)
            bk, bv = (look_around(bk), look_around(bv))
            bt = jnp.arange(n).reshape(w, WINDOW)
            btp = jnp.pad(bt, ((1, 0), (0, 0)), constant_values=-1)
            btk = jnp.concatenate([btp[:w], btp[1:]], axis=1)
            sim = jnp.einsum('bhwid,bhwjd->bhwij', bq, bk)
            i = bt[:, :, None]
            j = btk[:, None, :]
            mask = (i < j) | (i > j + WINDOW) | (j == -1)
            sim = jnp.where(mask, -jnp.finfo(sim.dtype).max, sim)
            attn = jax.nn.softmax(sim, axis=-1)
            out = jnp.einsum('bhwij,bhwjd->bhwid', attn, bv)
            return out.reshape(b, h, n, d)

        def _layer(x, wqkv, qs, ksc, wo, lg, lb, w1, b1, w2, b2):
            b, n, _ = x.shape
            h = shift_token(x)
            qkv = h @ wqkv
            q, k, v = jnp.split(qkv, 3, axis=-1)
            to_heads = lambda t: t.reshape(b, n, HEADS, DIM_HEAD).transpose(0, 2, 1, 3)
            q, k, v = (to_heads(q), to_heads(k), to_heads(v))
            q = l2norm(q) * qs
            k = l2norm(k) * ksc
            q, k = rotary_xpos(q, k)
            o = local_attention(q, k, v)
            o = o.transpose(0, 2, 1, 3).reshape(b, n, INNER)
            x = x + o @ wo
            h = shift_token(x)
            mu = h.mean(-1, keepdims=True)
            var = h.var(-1, keepdims=True)
            h = (h - mu) / jnp.sqrt(var + 1e-05) * lg + lb
            h = h @ w1 + b1
            a, g = jnp.split(h, 2, axis=-1)
            h = a * jax.nn.gelu(g, approximate=False)
            x = x + h @ w2 + b2
            return x
        key = jax.random.key(seed)
        ks = jax.random.split(key, 6)
        return {'x': jax.random.normal(ks[0], (B, N, DIM), jnp.float32), 'wqkv': jax.random.normal(ks[1], (DEPTH, DIM, 3 * INNER), jnp.float32) * 0.02, 'q_scale': jnp.ones((DEPTH, DIM_HEAD), jnp.float32), 'k_scale': jnp.ones((DEPTH, DIM_HEAD), jnp.float32), 'wo': jax.random.normal(ks[2], (DEPTH, INNER, DIM), jnp.float32) * 0.02, 'ln_g': jnp.ones((DEPTH, DIM), jnp.float32), 'ln_b': jnp.zeros((DEPTH, DIM), jnp.float32), 'w1': jax.random.normal(ks[3], (DEPTH, DIM, 2 * HID), jnp.float32) * 0.02, 'b1': jnp.zeros((DEPTH, 2 * HID), jnp.float32), 'w2': jax.random.normal(ks[4], (DEPTH, HID, DIM), jnp.float32) * 0.02, 'b2': jnp.zeros((DEPTH, DIM), jnp.float32)}
    _L0_ffn_all = _L0_ffn_setup()
    _L0_ffn_in = {k: v for k, v in _L0_ffn_all.items() if k in ('wqkv', 'q_scale', 'k_scale', 'wo', 'ln_g', 'ln_b', 'w1', 'b1', 'w2', 'b2')}
    del _L0_ffn_all

    def _L1_xattn_setup():
        import jax, jax.numpy as jnp
        import numpy as np
        D_MODEL = 128
        N_HEADS = 16
        HEAD_D = D_MODEL // N_HEADS
        B, L = (4, 256)
        EPS_CAUSAL = 1e-06

        def _feat(x):
            return jax.nn.elu(x) + 1.0

        def _causal_linear_attn(qs, ks, vs):

            def step(carry, xs):
                Si, Zi = carry
                q, k, v = xs
                Si = Si + jnp.einsum('bhd,bhk->bhdk', k, v)
                Zi = Zi + k
                num = jnp.einsum('bhd,bhkd->bhk', q, Si)
                Vi = num / (q * Zi + EPS_CAUSAL)
                return ((Si, Zi), Vi)
            Bn, Ln, H, D = qs.shape
            K = vs.shape[-1]
            Si0 = jnp.zeros((Bn, H, D, K), qs.dtype)
            Zi0 = jnp.zeros((Bn, H, D), qs.dtype)
            xs = (jnp.swapaxes(qs, 0, 1), jnp.swapaxes(ks, 0, 1), jnp.swapaxes(vs, 0, 1))
            _, out = jax.lax.scan(step, (Si0, Zi0), xs)
            return jnp.swapaxes(out, 0, 1)
        key = jax.random.key(seed)
        ks = jax.random.split(key, 11)
        s = 1.0 / np.sqrt(D_MODEL)
        inp = {'queries': jax.random.normal(ks[0], (B, L, D_MODEL), jnp.float32), 'keys': jax.random.normal(ks[1], (B, L, D_MODEL), jnp.float32), 'values': jax.random.normal(ks[2], (B, L, D_MODEL), jnp.float32), 'Wq': jax.random.uniform(ks[3], (D_MODEL, N_HEADS * HEAD_D), jnp.float32, -s, s), 'bq': jax.random.uniform(ks[4], (N_HEADS * HEAD_D,), jnp.float32, -s, s), 'Wk': jax.random.uniform(ks[5], (D_MODEL, N_HEADS * HEAD_D), jnp.float32, -s, s), 'bk': jax.random.uniform(ks[6], (N_HEADS * HEAD_D,), jnp.float32, -s, s), 'Wv': jax.random.uniform(ks[7], (D_MODEL, N_HEADS * HEAD_D), jnp.float32, -s, s), 'bv': jax.random.uniform(ks[8], (N_HEADS * HEAD_D,), jnp.float32, -s, s), 'Wo': jax.random.uniform(ks[9], (D_MODEL, D_MODEL), jnp.float32, -s, s), 'bo': jax.random.uniform(ks[10], (D_MODEL,), jnp.float32, -s, s)}
        return inp
    _L1_xattn_all = _L1_xattn_setup()
    _L1_xattn_in = {k: v for k, v in _L1_xattn_all.items() if k in ('Wq', 'bq', 'Wk', 'bk', 'Wv', 'bv', 'Wo', 'bo')}
    del _L1_xattn_all

    def _L1_ffn_setup():
        import jax, jax.numpy as jnp
        import numpy as np
        H, I, E, K = (128, 64, 32, 8)
        B, S = (4, 128)

        def silu(x):
            return x * jax.nn.sigmoid(x)
        key = jax.random.key(seed)
        ks = jax.random.split(key, 14)

        def w(k, shape, fan_in):
            return jax.random.normal(k, shape, jnp.float32) / np.float32(np.sqrt(fan_in))
        return {'hidden_states': jax.random.normal(ks[0], (B, S, H), jnp.float32), 'Wr': w(ks[1], (H, E), H), 'br': jnp.zeros((E,), jnp.float32), 'Wg_s': w(ks[2], (H, I), H), 'bg_s': jnp.zeros((I,), jnp.float32), 'Wu_s': w(ks[3], (H, I), H), 'bu_s': jnp.zeros((I,), jnp.float32), 'Wd_s': w(ks[4], (I, H), I), 'bd_s': jnp.zeros((H,), jnp.float32), 'Wg': w(ks[5], (E, H, I), H), 'bg': jnp.zeros((E, I), jnp.float32), 'Wu': w(ks[6], (E, H, I), H), 'bu': jnp.zeros((E, I), jnp.float32), 'Wd': w(ks[7], (E, I, H), I), 'bd': jnp.zeros((E, H), jnp.float32)}
    _L1_ffn_all = _L1_ffn_setup()
    _L1_ffn_in = {k: v for k, v in _L1_ffn_all.items() if k in ('Wr', 'br', 'Wg_s', 'bg_s', 'Wu_s', 'bu_s', 'Wd_s', 'bd_s', 'Wg', 'bg', 'Wu', 'bu', 'Wd', 'bd')}
    del _L1_ffn_all
    return {'x': x, 'ctx_1024': ctx_1024, 'g_xattn': g_xattn, 'g_ffn': g_ffn, 'L0_xattn_Wq': _L0_xattn_in['Wq'], 'L0_xattn_Wk': _L0_xattn_in['Wk'], 'L0_xattn_Wv': _L0_xattn_in['Wv'], 'L0_ffn_wqkv': _L0_ffn_in['wqkv'], 'L0_ffn_q_scale': _L0_ffn_in['q_scale'], 'L0_ffn_k_scale': _L0_ffn_in['k_scale'], 'L0_ffn_wo': _L0_ffn_in['wo'], 'L0_ffn_ln_g': _L0_ffn_in['ln_g'], 'L0_ffn_ln_b': _L0_ffn_in['ln_b'], 'L0_ffn_w1': _L0_ffn_in['w1'], 'L0_ffn_b1': _L0_ffn_in['b1'], 'L0_ffn_w2': _L0_ffn_in['w2'], 'L0_ffn_b2': _L0_ffn_in['b2'], 'L1_xattn_Wq': _L1_xattn_in['Wq'], 'L1_xattn_bq': _L1_xattn_in['bq'], 'L1_xattn_Wk': _L1_xattn_in['Wk'], 'L1_xattn_bk': _L1_xattn_in['bk'], 'L1_xattn_Wv': _L1_xattn_in['Wv'], 'L1_xattn_bv': _L1_xattn_in['bv'], 'L1_xattn_Wo': _L1_xattn_in['Wo'], 'L1_xattn_bo': _L1_xattn_in['bo'], 'L1_ffn_Wr': _L1_ffn_in['Wr'], 'L1_ffn_br': _L1_ffn_in['br'], 'L1_ffn_Wg_s': _L1_ffn_in['Wg_s'], 'L1_ffn_bg_s': _L1_ffn_in['bg_s'], 'L1_ffn_Wu_s': _L1_ffn_in['Wu_s'], 'L1_ffn_bu_s': _L1_ffn_in['bu_s'], 'L1_ffn_Wd_s': _L1_ffn_in['Wd_s'], 'L1_ffn_bd_s': _L1_ffn_in['bd_s'], 'L1_ffn_Wg': _L1_ffn_in['Wg'], 'L1_ffn_bg': _L1_ffn_in['bg'], 'L1_ffn_Wu': _L1_ffn_in['Wu'], 'L1_ffn_bu': _L1_ffn_in['bu'], 'L1_ffn_Wd': _L1_ffn_in['Wd'], 'L1_ffn_bd': _L1_ffn_in['bd']}

def reference(x, ctx_1024, g_xattn, g_ffn, L0_xattn_Wq, L0_xattn_Wk, L0_xattn_Wv, L0_ffn_wqkv, L0_ffn_q_scale, L0_ffn_k_scale, L0_ffn_wo, L0_ffn_ln_g, L0_ffn_ln_b, L0_ffn_w1, L0_ffn_b1, L0_ffn_w2, L0_ffn_b2, L1_xattn_Wq, L1_xattn_bq, L1_xattn_Wk, L1_xattn_bk, L1_xattn_Wv, L1_xattn_bv, L1_xattn_Wo, L1_xattn_bo, L1_ffn_Wr, L1_ffn_br, L1_ffn_Wg_s, L1_ffn_bg_s, L1_ffn_Wu_s, L1_ffn_bu_s, L1_ffn_Wd_s, L1_ffn_bd_s, L1_ffn_Wg, L1_ffn_bg, L1_ffn_Wu, L1_ffn_bu, L1_ffn_Wd, L1_ffn_bd):
    import jax
    import jax.numpy as jnp

    def _L0_xattn_ref(q, k, v, Wq, Wk, Wv):
        import jax, jax.numpy as jnp
        import numpy as np
        D_MODEL = 128
        NUM_HEADS = 16
        HEAD_DIM = D_MODEL // NUM_HEADS
        B, S = (4, 256)
        b, s, d = q.shape
        qp = jnp.einsum('bsd,ed->bse', q, Wq)
        kp = jnp.einsum('bsd,ed->bse', k, Wk)
        vp = jnp.einsum('bsd,ed->bse', v, Wv)
        qh = qp.reshape(b, s, NUM_HEADS, HEAD_DIM).transpose(0, 2, 1, 3)
        kh = kp.reshape(b, s, NUM_HEADS, HEAD_DIM).transpose(0, 2, 1, 3)
        vh = vp.reshape(b, s, NUM_HEADS, HEAD_DIM).transpose(0, 2, 1, 3)
        scores = jnp.einsum('bhqd,bhkd->bhqk', qh, kh) / jnp.sqrt(jnp.float32(HEAD_DIM))
        attn = jax.nn.softmax(scores, axis=-1)
        att = jnp.einsum('bhqk,bhkd->bhqd', attn, vh)
        return att.reshape(b, s, d)

    def _L0_ffn_ref(x, wqkv, q_scale, k_scale, wo, ln_g, ln_b, w1, b1, w2, b2):
        import jax, jax.numpy as jnp
        import numpy as np
        DIM = 128
        DEPTH = 2
        HEADS = 8
        DIM_HEAD = 64
        WINDOW = 64
        INNER = HEADS * DIM_HEAD
        HID = int(DIM * 4 * 2 / 3)
        B, N = (2, 1024)
        QK_SCALE = 8.0

        def shift_token(t):
            t1, t2 = jnp.split(t, 2, axis=-1)
            t2 = jnp.pad(t2, ((0, 0), (1, 0), (0, 0)))[:, :-1]
            return jnp.concatenate([t1, t2], axis=-1)

        def l2norm(t):
            return t / jnp.clip(jnp.linalg.norm(t, axis=-1, keepdims=True), 1e-12)

        def rotate_half(x):
            x1, x2 = jnp.split(x, 2, axis=-1)
            return jnp.concatenate([-x2, x1], axis=-1)

        def rotary_xpos(q, k):
            n = q.shape[-2]
            half_idx = jnp.arange(0, DIM_HEAD, 2, dtype=jnp.float32)
            inv_freq = 1.0 / 10000.0 ** (half_idx / DIM_HEAD)
            t = jnp.arange(n, dtype=jnp.float32)
            freqs = t[:, None] * inv_freq[None, :]
            freqs = jnp.concatenate([freqs, freqs], axis=-1)
            base = (half_idx + 0.4 * DIM_HEAD) / (1.4 * DIM_HEAD)
            power = (t - n // 2) / float(WINDOW // 2)
            scale = base[None, :] ** power[:, None]
            scale = jnp.concatenate([scale, scale], axis=-1)
            cos, sin = (jnp.cos(freqs), jnp.sin(freqs))
            q = q * cos * scale + rotate_half(q) * sin * scale
            k = k * cos / scale + rotate_half(k) * sin / scale
            return (q, k)

        def local_attention(q, k, v):
            b, h, n, d = q.shape
            w = n // WINDOW
            bq = q.reshape(b, h, w, WINDOW, d) * QK_SCALE
            bk = k.reshape(b, h, w, WINDOW, d)
            bv = v.reshape(b, h, w, WINDOW, d)

            def look_around(t):
                p = jnp.pad(t, ((0, 0), (0, 0), (1, 0), (0, 0), (0, 0)))
                return jnp.concatenate([p[:, :, :w], p[:, :, 1:]], axis=3)
            bk, bv = (look_around(bk), look_around(bv))
            bt = jnp.arange(n).reshape(w, WINDOW)
            btp = jnp.pad(bt, ((1, 0), (0, 0)), constant_values=-1)
            btk = jnp.concatenate([btp[:w], btp[1:]], axis=1)
            sim = jnp.einsum('bhwid,bhwjd->bhwij', bq, bk)
            i = bt[:, :, None]
            j = btk[:, None, :]
            mask = (i < j) | (i > j + WINDOW) | (j == -1)
            sim = jnp.where(mask, -jnp.finfo(sim.dtype).max, sim)
            attn = jax.nn.softmax(sim, axis=-1)
            out = jnp.einsum('bhwij,bhwjd->bhwid', attn, bv)
            return out.reshape(b, h, n, d)

        def _layer(x, wqkv, qs, ksc, wo, lg, lb, w1, b1, w2, b2):
            b, n, _ = x.shape
            h = shift_token(x)
            qkv = h @ wqkv
            q, k, v = jnp.split(qkv, 3, axis=-1)
            to_heads = lambda t: t.reshape(b, n, HEADS, DIM_HEAD).transpose(0, 2, 1, 3)
            q, k, v = (to_heads(q), to_heads(k), to_heads(v))
            q = l2norm(q) * qs
            k = l2norm(k) * ksc
            q, k = rotary_xpos(q, k)
            o = local_attention(q, k, v)
            o = o.transpose(0, 2, 1, 3).reshape(b, n, INNER)
            x = x + o @ wo
            h = shift_token(x)
            mu = h.mean(-1, keepdims=True)
            var = h.var(-1, keepdims=True)
            h = (h - mu) / jnp.sqrt(var + 1e-05) * lg + lb
            h = h @ w1 + b1
            a, g = jnp.split(h, 2, axis=-1)
            h = a * jax.nn.gelu(g, approximate=False)
            x = x + h @ w2 + b2
            return x
        for l in range(DEPTH):
            x = _layer(x, wqkv[l], q_scale[l], k_scale[l], wo[l], ln_g[l], ln_b[l], w1[l], b1[l], w2[l], b2[l])
        return x

    def _L1_xattn_ref(queries, keys, values, Wq, bq, Wk, bk, Wv, bv, Wo, bo):
        import jax, jax.numpy as jnp
        import numpy as np
        D_MODEL = 128
        N_HEADS = 16
        HEAD_D = D_MODEL // N_HEADS
        B, L = (4, 256)
        EPS_CAUSAL = 1e-06

        def _feat(x):
            return jax.nn.elu(x) + 1.0

        def _causal_linear_attn(qs, ks, vs):

            def step(carry, xs):
                Si, Zi = carry
                q, k, v = xs
                Si = Si + jnp.einsum('bhd,bhk->bhdk', k, v)
                Zi = Zi + k
                num = jnp.einsum('bhd,bhkd->bhk', q, Si)
                Vi = num / (q * Zi + EPS_CAUSAL)
                return ((Si, Zi), Vi)
            Bn, Ln, H, D = qs.shape
            K = vs.shape[-1]
            Si0 = jnp.zeros((Bn, H, D, K), qs.dtype)
            Zi0 = jnp.zeros((Bn, H, D), qs.dtype)
            xs = (jnp.swapaxes(qs, 0, 1), jnp.swapaxes(ks, 0, 1), jnp.swapaxes(vs, 0, 1))
            _, out = jax.lax.scan(step, (Si0, Zi0), xs)
            return jnp.swapaxes(out, 0, 1)
        N, Lq, _ = queries.shape
        H = N_HEADS
        Q = (queries @ Wq + bq).reshape(N, Lq, H, -1)
        Kp = (keys @ Wk + bk).reshape(N, keys.shape[1], H, -1)
        V = (values @ Wv + bv).reshape(N, values.shape[1], H, -1)
        Q_lin = _feat(Q)
        K_lin = _feat(Kp)
        V_lin = _causal_linear_attn(Q_lin, K_lin, V)
        new_values = V_lin.reshape(N, Lq, -1)
        return new_values @ Wo + bo

    def _L1_ffn_ref(hidden_states, Wr, br, Wg_s, bg_s, Wu_s, bu_s, Wd_s, bd_s, Wg, bg, Wu, bu, Wd, bd):
        import jax, jax.numpy as jnp
        import numpy as np
        H, I, E, K = (128, 64, 32, 8)
        B, S = (4, 128)

        def silu(x):
            return x * jax.nn.sigmoid(x)
        b, s, h = hidden_states.shape
        T = b * s
        x = hidden_states.reshape(T, h)
        logits = jnp.dot(x.astype(jnp.float32), Wr) + br
        aff = jax.nn.sigmoid(logits)
        top_v, top_i = jax.lax.top_k(aff, K)
        top_w = top_v / (jnp.sum(top_v, axis=-1, keepdims=True) + 1e-09)
        top_w = top_w.astype(hidden_states.dtype)
        e_total = Wr.shape[1]
        w_full = jnp.zeros((T, e_total), hidden_states.dtype)
        w_full = w_full.at[jnp.arange(T)[:, None], top_i].set(top_w)
        shared = jnp.dot(silu(jnp.dot(x, Wg_s) + bg_s) * (jnp.dot(x, Wu_s) + bu_s), Wd_s) + bd_s
        gate = silu(jnp.einsum('th,ehi->eti', x, Wg) + bg[:, None, :])
        up = jnp.einsum('th,ehi->eti', x, Wu) + bu[:, None, :]
        down = jnp.einsum('eti,eih->eth', gate * up, Wd) + bd[:, None, :]
        routed = jnp.einsum('te,eth->th', w_full, down)
        return (shared + routed).reshape(b, s, h)
    x = x + jnp.tanh(g_xattn[0]) * _L0_xattn_ref(_layernorm(x, axis=-1), ctx_1024, ctx_1024, L0_xattn_Wq, L0_xattn_Wk, L0_xattn_Wv)
    x = x + jnp.tanh(g_ffn[0]) * _L0_ffn_ref(_layernorm(x, axis=-1), L0_ffn_wqkv, L0_ffn_q_scale, L0_ffn_k_scale, L0_ffn_wo, L0_ffn_ln_g, L0_ffn_ln_b, L0_ffn_w1, L0_ffn_b1, L0_ffn_w2, L0_ffn_b2)
    x = x + jnp.tanh(g_xattn[1]) * _L1_xattn_ref(_layernorm(x, axis=-1), ctx_1024, ctx_1024, L1_xattn_Wq, L1_xattn_bq, L1_xattn_Wk, L1_xattn_bk, L1_xattn_Wv, L1_xattn_bv, L1_xattn_Wo, L1_xattn_bo)
    x = x + jnp.tanh(g_ffn[1]) * _L1_ffn_ref(_layernorm(x, axis=-1), L1_ffn_Wr, L1_ffn_br, L1_ffn_Wg_s, L1_ffn_bg_s, L1_ffn_Wu_s, L1_ffn_bu_s, L1_ffn_Wd_s, L1_ffn_bd_s, L1_ffn_Wg, L1_ffn_bg, L1_ffn_Wu, L1_ffn_bu, L1_ffn_Wd, L1_ffn_bd)
    return x

_drawn_inputs = setup_inputs


def setup_inputs(seed=0):
    import zlib

    import numpy as np

    out = dict(_drawn_inputs(seed))
    spreads = {'g_ffn': (-1.0, 0.2),
     'L0_ffn_q_scale': (1.0, 0.6),
     'L0_ffn_k_scale': (1.0, 0.6),
     'L0_ffn_ln_g': (1.0, 0.6),
     'L0_ffn_ln_b': (0.0, 0.708),
     'L0_ffn_b1': (0.0, 0.1),
     'L0_ffn_b2': (0.0, 0.1),
     'L1_ffn_br': (0.0, 0.1),
     'L1_ffn_bg_s': (0.0, 0.1),
     'L1_ffn_bu_s': (0.0, 0.1),
     'L1_ffn_bd_s': (0.0, 0.1),
     'L1_ffn_bg': (0.0, 0.424),
     'L1_ffn_bu': (0.0, 0.458),
     'L1_ffn_bd': (0.0, 0.1)}
    factors = {'L1_xattn_bk': 5.956}
    for name, (base, spread) in spreads.items():
        noise = np.random.default_rng([zlib.crc32(name.encode()), seed]).standard_normal(out[name].shape)
        drawn = base * np.exp(spread * noise) if base else spread * noise
        out[name] = jnp.asarray(drawn.astype(out[name].dtype))
    for name, factor in factors.items():
        out[name] = (out[name] * factor).astype(out[name].dtype)
    return out
```

```python
from contextlib import ExitStack

import numpy as np
import concourse.bass as bass
from concourse import mybir

F32 = mybir.dt.float32
BF16 = mybir.dt.bfloat16
ALU = mybir.AluOpType
ACT = mybir.ActivationFunctionType
AX_X = mybir.AxisListType.X

B, N, D = 8, 256, 128
NB = 2
TURNS = B // NB
TPB = N // 128
T = NB * TPB
TOK = T * 128
H, DH = 16, 8
SLOT = 64
LH, LD, WIN = 8, 64, 64
LAYERS = 2
INNER = LH * LD
HID = int(D * 4 * 2 / 3)
HCH = [(c, min(128, HID - c)) for c in range(0, HID, 128)]
E, I, TOPK = 32, 64, 8
PAIRS = E // 2
VS = 9 * 9
EPS = 1e-5
NEG = -1.0e30

C_ID, C_CAUSAL, C_ONES, C_MEAN, C_DIAG, C_HEAD, C_ROT = 0, 128, 256, 384, 512, 640, 656
ROTW = TPB * 2 * 2 * LD
C_ALL = C_ROT + ROTW
K_ID, K_MQ, K_MK, K_MAX, K_SEL = 0, 128, 320, 512, 512 + H * 128
K_ALL = K_SEL + PAIRS * 128
V_BG, V_BU = 0, PAIRS
V_LG, V_LB, V_B2 = 2 * PAIRS, 2 * PAIRS + LAYERS, 2 * PAIRS + 2 * LAYERS
V_B1 = V_B2 + LAYERS
V_BO = V_B1 + LAYERS * 2 * len(HCH)
V_BDS, V_BGS, V_BUS, V_ALL = V_BO + 1, V_BO + 2, V_BO + 3, V_BO + 4


def shape_constants():
    p = np.arange(128)[:, None]
    f = np.arange(128)[None, :]
    c = np.zeros((128, C_ALL), np.float32)
    c[:, C_ID:C_ID + 128] = p == f
    c[:, C_CAUSAL:C_CAUSAL + 128] = p <= f
    c[:, C_ONES:C_ONES + 128] = 1
    c[:, C_MEAN:C_MEAN + 128] = 1.0 / D
    c[:, C_DIAG:C_DIAG + 128] = p // DH == f // DH
    c[:, C_HEAD:C_HEAD + H] = p // DH == np.arange(H)[None, :]
    half = np.arange(0, LD, 2, dtype=np.float32)
    inv = np.float32(1.0) / np.float32(10000.0) ** (half / np.float32(LD))
    t = np.arange(N, dtype=np.float32)
    ang = np.concatenate([t[:, None] * inv[None, :]] * 2, 1).astype(np.float32)
    base = ((half + np.float32(0.4 * LD)) / np.float32(1.4 * LD)).astype(np.float32)
    power = (t - N // 2) / np.float32(WIN // 2)
    sc = np.concatenate([base[None, :] ** power[:, None]] * 2, 1).astype(np.float32)
    sign = np.where(np.arange(LD) < LD // 2, -1.0, 1.0).astype(np.float32)[None, :]
    rot = np.zeros((128, TPB, 2, 2, LD), np.float32)
    for tile in range(TPB):
        r = slice(128 * tile, 128 * tile + 128)
        for qk, s in ((0, sc[r]), (1, 1 / sc[r])):
            rot[:, tile, qk, 0] = np.cos(ang[r]) * s
            rot[:, tile, qk, 1] = np.sin(ang[r]) * s * sign
    c[:, C_ROT:] = rot.reshape(128, -1)

    k = np.zeros((128, K_ALL), np.float32)
    k[:, K_ID:K_ID + 128] = p == f
    key = np.arange(WIN + 128)[None, :] - WIN
    k[:, K_MQ:K_MQ + 192] = np.where((key <= p) & (key >= p - WIN), 0, NEG)
    q = np.arange(128 + WIN)[None, :]
    k[:, K_MK:K_MK + 192] = np.where((p <= q) & (q <= p + WIN), 0, NEG)
    for h in range(H):
        for part in range(3):
            k[part * H + h, K_MAX + h * 128:K_MAX + h * 128 + 128] = -1
    for pr in range(PAIRS):
        for part in range(3):
            for e in range(2):
                at = K_SEL + pr * 128 + e * 64
                k[part * E + 2 * pr + e, at:at + 64] = 1
    return c, k


def flamingo(nc, a, out):
    with ExitStack() as ctx:
        def sb(name, shape, dt=F32):
            return ctx.enter_context(nc.sbuf_tensor(name, shape, dt))

        counts, SET = {}, 3
        turn_sems = []

        def sem(name):
            s = ctx.enter_context(nc.semaphore(name))
            turn_sems.append(s)
            return s

        bank = [ctx.enter_context(nc.psum_tensor(f"bank{i}", [128, 512], F32)) for i in range(8)]

        def bbank(i):
            return bank[i][:, :].bitcast(BF16)

        cf = sb("cf", [128, C_ALL])
        cb = sb("cb", [128, K_ALL], BF16)
        ident, causal = cf[:, C_ID:C_ID + 128], cf[:, C_CAUSAL:C_CAUSAL + 128]
        ones, mean = cf[:, C_ONES:C_ONES + 128], cf[:, C_MEAN:C_MEAN + 128]
        diag = cf[:, C_DIAG:C_DIAG + 128]
        identb = cb[:, K_ID:K_ID + 128]
        rot_c = cf[:, C_ROT:].rearrange("p (t k w d) -> p t k w d", t=TPB, k=2, w=2)
        w_a = sb("w_a", [128, 3, 128])
        w_c = sb("w_c", [128, 4, 128])
        row = sb("row", [1, 3 * 128 + E])
        w_qkv = sb("w_qkv", [128, LAYERS, 3 * INNER])
        w_o = sb("w_o", [128, LAYERS, INNER // 128, D])
        w_1 = sb("w_1", [128, LAYERS, 2 * HID])
        w_2 = sb("w_2", [128, LAYERS, len(HCH), D])
        w_r = sb("w_r", [128, E])
        w_gs = sb("w_gs", [128, 2, I])
        w_ds = sb("w_ds", [I, D])
        w_g = sb("w_g", [128, E, I])
        w_u = sb("w_u", [128, E, I])
        w_d = sb("w_d", [128, PAIRS, D])
        b_d = sb("b_d", [E, D])
        vcol = sb("vcol", [128, V_ALL])
        gate = sb("gate", [128, 4])
        tg = sb("tg", [128, 4])
        qksc = sb("qksc", [128, LAYERS, 2, LD])
        rot = sb("rot", [128, LAYERS, TPB, 2, 2, LD])
        bog = sb("bog", [128, 1])

        x_tok = sb("x_tok", [128, T, D])
        c_tok = sb("c_tok", [128, T, D])
        cT = sb("cT", [128, TOK])
        xT = sb("xT", [128, TOK])
        ln_c, ln_sq, ln_r = (sb(n, [128, TOK]) for n in ("ln_c", "ln_sq", "ln_r"))
        nT = sb("nT", [128, TOK])
        kv_c = sb("kv_c", [128, 2, T, D])
        mx = sb("mx", [128, T, H])
        mx_r = sb("mx_r", [128, T, H])
        mx_p = sb("mx_p", [128, T, 3, H], BF16)
        mxT = sb("mxT", [3 * H, TOK], BF16)
        PT = sb("PT", [128, 4, 2, N])
        oraw = sb("oraw", [128, 2, 512])
        rsum = sb("rsum", [128, T, H])
        att = sb("att", [128, T, D])
        order = nc.dram_tensor("order_dram", (NB, H, N, DH), F32, kind="Internal").ap()
        fT = sb("fT", [128, TOK])
        hT = sb("hT", [128, NB, N])
        lqT = sb("lqT", [128, 2, 4, TOK])
        qS = lqT[:, :, :, :].rearrange("p e a n -> p (e a n)").bitcast(BF16)\
            .rearrange("p (e a n) -> p e a n", e=2, a=H // 2)
        qk_sq = sb("qk_sq", [128, 2, INNER])
        qk_ss = sb("qk_ss", [128, 2 * T, LH])
        qk_lg = sb("qk_lg", [128, 2 * T, LH])
        qk_in = sb("qk_in", [128, 2 * T, LH])
        lv = sb("lv", [128, T, LH, LD + 1])
        m0 = sb("m0", [128, NB, 128])
        r_e, r_1, aff, rep = (sb(n, [128, T, E]) for n in ("r_e", "r_1", "aff", "rep"))
        top = sb("top", [128, T, TOPK])
        tsum, tinv = sb("tsum", [128, T]), sb("tinv", [128, T])
        w_m, w_t, w_res = (sb(n, [128, T, E]) for n in ("w_m", "w_t", "w_res"))
        w_p = sb("w_p", [128, T, 3, E], BF16)
        wS = sb("wS", [3 * E, TOK], BF16)
        wT = sb("wT", [E, TOK])
        o_out = c_tok

        arena = sb("arena", [128, 3 * 8 * INNER])
        arena2 = sb("arena2", [128, 4 * TOK])

        def part(at, cols, tile=arena):
            return tile[:, at:at + cols]

        w_raw = part(0, 384).rearrange("p (k n) -> p k n", k=3)
        vrow = arena[0:V_ALL, 512:640]
        stack = part(0, 2048).bitcast(BF16).rearrange("p (t h s) -> p t h s", t=T, h=H)
        kS = part(2048, 2048).bitcast(BF16).rearrange("p (a n) -> p a n", a=H // 2)
        part_f = part(4096, TOK)
        part_h, part_m, part_l = (part(4608 + 256 * n, 256).bitcast(BF16) for n in range(3))
        va = part(5376, 2 * T * 8 * VS).rearrange("p (t g x) -> p t g x", t=T, g=2)
        va_one = part(5376, 2 * T * 8 * VS).rearrange("p (t x) -> p t x", x=VS)[:, :, DH:DH + 1]
        qk, qk_c, qk_s = (part(4096 * n, 4096).rearrange("p (m h d) -> p m h d", m=2 * T, h=LH) for n in range(3))
        o_tok = part(8192, 2048).rearrange("p (t h d) -> p t h d", t=T, h=LH)
        oT = part(10240, 2048).rearrange("p (c n) -> p c n", c=4)
        gel, hid = (part(1536 * n, 1536).rearrange("p (c n) -> p c n", c=len(HCH)) for n in range(2))
        lkT = part(0, 2048, arena2).rearrange("p (c n) -> p c n", c=4)
        qh = part(0, 8192).rearrange("p (h n) -> p h n", h=H)
        am = part(8192, 1536).rearrange("p (r n) -> p r n", r=3)
        f_min, f_exp = (part(9728 + 1024 * n, 1024).rearrange("p (k n) -> p k n", k=2) for n in range(2))
        feat = part(0, 1024, arena2).rearrange("p (k t d) -> p k t d", k=2, t=T)
        fqT, vT = part(1024, TOK, arena2), part(1536, TOK, arena2)
        den, rden, nv, nvT, yC = ln_sq, ln_r, att, ln_c, ln_sq
        sg, up, hm = (part(1024 * n, 1024).rearrange("p (r n) -> p r n", r=2) for n in range(3))
        yD = ln_sq

        s_const = sem("s_const")
        s_wA = sem("s_wA")
        s_w = sem("s_w")
        s_zero = sem("s_zero")
        s_setT = sem("s_setT")
        s_set = sem("s_set")
        s_tanh = sem("s_tanh")
        s_go = sem("s_go")
        turn_sems.clear()
        s_endP, s_endA, s_endD, s_endG = (sem(n) for n in ("s_endP", "s_endA", "s_endD", "s_endG"))
        s_load = sem("s_load")
        s_out = sem("s_out")
        s_inT = sem("s_inT")
        s_cT = sem("s_cT")
        s_src = sem("s_src")
        s_mu, s_cen, s_sq, s_var = (sem(n) for n in ("s_mu", "s_cen", "s_sq", "s_var"))
        s_lg, s_rstd, s_norm = (sem(n) for n in ("s_lg", "s_rstd", "s_norm"))
        s_pj = sem("s_pj")
        s_pe = sem("s_pe")
        s_sp = sem("s_sp")
        s_seenP, s_seenA, s_seenD, s_seenG = (sem(n) for n in ("s_seenP", "s_seenA", "s_seenD", "s_seenG"))
        s_pad = sem("s_pad")
        s_st = sem("s_st")
        s_stT = sem("s_stT")
        s_stD = sem("s_stD")
        s_stA = sem("s_stA")
        s_sA = sem("s_sA")
        s_mA = sem("s_mA")
        s_mp = sem("s_mp")
        s_mT = sem("s_mT")
        s_mS = sem("s_mS")
        s_zA = sem("s_zA")
        s_eA = sem("s_eA")
        s_oA = sem("s_oA")
        s_rA = sem("s_rA")
        s_tA = sem("s_tA")
        s_qA = sem("s_qA")
        s_nA = sem("s_nA")
        s_wrA = sem("s_wrA")
        s_rdA0, s_rdA1 = sem("s_rdA0"), sem("s_rdA1")
        s_yA = sem("s_yA")
        s_hh = sem("s_hh")
        s_pB = sem("s_pB")
        s_cB = sem("s_cB")
        s_s2 = sem("s_s2")
        s_ss = sem("s_ss")
        s_sm = sem("s_sm")
        s_sl = sem("s_sl")
        s_si = sem("s_si")
        s_rs = sem("s_rs")
        s_rc = sem("s_rc")
        s_ra = sem("s_ra")
        s_rn = sem("s_rn")
        s_tB = sem("s_tB")
        s_uB = sem("s_uB")
        NSB = NB * (LH // 4 + LH // 2)
        s_sB = sem("s_sB")
        s_mB = sem("s_mB")
        s_zB = sem("s_zB")
        s_eB = sem("s_eB")
        s_oB = sem("s_oB")
        s_rB = sem("s_rB")
        s_vB = sem("s_vB")
        s_qB = sem("s_qB")
        s_nB = sem("s_nB")
        s_wB = sem("s_wB")
        s_xB = sem("s_xB")
        s_yB = sem("s_yB")
        s_zz = sem("s_zz")
        s_af = sem("s_af")
        s_f1 = sem("s_f1")
        s_f2 = sem("s_f2")
        s_f3 = sem("s_f3")
        s_f4 = sem("s_f4")
        s_f5 = sem("s_f5")
        s_cq = sem("s_cq")
        s_fm = sem("s_fm")
        s_fe = sem("s_fe")
        s_ff = sem("s_ff")
        s_ct = sem("s_ct")
        s_cu = sem("s_cu")
        s_qh = sem("s_qh")
        s_ca = sem("s_ca")
        s_cm = sem("s_cm")
        s_am = sem("s_am")
        s_m0 = sem("s_m0")
        s_m1 = sem("s_m1")
        s_nu = sem("s_nu")
        s_de = sem("s_de")
        s_nt = sem("s_nt")
        s_nc = sem("s_nc")
        s_yc = sem("s_yc")
        s_yd = sem("s_yd")
        s_lo = sem("s_lo")
        s_le = sem("s_le")
        s_la = sem("s_la")
        s_tk = sem("s_tk")
        s_tw = sem("s_tw")
        s_wp = sem("s_wp")
        s_wq = sem("s_wq")
        s_wr = sem("s_wr")
        s_g = sem("s_g")
        s_u = sem("s_u")
        s_sg = sem("s_sg")
        s_up = sem("s_up")
        s_hm = sem("s_hm")
        s_dn = sem("s_dn")
        s_y1 = sem("s_y1")
        s_x4 = sem("s_x4")
        s_xt = sem("s_xt")
        s_xo = sem("s_xo")

        turn_range = range(turn_sems[0].num, turn_sems[-1].num + 1)
        assert len(turn_range) == len(turn_sems)
        block = ctx.enter_context(nc.Block())

        def flat(t):
            return t.rearrange("p t d -> p (t d)")

        @block.sync
        def _(sp):
            sp.dma_start(cf[:, :], a["c_f32"]).then_inc(s_const, 16)
            sp.dma_start(cb[:, :], a["c_bf16"]).then_inc(s_const, 16)
            sp.wait_ge(s_const, 32)
            sp.sem_inc(s_go, 1)
            with sp.Fori(0, TURNS) as it:
                for src, dst in ((a["x"], x_tok), (a["ctx_1024"], c_tok)):
                    sp.dma_start(dst[:, :, :], src.rearrange("(i b) (t p) d -> i p (b t) d", b=NB, p=128)[it])\
                      .then_inc(s_load, 16)
                for bb, s_back in ((0, s_rdA0), (1, s_rdA1)):
                    sp.wait_ge(s_nA, bb + 1)
                    for t in range(TPB):
                        sp.dma_start(order[bb, :, 128 * t:128 * t + 128, :].rearrange("h q d -> q h d"),
                                     att[:, TPB * bb + t, :].rearrange("p (h d) -> p h d", d=DH)).then_inc(s_wrA, 16)
                    sp.wait_ge(s_wrA, 32 * (bb + 1))
                    sp.dma_start(x_tok[:, TPB * bb:TPB * bb + TPB, :],
                                 order[bb].rearrange("h (a b) d -> (h a) (b d)", b=16).rearrange("(t p) c -> p t c", p=128))\
                      .then_inc(s_back, 16)
                sp.wait_ge(s_xo, 1)
                sp.dma_start(out.rearrange("(i b) (t p) d -> i p (b t) d", b=NB, p=128)[it], o_out[:, :, :])\
                  .then_inc(s_out, 16)
                sp.wait_ge(s_out, 16)
                for s in (s_endP, s_endA, s_endD, s_endG):
                    sp.wait_ge(s, 1)
                sp.sem_clear(turn_range)
                sp.sem_inc(s_go, 1)

        @block.gpsimd
        def _(pool):
            loads = [(w_raw[:, n, :], a[f"L0_xattn_W{c}"]) for n, c in enumerate("qkv")]
            loads += [(row[0:1, 128 * n:128 * n + 128], a[f"L1_xattn_b{c}"].rearrange("(a n) -> a n", a=1))
                      for n, c in enumerate("qkv")]
            loads += [(row[0:1, 384:384 + E], a["L1_ffn_br"].rearrange("(a n) -> a n", a=1))]
            loads += [(vrow[V_BG:V_BG + PAIRS, :], a["L1_ffn_bg"].rearrange("(p e) i -> p (e i)", e=2)),
                      (vrow[V_BU:V_BU + PAIRS, :], a["L1_ffn_bu"].rearrange("(p e) i -> p (e i)", e=2)),
                      (vrow[V_LG:V_LG + LAYERS, :], a["L0_ffn_ln_g"]),
                      (vrow[V_LB:V_LB + LAYERS, :], a["L0_ffn_ln_b"]),
                      (vrow[V_B2:V_B2 + LAYERS, :], a["L0_ffn_b2"]),
                      (vrow[V_BO:V_BO + 1, :], a["L1_xattn_bo"].rearrange("(a n) -> a n", a=1)),
                      (vrow[V_BDS:V_BDS + 1, :], a["L1_ffn_bd_s"].rearrange("(a n) -> a n", a=1)),
                      (vrow[V_BGS:V_BGS + 1, 0:I], a["L1_ffn_bg_s"].rearrange("(a n) -> a n", a=1)),
                      (vrow[V_BUS:V_BUS + 1, 0:I], a["L1_ffn_bu_s"].rearrange("(a n) -> a n", a=1))]
            for l in range(LAYERS):
                for half in range(2):
                    for c, (c0, w) in enumerate(HCH):
                        r = V_B1 + (l * 2 + half) * len(HCH) + c
                        loads += [(vrow[r:r + 1, 0:w],
                                   a["L0_ffn_b1"][l:l + 1, half * HID + c0:half * HID + c0 + w])]
            loads += [(gate[:, 0:2], a["g_xattn"].rearrange("(a n) -> a n", a=1).to_broadcast([128, 2])),
                      (gate[:, 2:4], a["g_ffn"].rearrange("(a n) -> a n", a=1).to_broadcast([128, 2]))]
            for l in range(LAYERS):
                loads += [(qksc[:, l, 0, :], a["L0_ffn_q_scale"][l:l + 1, :].to_broadcast([128, LD])),
                          (qksc[:, l, 1, :], a["L0_ffn_k_scale"][l:l + 1, :].to_broadcast([128, LD]))]
            pool.wait_ge(s_zero, 1)
            for dst, src in loads:
                pool.dma_start(dst, src).then_inc(s_wA, 16)
            first = len(loads)
            loads = [(w_c[:, n, :], a[f"L1_xattn_W{c}"]) for n, c in enumerate("qkvo")]
            for l in range(LAYERS):
                loads += [(w_qkv[:, l, :], a["L0_ffn_wqkv"][l]),
                          (w_o[:, l, :, :], a["L0_ffn_wo"][l].rearrange("(c p) n -> p c n", p=128)),
                          (w_1[:, l, :], a["L0_ffn_w1"][l])]
                loads += [(w_2[0:w, l, c, :], a["L0_ffn_w2"][l, c0:c0 + w, :]) for c, (c0, w) in enumerate(HCH)]
            loads += [(w_r[:, :], a["L1_ffn_Wr"]), (w_gs[:, 0, :], a["L1_ffn_Wg_s"]),
                      (w_gs[:, 1, :], a["L1_ffn_Wu_s"]), (w_ds[:, :], a["L1_ffn_Wd_s"]),
                      (w_g[:, :, :], a["L1_ffn_Wg"].rearrange("e h i -> h e i")),
                      (w_u[:, :, :], a["L1_ffn_Wu"].rearrange("e h i -> h e i")),
                      (w_d[:, :, :], a["L1_ffn_Wd"].rearrange("(p e) i h -> (e i) p h", e=2)),
                      (b_d[:, :], a["L1_ffn_bd"])]
            for dst, src in loads:
                pool.dma_start(dst, src).then_inc(s_w, 16)
            counts["wA"], counts["w"] = 16 * first, 16 * len(loads)
            pool.wait_ge(s_set, SET)

            with pool.Fori(0, TURNS) as it:
                pool.wait_ge(s_go, it + 1)

                def wait(s, k):
                    pool.wait_ge(s, k)

                pool.sem_inc(s_seenG, 1)
                wait(s_seenG, 1)
                nc.gpsimd.memset(stack[:, :, :, 48:SLOT], 0.0)
                nc.gpsimd.memset(va[:, :, :, :], 0.0).then_inc(s_pad, 1)
                wait(s_pad, 1)
                nc.gpsimd.memset(va_one, 1.0).then_inc(s_pad, 1)
                for l in range(LAYERS):
                    for m in range(2 * T):
                        wait(s_cB, l * 3 * T + 3 * (m // 2) + m % 2 + 1)
                        tab = rot[:, l, (m // 2) % TPB, m % 2, 1, :].unsqueeze(1)
                        h2 = LD // 2
                        nc.gpsimd.tensor_tensor(qk_s[:, m, :, 0:h2], qk[:, m, :, h2:LD],
                                                tab[:, :, 0:h2].to_broadcast([128, LH, h2]), ALU.mult)
                        nc.gpsimd.tensor_tensor(qk_s[:, m, :, h2:LD], qk[:, m, :, 0:h2],
                                                tab[:, :, h2:LD].to_broadcast([128, LH, h2]), ALU.mult)\
                          .then_inc(s_rs, 1)
                wait(s_xo, 1)
                pool.drain().then_inc(s_endG, 1)

        @block.tensor
        def _(pe):
            mm, tr = nc.tensor.matmul, nc.tensor.transpose
            pe.wait_ge(s_const, 32)
            pe.wait_ge(s_wA, counts["wA"])
            for n in range(3):
                tr(bank[0][:, 128 * n:128 * n + 128], w_raw[:, n, :], ident)
            tr(bank[1][:, 0:V_ALL], vrow[:, :], ident[0:V_ALL, 0:V_ALL]).then_inc(s_setT, 1)
            pe.wait_ge(s_w, counts["w"])
            pe.wait_ge(s_set, SET)
            with pe.Fori(0, TURNS) as it:
                pe.wait_ge(s_go, it + 1)
                pe.sem_inc(s_seenP, 1)

                def wait(s, k):
                    pe.wait_ge(s, k)

                def norm_pe(n, src):
                    wait(s_src, n + 1)
                    mm(bank[0][:, :], mean, src[:, :], start=True, stop=True).then_inc(s_mu, 1)
                    wait(s_sq, n + 1)
                    mm(bank[1][:, :], mean, ln_sq[:, :], start=True, stop=True).then_inc(s_var, 1)

                def max_transposed(n, to):
                    wait(s_mp, 4 * n + 4)
                    for t in range(T):
                        last = tr(bbank(to)[0:3 * H, 128 * t:128 * t + 128],
                                  mx_p[:, t, :, :].rearrange("p a h -> p (a h)"), identb)
                    last.then_inc(s_mT, 1)
                    wait(s_mS, n + 1)

                wait(s_load, 32)
                for n, src in enumerate((x_tok, c_tok)):
                    for t in range(T):
                        last = tr(bank[n][:, 128 * t:128 * t + 128], src[:, t, :], ident)
                    last.then_inc(s_inT, 1)

                wait(s_cT, 1)
                for n, w in enumerate((w_a[:, 1, :], w_a[:, 2, :], w_c[:, 1, :], w_c[:, 2, :])):
                    for t in range(T):
                        o = bank[2 + n][:, 128 * t:128 * t + 128]
                        last = mm(o, cT[:, 128 * t:128 * t + 128], w, start=True, stop=n < 2)
                        if n >= 2:
                            last = mm(o, ones[0:1, :], row[0:1, 128 * (n - 1):128 * n], start=False, stop=True)
                    last.then_inc(s_pj, 1)
                norm_pe(0, xT)
                wait(s_norm, 1)
                for t in range(T):
                    last = mm(bank[6][:, 128 * t:128 * t + 128], nT[:, 128 * t:128 * t + 128], w_a[:, 0, :],
                              start=True, stop=True)
                last.then_inc(s_pj, 1)
                wait(s_pad, 2)
                for n in range(2):
                    wait(s_st, n + 1)
                    for t in range(T):
                        if n == 0 and t == 1:
                            wait(s_pe, 3)
                        if n == 1:
                            wait(s_stD, t + 1)
                        for p in range(H // 2):
                            last = tr(bbank(2 + t)[:, 128 * p:128 * p + 128],
                                      stack[:, t, 2 * p:2 * p + 2, :].rearrange("p h s -> p (h s)"), identb)
                        last.then_inc(s_stT, 1)
                ring = (0, 1, 6, 7)
                for t in range(T):
                    wait(s_stA, t + 1)
                    for p in range(H // 2):
                        n = t * (H // 2) + p
                        if n >= 4:
                            wait(s_mA, n - 3)
                        for e in range(2):
                            last = mm(bank[ring[n % 4]][:, 256 * e:256 * e + 256],
                                      qS[:, e, p, 128 * t:128 * t + 128],
                                      kS[:, p, N * (t // TPB):N * (t // TPB) + N], start=True, stop=True)
                        last.then_inc(s_sA, 1)
                max_transposed(0, 2)

                def score_A(n):
                    bb, p, kt = n // H, n % H // 2, n % 2
                    if n >= 3:
                        wait(s_eA, n - 2)
                    o = bank[3 + n % 3]
                    k0 = N * bb + 128 * kt
                    for e in range(2):
                        h = 2 * p + e
                        mm(o[:, N * e:N * e + N], cb[0:3 * H, K_MAX + 128 * h:K_MAX + 128 * h + 128],
                           mxT[:, N * bb:N * bb + N], start=(e == 0), stop=False, skip_group_check=True)
                    mm(o[:, :], kS[:, p, k0:k0 + 128], qS[:, :, p, N * bb:N * bb + N], start=False, stop=True,
                       skip_group_check=True).then_inc(s_zA, 1)

                def value_A(n):
                    bb, p, kt = n // H, n % H // 2, n % 2
                    wait(s_eA, n + 1)
                    g = p // 4
                    for e in range(2):
                        h8 = (2 * p + e) % 8
                        last = mm(bank[6 + bb][0:72, N * g:N * g + N],
                                  va[:, TPB * bb + kt, g, 72 * h8:72 * h8 + 72],
                                  PT[:, n % 4, e, 0:N], start=(p % 4 == 0 and kt == 0 and e == 0),
                                  stop=(p % 4 == 3 and kt == 1 and e == 1))
                    last.then_inc(s_oA, 1)

                LAG = 2
                for n in range(NB * H + LAG):
                    if n < NB * H:
                        score_A(n)
                    if n >= LAG:
                        value_A(n - LAG)
                for bb in range(NB):
                    wait(s_rA, bb + 1)
                    for t in range(TPB):
                        for g in range(2):
                            last = tr(bank[1 + bb][:, 72 * (2 * t + g):72 * (2 * t + g) + 72],
                                      oraw[0:72, bb, N * g + 128 * t:N * g + 128 * t + 128], ident[0:72, 0:72])
                    last.then_inc(s_tA, 1)
                for t in range(T):
                    wait((s_rdA0, s_rdA1)[t // TPB], 16)
                    last = tr(bank[0][:, 128 * t:128 * t + 128], x_tok[:, t, :], ident)
                last.then_inc(s_yA, 1)

                norm_pe(1, xT)
                for l in range(LAYERS):
                    wait(s_hh, 2 * l + 1)
                    for t in range(T):
                        for part in range(3):
                            n = 3 * t + part
                            if n >= 6:
                                wait(s_cB, l * 3 * T + n - 5)
                            mm(bank[2 + n % 6][:, :], hT[:, :, :].rearrange("p b n -> p (b n)")[:, 128 * t:128 * t + 128],
                               w_qkv[:, l, INNER * part:INNER * part + INNER], start=True, stop=True)\
                                .then_inc(s_pB, 1)
                    for m in range(2 * T):
                        wait(s_rn, l * 2 * T + m + 1)
                        if m < 6:
                            wait(s_cB, l * 3 * T + m + 7)
                        else:
                            wait(s_uB, l * 2 * T + m - 5)
                        for p in range(4):
                            last = tr(bank[2 + m % 6][:, 128 * p:128 * p + 128],
                                      qk_c[:, m, 2 * p:2 * p + 2, :].rearrange("p h d -> p (h d)"), ident)
                        last.then_inc(s_tB, 1)
                    n = 0
                    for bb in range(NB):
                        wait(s_uB, l * 2 * T + 4 * bb + 4)
                        if bb == 0:
                            wait(s_uB, l * 2 * T + 2 * T)
                        for t, per in ((0, 4), (1, 2)):
                            w = 128 + WIN * t
                            for h0 in range(0, LH, per):
                                if n >= 4:
                                    wait(s_mB, l * NSB + n - 3)
                                for j in range(per):
                                    h = h0 + j
                                    o = bank[n % 4][:, w * j:w * j + w]
                                    q0 = N * bb + 128 * t
                                    mm(o, lqT[:, h % 2, h // 2, q0:q0 + 128],
                                       lkT[:, h // 2, q0 - WIN * t:q0 + 128], start=True, stop=False)
                                    last = mm(o, identb, cb[:, K_MQ + WIN * (1 - t):K_MQ + 192],
                                              start=False, stop=True)
                                last.then_inc(s_sB, 1)
                                n += 1
                    max_transposed(1 + l, 4)

                    def score_B(n):
                        bb, h = n // LH, n % LH
                        if n >= 3:
                            wait(s_eB, l * NB * LH + n - 2)
                        for kt, (c0, w) in enumerate(((0, 192), (192, 128))):
                            o = bank[5 + n % 3][:, c0:c0 + w]
                            k0 = N * bb + 128 * kt
                            mm(o, lkT[:, h // 2, k0:k0 + 128], lqT[:, h % 2, h // 2, k0:k0 + w],
                               start=True, stop=False)
                            mm(o, identb, cb[:, K_MK:K_MK + w], start=False, stop=False)
                            last = mm(o, cb[0:3 * H, K_MAX + 128 * h:K_MAX + 128 * h + 128],
                                      mxT[:, k0:k0 + w], start=False, stop=True)
                        last.then_inc(s_zB, 1)

                    def value_B(n):
                        bb, h = n // LH, n % LH
                        wait(s_eB, l * NB * LH + n + 1)
                        g = n // 2
                        if h % 2 == 0 and g >= 2:
                            wait(s_rB, l * NB * LH // 2 + g - 1)
                        P = PT[:, n % 4, :, :].rearrange("p a b -> p (a b)")
                        o = bank[g % 2][0:LD + 1, N * (h % 2):N * (h % 2) + N]
                        mm(o[:, 0:192], lv[:, TPB * bb, h, :], P[:, 0:192], start=True, stop=True)
                        mm(o[:, 128:256], lv[:, TPB * bb + 1, h, :], P[:, 192:320], start=False, stop=True,
                           skip_group_check=True).then_inc(s_oB, 1)

                    def back_B(g):
                        base = l * NB * LH // 2
                        wait(s_rB, base + g + 1)
                        if g >= 2:
                            wait(s_nB, base + g - 1)
                        for t in range(TPB):
                            for e in range(2):
                                k = 2 * t + e
                                last = tr(bank[2 + g % 2][:, (LD + 1) * k:(LD + 1) * k + LD + 1],
                                          oraw[0:LD + 1, g % 2, N * e + 128 * t:N * e + 128 * t + 128],
                                          ident[0:LD + 1, 0:LD + 1])
                        last.then_inc(s_vB, 1)

                    for n in range(NB * LH + 5):
                        if n < NB * LH:
                            score_B(n)
                        if 2 <= n < NB * LH + 2:
                            value_B(n - 2)
                        if n >= 5 and (n - 5) % 2 == 0:
                            back_B((n - 5) // 2)
                    for t in range(T):
                        wait(s_nB, l * NB * LH // 2 + (t // TPB + 1) * LH // 2)
                        for p in range(4):
                            last = tr(bank[4 + t][:, 128 * p:128 * p + 128],
                                      o_tok[:, t, 2 * p:2 * p + 2, :].rearrange("p h d -> p (h d)"), ident)
                        last.then_inc(s_wB, 1)
                    wait(s_xB, l * T + T)
                    for c in range(4):
                        last = mm(bank[0][:, :], w_o[:, l, c, :], oT[:, c, :], start=(c == 0), stop=(c == 3))
                    last.then_inc(s_yB, 1)
                    norm_pe(2 + l, hT[:, :, :].rearrange("p b n -> p (b n)"))
                    wait(s_af, l + 1)
                    for c, (c0, w) in enumerate(HCH):
                        for half in range(2):
                            at = half * HID + c0
                            last = mm(bank[2 + 2 * c + half][0:w, :], w_1[:, l, at:at + w], nT[:, :],
                                      start=True, stop=True)
                        last.then_inc(s_f1, 1)
                    for c, (c0, w) in enumerate(HCH):
                        wait(s_f3, l * len(HCH) + c + 1)
                        last = mm(bank[0][:, :], w_2[0:w, l, c, :], hid[0:w, c, :],
                                  start=(c == 0), stop=(c == len(HCH) - 1))
                    last.then_inc(s_f4, 1)

                norm_pe(4, xT)
                wait(s_norm, 5)
                for t in range(T):
                    o = bank[2][:, 128 * t:128 * t + 128]
                    mm(o, nT[:, 128 * t:128 * t + 128], w_c[:, 0, :], start=True, stop=False)
                    last = mm(o, ones[0:1, :], row[0:1, 0:128], start=False, stop=True)
                last.then_inc(s_cq, 1)
                wait(s_ff, 2)
                for n, src in enumerate((feat[:, 0], kv_c[:, 1])):
                    for t in range(T):
                        last = tr(bank[3 + n][:, 128 * t:128 * t + 128], src[:, t, :], ident)
                    last.then_inc(s_ct, 1)
                for bb in range(NB):
                    last = mm(bank[1][:, 128 * bb:128 * bb + 128], kv_c[:, 1, TPB * bb, :], feat[:, 1, TPB * bb, :],
                              start=True, stop=True)
                last.then_inc(s_m0, 1)
                wait(s_cu, 1)
                for t in range(T):
                    o = bank[3][:, 128 * t:128 * t + 128]
                    last = mm(o, causal, feat[:, 1, t, :], start=True, stop=t % TPB == 0)
                    if t % TPB:
                        last = mm(o, ones, feat[:, 1, t - 1, :], start=False, stop=True)
                last.then_inc(s_nu, 1)
                wait(s_cu, 2)

                def cross(n):
                    t, g = n // 4, n % 4
                    if t == 0:
                        wait(s_qh, g + 1)
                    if n >= 3:
                        wait(s_cm, n - 2)
                    mm(bank[5 + n % 3][:, :], vT[:, 128 * t:128 * t + 128], qh[:, 4 * g:4 * g + 4, 128 * t:128 * t + 128],
                       start=True, stop=True).then_inc(s_ca, 1)

                def numer(n):
                    t, g = n // 4, n % 4
                    o = bank[2][:, 128 * t:128 * t + 128]
                    if g == 0 and t % TPB:
                        wait(s_m1, 1)
                        mm(o, fqT[:, 128 * t:128 * t + 128], m0[:, t // TPB, :], start=True, stop=False,
                           skip_group_check=True)
                    wait(s_cm, n + 1)
                    for j in range(4):
                        h = 4 * g + j
                        last = mm(o[:, DH * h:DH * h + DH], am[:, n % 3, 128 * j:128 * j + 128],
                                  feat[:, 1, t, DH * h:DH * h + DH], start=(t % TPB == 0), stop=True,
                                  skip_group_check=True)
                    return last

                for n in range(4 * T + 2):
                    if n < 4 * T:
                        cross(n)
                    if n >= 2:
                        last = numer(n - 2)
                        last.then_inc(s_am, 1)
                wait(s_de, 4)
                for t in range(T):
                    last = tr(bank[4][:, 128 * t:128 * t + 128], nv[:, t, :], ident)
                last.then_inc(s_nt, 1)
                wait(s_nc, 1)
                mm(bank[5][:, :], w_c[:, 3, :], nvT[:, :], start=True, stop=True).then_inc(s_yc, 1)

                norm_pe(5, xT)
                wait(s_norm, 6)
                for t in range(T):
                    o = bank[2][:, E * t:E * t + E]
                    mm(o, nT[:, 128 * t:128 * t + 128], w_r[:, :], start=True, stop=False)
                    last = mm(o, ones[0:1, :], row[0:1, 384:384 + E], start=False, stop=True)
                last.then_inc(s_lo, 1)
                wait(s_wp, 4)
                for t in range(T):
                    last = tr(bbank(3)[0:3 * E, 128 * t:128 * t + 128],
                              w_p[:, t, :, :].rearrange("p a e -> p (a e)"), identb)
                last.then_inc(s_wq, 1)
                for t in range(T):
                    last = tr(bank[4][0:E, 128 * t:128 * t + 128], w_t[:, t, :], ident)
                last.then_inc(s_wq, 1)
                wait(s_wr, 2)
                mm(bank[0][:, :], b_d[:, :], wT[:, :], start=True, stop=False)

                def expert_in(n):
                    m = 128 if n < PAIRS else I
                    if n < PAIRS:
                        gw = w_g[:, 2 * n:2 * n + 2, :].rearrange("p e i -> p (e i)")
                        uw = w_u[:, 2 * n:2 * n + 2, :].rearrange("p e i -> p (e i)")
                    else:
                        gw, uw = w_gs[:, 0, :], w_gs[:, 1, :]
                    if n >= 2:
                        wait(s_sg, n - 1)
                    mm(bank[2 + 3 * (n % 2)][0:m, :], gw, nT[:, :], start=True, stop=True).then_inc(s_g, 1)
                    if n >= 2:
                        wait(s_hm, n - 1)
                    last = mm(bank[3 + 3 * (n % 2)][0:m, :], uw, nT[:, :], start=True, stop=True)
                    if n < PAIRS:
                        last = mm(bank[4 + 3 * (n % 2)][:, :], cb[0:3 * E, K_SEL + 128 * n:K_SEL + 128 * n + 128],
                                  wS[:, :], start=True, stop=True)
                    last.then_inc(s_u, 1)

                def expert_out(n):
                    wait(s_hm, n + 1)
                    if n < PAIRS:
                        mm(bank[0][:, :], w_d[:, n, :], hm[:, n % 2, :], start=False, stop=False).then_inc(s_dn, 1)
                    else:
                        mm(bank[0][:, :], w_ds[:, :], hm[0:I, n % 2, :], start=False, stop=True).then_inc(s_dn, 1)

                for n in range(PAIRS + 2):
                    if n <= PAIRS:
                        expert_in(n)
                    if n >= 1:
                        expert_out(n - 1)
                wait(s_x4, 1)
                for t in range(T):
                    last = tr(bank[1][:, 128 * t:128 * t + 128], xT[:, 128 * t:128 * t + 128], ident)
                last.then_inc(s_xt, 1)
                wait(s_xo, 1)
                pe.drain().then_inc(s_endP, 1)

        @block.scalar
        def _(act):
            A = nc.scalar.activation
            act.wait_ge(s_wA, counts["wA"])
            A(tg[:, :], gate[:, :], ACT.Tanh).then_inc(s_tanh, 1)
            act.wait_ge(s_set, SET)
            with act.Fori(0, TURNS) as it:
                act.wait_ge(s_go, it + 1)
                act.sem_inc(s_seenA, 1)

                def wait(s, k):
                    act.wait_ge(s, k)

                def norm_act(n):
                    wait(s_var, n + 1)
                    A(ln_r[:, :], bank[1][:, :], ACT.Ln, bias=EPS).then_inc(s_lg, 1)
                    wait(s_lg, n + 1)
                    A(ln_r[:, :], ln_r[:, :], ACT.Exp, scale=-0.5).then_inc(s_rstd, 1)

                def max_act(n, frm):
                    wait(s_mT, n + 1)
                    A(mxT[:, :], bbank(frm)[0:3 * H, 0:TOK], ACT.Copy).then_inc(s_mS, 1)

                wait(s_inT, 2)
                A(cT[:, :], bank[1][:, :], ACT.Copy).then_inc(s_cT, 1)
                norm_act(0)
                wait(s_pj, 2)
                wait(s_pad, 2)
                for g in range(2):
                    last = A(va[:, :, g, :].rearrange("p t (h x) -> p t h x", x=VS)[:, :, :, 0:DH],
                             bank[3][:, :].rearrange("p (t g h d) -> p t g h d", t=T, g=2, h=8)[:, :, g], ACT.Copy)
                last.then_inc(s_pe, 1)
                for n in range(2):
                    wait(s_pj, 3 + n)
                    A(flat(kv_c[:, n]), bank[4 + n][:, :], ACT.Copy).then_inc(s_pe, 1)
                for t in range(T):
                    wait(s_stT, T + t + 1)
                    for e in range(2):
                        last = A(qS[64 * e:64 * e + 64, e, :, 128 * t:128 * t + 128],
                                 bbank(2 + t)[64 * e:64 * e + 64, :].rearrange("p (a n) -> p a n", a=H // 2), ACT.Copy)
                    last.then_inc(s_stA, 1)
                max_act(0, 2)
                for n in range(NB * H):
                    wait(s_zA, n + 1)
                    if n >= 4:
                        wait(s_oA, n - 3)
                    A(PT[:, n % 4, :, 0:N], bank[3 + n % 3][:, :].rearrange("p (e q) -> p e q", e=2), ACT.Exp,
                      scale=float(DH) ** -0.5).then_inc(s_eA, 1)
                    if n == H + 2:
                        wait(s_oA, H)
                        A(oraw[0:72, 0, :], bank[6][0:72, :], ACT.Copy).then_inc(s_rA, 1)
                wait(s_oA, NB * H)
                A(oraw[0:72, 1, :], bank[7][0:72, :], ACT.Copy).then_inc(s_rA, 1)

                norm_act(1)
                for l in range(LAYERS):
                    def inverse(t):
                        wait(s_sm, l * T + t + 1)
                        A(qk_lg[:, 2 * t:2 * t + 2, :], qk_ss[:, 2 * t:2 * t + 2, :], ACT.Ln, scale=2.0 ** 20)\
                            .then_inc(s_sl, 1)
                        wait(s_sl, l * T + t + 1)
                        A(qk_in[:, 2 * t:2 * t + 2, :], qk_lg[:, 2 * t:2 * t + 2, :], ACT.Exp, scale=-0.5,
                          bias=float(10 * np.log(2.0))).then_inc(s_si, 1)

                    for t in range(T):
                        for part in range(3):
                            n = l * 3 * T + 3 * t + part
                            wait(s_pB, n + 1)
                            src = bank[2 + (3 * t + part) % 6]
                            if part == 2:
                                A(lv[:, t, :, 0:LD], src[:, :].rearrange("p (h d) -> p h d", h=LH), ACT.Copy)\
                                    .then_inc(s_cB, 1)
                                continue
                            m = 2 * t + part
                            A(qk[:, m, :, :].rearrange("p h d -> p (h d)"), src[:, :], ACT.Copy).then_inc(s_cB, 1)
                            wait(s_cB, n + 1)
                            if m >= 2:
                                wait(s_ss, l * 2 * T + m - 1)
                            A(qk_sq[:, m % 2, :], qk[:, m, :, :].rearrange("p h d -> p (h d)"), ACT.Square)\
                                .then_inc(s_s2, 1)
                        if t:
                            inverse(t - 1)
                    inverse(T - 1)
                    for m in range(2 * T):
                        wait(s_tB, l * 2 * T + m + 1)
                        t, src = m // 2, bank[2 + m % 6]
                        v = src[:, :].rearrange("p (a n) -> p a n", a=4)
                        if m % 2:
                            A(lkT[:, :, 128 * t:128 * t + 128], v, ACT.Copy).then_inc(s_uB, 1)
                        else:
                            for e in range(2):
                                last = A(lqT[64 * e:64 * e + 64, e, :, 128 * t:128 * t + 128],
                                         v[64 * e:64 * e + 64], ACT.Copy)
                            last.then_inc(s_uB, 1)
                    max_act(1 + l, 4)
                    base = l * NB * LH

                    def raw_B(g):
                        wait(s_oB, base + 2 * g + 2)
                        if g >= 2:
                            wait(s_vB, base // 2 + g - 1)
                        A(oraw[0:LD + 1, g % 2, :], bank[g % 2][0:LD + 1, :], ACT.Copy).then_inc(s_rB, 1)

                    for n in range(NB * LH):
                        wait(s_zB, base + n + 1)
                        if n >= 4:
                            wait(s_oB, base + n - 3)
                        A(PT[:, n % 4, :, :].rearrange("p a b -> p (a b)")[:, 0:320], bank[5 + n % 3][:, 0:320],
                          ACT.Exp, scale=8.0).then_inc(s_eB, 1)
                        if n >= 3 and n % 2:
                            raw_B((n - 3) // 2)
                    raw_B(NB * LH // 2 - 1)
                    for t in range(T):
                        wait(s_wB, l * T + t + 1)
                        A(oT[:, :, 128 * t:128 * t + 128], bank[4 + t][:, :].rearrange("p (a n) -> p a n", a=4),
                          ACT.Copy).then_inc(s_xB, 1)
                    norm_act(2 + l)
                    for c, (c0, w) in enumerate(HCH):
                        n = l * len(HCH) + c
                        wait(s_f1, n + 1)
                        v = V_B1 + (l * 2 + 1) * len(HCH) + c
                        A(gel[0:w, c, :], bank[3 + 2 * c][0:w, :], ACT.Gelu, bias=vcol[0:w, v:v + 1]).then_inc(s_f2, 1)
                norm_act(4)
                for n in range(2):
                    wait(s_fm, n + 1)
                    A(f_exp[:, n, :], f_min[:, n, :], ACT.Exp).then_inc(s_fe, 1)
                for n, dst in enumerate((fqT, vT)):
                    wait(s_ct, n + 1)
                    A(dst[:, :], bank[3 + n][:, :], ACT.Copy).then_inc(s_cu, 1)
                wait(s_nt, 1)
                A(nvT[:, :], bank[4][:, :], ACT.Copy).then_inc(s_nc, 1)
                norm_act(5)
                wait(s_lo, 1)
                A(flat(r_e), bank[2][:, 0:T * E], ACT.Exp, scale=-1.0).then_inc(s_le, 1)
                wait(s_wq, 1)
                A(wS[:, :], bbank(3)[0:3 * E, 0:TOK], ACT.Copy).then_inc(s_wr, 1)
                wait(s_wq, 2)
                A(wT[:, :], bank[4][0:E, :], ACT.Copy).then_inc(s_wr, 1)
                for n in range(PAIRS + 1):
                    m = 128 if n < PAIRS else I
                    v = V_BG + n if n < PAIRS else V_BGS
                    wait(s_g, n + 1)
                    if n >= 2:
                        wait(s_up, n - 1)
                    A(sg[0:m, n % 2, :], bank[2 + 3 * (n % 2)][0:m, :], ACT.Silu, bias=vcol[0:m, v:v + 1])\
                        .then_inc(s_sg, 1)
                wait(s_xt, 1)
                A(flat(o_out), bank[1][:, :], ACT.Copy).then_inc(s_xo, 1)
                wait(s_xo, 1)
                act.drain().then_inc(s_endA, 1)

        @block.vector
        def _(dve):
            V = nc.vector
            V.memset(vrow[:, :], 0.0).then_inc(s_zero, 1)
            V.memset(lqT[:, :, :, :], 0.0)
            V.memset(mx[:, :, :], 0.0)
            V.memset(hT[:, :, :], 0.0)
            V.memset(lv[:, :, :, LD:LD + 1], 1.0).then_inc(s_set, 1)
            dve.wait_ge(s_setT, 1)
            V.tensor_copy(flat(w_a), bank[0][:, 0:384])
            V.tensor_copy(vcol[:, :], bank[1][:, 0:V_ALL]).then_inc(s_set, 1)
            dve.wait_ge(s_const, 32)
            dve.wait_ge(s_wA, counts["wA"])
            h2 = LD // 2
            for l in range(LAYERS):
                for t in range(TPB):
                    for k in range(2):
                        V.tensor_tensor(rot[:, l, t, k, 0, :], rot_c[:, t, k, 0, :], qksc[:, l, k, :], ALU.mult)
                        V.tensor_tensor(rot[:, l, t, k, 1, 0:h2], rot_c[:, t, k, 1, 0:h2], qksc[:, l, k, h2:LD], ALU.mult)
                        V.tensor_tensor(rot[:, l, t, k, 1, h2:LD], rot_c[:, t, k, 1, h2:LD], qksc[:, l, k, 0:h2], ALU.mult)
            dve.wait_ge(s_set, 2)
            dve.wait_ge(s_tanh, 1)
            V.tensor_tensor(bog[:, :], vcol[:, V_BO:V_BO + 1], tg[:, 1:2], ALU.mult).then_inc(s_set, 1)
            dve.wait_ge(s_set, SET)
            with dve.Fori(0, TURNS) as it:
                dve.wait_ge(s_go, it + 1)
                dve.sem_inc(s_seenD, 1)

                def wait(s, k):
                    dve.wait_ge(s, k)

                def norm_dve(n, src, dst):
                    wait(s_mu, n + 1)
                    V.tensor_tensor(ln_c[:, :], src, bank[0][:, :], ALU.subtract).then_inc(s_cen, 1)
                    wait(s_cen, n + 1)
                    V.tensor_tensor(ln_sq[:, :], ln_c[:, :], ln_c[:, :], ALU.mult).then_inc(s_sq, 1)
                    wait(s_rstd, n + 1)
                    V.tensor_tensor(dst, ln_c[:, :], ln_r[:, :], ALU.mult).then_inc(s_norm, 1)

                def split(n, src, hi, mid, lo, res, s, k0):
                    V.tensor_copy(hi, src).then_inc(s, 1)
                    wait(s, k0 + 1)
                    V.tensor_tensor(res, src, hi, ALU.subtract).then_inc(s, 1)
                    wait(s, k0 + 2)
                    V.tensor_copy(mid, res).then_inc(s, 1)
                    wait(s, k0 + 3)
                    V.tensor_tensor(lo, res, mid, ALU.subtract).then_inc(s, 1)
                    wait(s, k0 + 4)

                def split_stack(n, src):
                    split(n, src, part_h[:, :], part_m[:, :], part_l[:, :], part_f[:, :], s_sp, 4 * n)
                    st = stack[:, :, :, 0:48].rearrange("p t h (s d) -> p (t h) s d", d=DH)
                    parts = [p[:, :].rearrange("p (h d) -> p h d", d=DH) for p in (part_h, part_m, part_l)]
                    if n == 0:
                        order = (0, 1, 2, 0, 1, 0)
                    else:
                        wait(s_stT, T)
                        order = (0, 0, 0, 1, 1, 2)
                    for slot, part in enumerate(order):
                        last = V.tensor_copy(st[:, :, slot, :], parts[part])
                    last.then_inc(s_st, 1)

                def scaled(m, l):
                    wait(s_si, l * T + m // 2 + 1)
                    wait(s_ra, l * 2 * T + m + 1)
                    V.tensor_tensor(qk_c[:, m], qk_c[:, m], qk_in[:, m, :].unsqueeze(2).to_broadcast([128, LH, LD]),
                                    ALU.mult).then_inc(s_rn, 1)

                def max_split(n):
                    split(n, mx[:, :, :], mx_p[:, :, 0, :], mx_p[:, :, 1, :], mx_p[:, :, 2, :], mx_r[:, :, :], s_mp, 4 * n)

                wait(s_inT, 1)
                V.tensor_copy(xT[:, :], bank[0][:, :]).then_inc(s_src, 1)
                norm_dve(0, xT[:, :], nT[:, :])
                wait(s_pj, 1)
                split_stack(0, bank[2][:, :])
                for t in range(T):
                    wait(s_stT, t + 1)
                    V.tensor_copy(kS[:, :, 128 * t:128 * t + 128], bbank(2 + t).rearrange("p (a n) -> p a n", a=H // 2))\
                     .then_inc(s_stD, 1)
                wait(s_pj, 5)
                split_stack(1, bank[6][:, :])
                ring = (0, 1, 6, 7)
                for n in range(T * H // 2):
                    t, p = n // (H // 2), n % (H // 2)
                    wait(s_sA, n + 1)
                    V.tensor_reduce(mx[:, t, 2 * p:2 * p + 2], bank[ring[n % 4]][:, :].rearrange("p (e k) -> p e k", e=2),
                                    AX_X, ALU.max).then_inc(s_mA, 1)
                wait(s_mA, T * H // 2)
                max_split(0)
                for bb in range(NB):
                    wait(s_tA, bb + 1)
                    src = bank[1 + bb][:, 0:TPB * 144].rearrange("p (a x) -> p a x", x=9)
                    r = rsum[:, TPB * bb:TPB * bb + TPB, :].rearrange("p t h -> p (t h)").unsqueeze(2)
                    V.reciprocal(r, src[:, :, 8:9]).then_inc(s_qA, 1)
                    wait(s_qA, bb + 1)
                    V.tensor_tensor(att[:, TPB * bb:TPB * bb + TPB, :].rearrange("p t (h d) -> p (t h) d", d=DH),
                                    src[:, :, 0:8], r.to_broadcast([128, TPB * H, DH]), ALU.mult).then_inc(s_nA, 1)
                wait(s_yA, 1)
                V.scalar_tensor_tensor(out=xT[:, :], in0=bank[0][:, :], scalar=tg[:, 0:1], in1=xT[:, :],
                                       op0=ALU.mult, op1=ALU.add).then_inc(s_src, 1)
                wait(s_src, 2)
                norm_dve(1, xT[:, :], fT[:, :])

                def shifted():
                    f3 = fT[:, :].rearrange("p (b n) -> p b n", b=NB)
                    V.tensor_copy(hT[0:64, :, :], f3[0:64])
                    return V.tensor_copy(hT[64:128, :, 1:N], f3[64:128, :, 0:N - 1])

                for l in range(LAYERS):
                    if l == 0:
                        wait(s_norm, 2)
                    else:
                        wait(s_f5, l)
                    shifted().then_inc(s_hh, 1)
                    b2 = l * 2 * T
                    for m in range(2 * T):
                        t = m // 2
                        wait(s_s2, b2 + m + 1)
                        V.tensor_reduce(qk_ss[:, m, :], qk_sq[:, m % 2, :].rearrange("p (h d) -> p h d", h=LH),
                                        AX_X, ALU.add).then_inc(s_ss, 1)
                        if m % 2:
                            wait(s_ss, b2 + m + 1)
                            V.tensor_scalar(qk_ss[:, m - 1:m + 1, :], qk_ss[:, m - 1:m + 1, :], 1e-24, None, ALU.max)\
                             .then_inc(s_sm, 1)
                        tab = rot[:, l, t % TPB, m % 2, 0, :].unsqueeze(1).to_broadcast([128, LH, LD])
                        V.tensor_tensor(qk_c[:, m], qk[:, m], tab, ALU.mult).then_inc(s_rc, 1)
                        wait(s_rc, b2 + m + 1)
                        wait(s_rs, b2 + m + 1)
                        V.tensor_tensor(qk_c[:, m], qk_c[:, m], qk_s[:, m], ALU.add).then_inc(s_ra, 1)
                        if m >= 2:
                            scaled(m - 2, l)
                    for m in (2 * T - 2, 2 * T - 1):
                        scaled(m, l)
                    n = 0
                    for bb in range(NB):
                        for t, per in ((0, 4), (1, 2)):
                            w = 128 + WIN * t
                            for h0 in range(0, LH, per):
                                wait(s_sB, l * NSB + n + 1)
                                V.tensor_reduce(mx[:, TPB * bb + t, h0:h0 + per],
                                                bank[n % 4][:, 0:w * per].rearrange("p (h k) -> p h k", h=per),
                                                AX_X, ALU.max).then_inc(s_mB, 1)
                                n += 1
                    wait(s_mB, l * NSB + NSB)
                    max_split(1 + l)
                    for g in range(NB * LH // 2):
                        k = l * NB * LH // 2 + g
                        bb, p = g // (LH // 2), g % (LH // 2)
                        wait(s_vB, k + 1)
                        src = bank[2 + g % 2][:, 0:4 * (LD + 1)].rearrange("p (t e x) -> p t e x", t=TPB, e=2)
                        r = rsum[:, TPB * bb:TPB * bb + TPB, 2 * p:2 * p + 2]
                        V.reciprocal(r.unsqueeze(3), src[:, :, :, LD:LD + 1]).then_inc(s_qB, 1)
                        wait(s_qB, k + 1)
                        V.tensor_tensor(o_tok[:, TPB * bb:TPB * bb + TPB, 2 * p:2 * p + 2, :], src[:, :, :, 0:LD],
                                        r.unsqueeze(3).to_broadcast([128, TPB, 2, LD]), ALU.mult).then_inc(s_nB, 1)
                    wait(s_yB, l + 1)
                    V.tensor_tensor(fT[:, :], fT[:, :], bank[0][:, :], ALU.add).then_inc(s_zz, 1)
                    wait(s_zz, l + 1)
                    shifted().then_inc(s_hh, 1)
                    wait(s_hh, 2 * l + 2)
                    V.sem_inc(s_src, 1)
                    norm_dve(2 + l, hT[:, :, :].rearrange("p b n -> p (b n)"), nT[:, :])
                    wait(s_norm, 3 + l)
                    V.tensor_scalar(nT[:, :], nT[:, :], vcol[:, V_LG + l:V_LG + l + 1], vcol[:, V_LB + l:V_LB + l + 1],
                                    ALU.mult, ALU.add).then_inc(s_af, 1)
                    for c, (c0, w) in enumerate(HCH):
                        wait(s_f2, l * len(HCH) + c + 1)
                        v = V_B1 + l * 2 * len(HCH) + c
                        V.scalar_tensor_tensor(out=hid[0:w, c, :], in0=bank[2 + 2 * c][0:w, :], scalar=vcol[0:w, v:v + 1],
                                               in1=gel[0:w, c, :], op0=ALU.add, op1=ALU.mult).then_inc(s_f3, 1)
                    wait(s_f4, l + 1)
                    V.scalar_tensor_tensor(out=fT[:, :], in0=bank[0][:, :], scalar=vcol[:, V_B2 + l:V_B2 + l + 1],
                                           in1=fT[:, :], op0=ALU.add, op1=ALU.add).then_inc(s_f5, 1)
                wait(s_f5, LAYERS)
                V.scalar_tensor_tensor(out=xT[:, :], in0=fT[:, :], scalar=tg[:, 2:3], in1=xT[:, :],
                                       op0=ALU.mult, op1=ALU.add).then_inc(s_src, 1)
                wait(s_src, 5)
                norm_dve(4, xT[:, :], nT[:, :])
                wait(s_cq, 1)
                srcs = (bank[2][:, :], flat(kv_c[:, 0]))
                for n in range(2):
                    V.tensor_scalar(f_min[:, n, :], srcs[n], 0.0, None, ALU.min).then_inc(s_fm, 1)
                for n in range(2):
                    wait(s_fe, n + 1)
                    V.scalar_tensor_tensor(out=flat(feat[:, n]), in0=srcs[n], scalar=0.0, in1=f_exp[:, n, :],
                                           op0=ALU.max, op1=ALU.add).then_inc(s_ff, 1)
                wait(s_cu, 1)
                for g in range(4):
                    for j in range(4):
                        h = 4 * g + j
                        last = V.tensor_scalar(qh[:, h, :], fqT[:, :], cf[:, C_HEAD + h:C_HEAD + h + 1], None, ALU.mult)
                    last.then_inc(s_qh, 1)
                wait(s_m0, 1)
                V.tensor_tensor(m0[:, :, :], bank[1][:, 0:256].rearrange("p (b n) -> p b n", b=NB),
                                diag.unsqueeze(1).to_broadcast([128, NB, 128]), ALU.mult).then_inc(s_m1, 1)
                for n in range(4 * T):
                    wait(s_ca, n + 1)
                    if n >= 3:
                        wait(s_am, n - 2)
                    V.tensor_tensor(am[:, n % 3, :].rearrange("p (h i) -> p h i", h=4),
                                    bank[5 + n % 3][:, :].rearrange("p (h i) -> p h i", h=4),
                                    causal.unsqueeze(1).to_broadcast([128, 4, 128]), ALU.mult).then_inc(s_cm, 1)
                wait(s_nu, 1)
                V.tensor_tensor(den[:, :], flat(feat[:, 0]), bank[3][:, :], ALU.mult).then_inc(s_de, 1)
                wait(s_de, 1)
                V.tensor_scalar(den[:, :], den[:, :], 1e-6, None, ALU.add).then_inc(s_de, 1)
                wait(s_de, 2)
                V.reciprocal(rden[:, :], den[:, :]).then_inc(s_de, 1)
                wait(s_de, 3)
                wait(s_am, 4 * T)
                V.tensor_tensor(flat(nv), bank[2][:, :], rden[:, :], ALU.mult).then_inc(s_de, 1)
                wait(s_yc, 1)
                V.tensor_scalar(yC[:, :], bank[5][:, :], tg[:, 1:2], bog[:, :], ALU.mult, ALU.add).then_inc(s_yd, 1)
                wait(s_yd, 1)
                V.tensor_tensor(xT[:, :], yC[:, :], xT[:, :], ALU.add).then_inc(s_src, 1)
                wait(s_src, 6)
                norm_dve(5, xT[:, :], nT[:, :])
                wait(s_le, 1)
                V.tensor_scalar(flat(r_1), flat(r_e), 1.0, None, ALU.add).then_inc(s_la, 1)
                wait(s_la, 1)
                V.reciprocal(flat(aff), flat(r_1)).then_inc(s_la, 1)
                wait(s_la, 2)
                for t in range(T):
                    V.max(top[:, t, :], aff[:, t, :]).then_inc(s_tk, 1)
                for t in range(T):
                    wait(s_tk, t + 1)
                    V.match_replace(rep[:, t, :], top[:, t, :], aff[:, t, :], -1.0).then_inc(s_tk, 1)
                V.tensor_reduce(tsum[:, :], top[:, :, :], AX_X, ALU.add).then_inc(s_tw, 1)
                wait(s_tw, 1)
                V.tensor_scalar(tsum[:, :], tsum[:, :], 1e-9, None, ALU.add).then_inc(s_tw, 1)
                wait(s_tw, 2)
                V.reciprocal(tinv[:, :], tsum[:, :]).then_inc(s_tw, 1)
                wait(s_tk, 2 * T)
                V.scalar_tensor_tensor(out=flat(w_m), in0=flat(rep), scalar=-1.0, in1=flat(aff),
                                       op0=ALU.is_equal, op1=ALU.mult).then_inc(s_tw, 1)
                wait(s_tw, 4)
                V.tensor_tensor(w_t[:, :, :], w_m[:, :, :], tinv[:, :].unsqueeze(2).to_broadcast([128, T, E]), ALU.mult)\
                 .then_inc(s_tw, 1)
                wait(s_tw, 5)
                split(0, w_t[:, :, :], w_p[:, :, 0, :], w_p[:, :, 1, :], w_p[:, :, 2, :], w_res[:, :, :], s_wp, 0)
                for n in range(PAIRS + 1):
                    m = 128 if n < PAIRS else I
                    v = V_BU + n if n < PAIRS else V_BUS
                    wait(s_sg, n + 1)
                    wait(s_u, n + 1)
                    if n >= 2:
                        wait(s_dn, n - 1)
                    dst = up if n < PAIRS else hm
                    last = V.scalar_tensor_tensor(out=dst[0:m, n % 2, :], in0=bank[3 + 3 * (n % 2)][0:m, :],
                                                  scalar=vcol[0:m, v:v + 1], in1=sg[0:m, n % 2, :],
                                                  op0=ALU.add, op1=ALU.mult)
                    last.then_inc(s_up, 1)
                    wait(s_up, n + 1)
                    if n < PAIRS:
                        V.tensor_tensor(hm[:, n % 2, :], up[:, n % 2, :], bank[4 + 3 * (n % 2)][:, :], ALU.mult)\
                         .then_inc(s_hm, 1)
                    else:
                        V.sem_inc(s_hm, 1)
                wait(s_dn, PAIRS + 1)
                V.tensor_scalar(yD[:, :], bank[0][:, :], vcol[:, V_BDS:V_BDS + 1], tg[:, 3:4], ALU.add, ALU.mult)\
                 .then_inc(s_y1, 1)
                wait(s_y1, 1)
                V.tensor_tensor(xT[:, :], yD[:, :], xT[:, :], ALU.add).then_inc(s_x4, 1)
                wait(s_xo, 1)
                dve.drain().then_inc(s_endD, 1)


_OUT = ((B, N, D), "float32")


def kernel(**inputs):
    import numpy as _np
    import ml_dtypes as _ml
    import concourse.bacc as _bacc
    from concourse import mybir as _mybir
    from concourse.bass_utils import run_bass_kernel_spmd as _run

    nc = _bacc.Bacc("TRN2", target_bir_lowering=False, num_devices=1)
    c_f32, c_bf16 = shape_constants()
    arrays, args = {}, {}
    for name, v in list(inputs.items()) + [("c_f32", c_f32), ("c_bf16", c_bf16.astype(_ml.bfloat16))]:
        v = _np.ascontiguousarray(v)
        arrays[f"in_{name}"] = v
        args[name] = nc.dram_tensor(f"in_{name}", v.shape, _mybir.dt.from_np(v.dtype), kind="ExternalInput").ap()
    shape, dtype = _OUT
    out = nc.dram_tensor("out_0", shape, _mybir.dt.from_np(_np.dtype(dtype)), kind="ExternalOutput").ap()
    flamingo(nc, args, out)
    r = _run(nc, [arrays], core_ids=[0])
    return r.results[0]["out_0"]
```

```python
from contextlib import ExitStack

import numpy as np
import concourse.bass as bass
from concourse import mybir

F32 = mybir.dt.float32
BF16 = mybir.dt.bfloat16
ALU = mybir.AluOpType
ACT = mybir.ActivationFunctionType
AX_X = mybir.AxisListType.X

B, N, D = 8, 256, 128
NB = 2
TURNS = B // NB
TPB = N // 128
T = NB * TPB
TOK = T * 128
H, DH = 16, 8
SLOT = 64
LH, LD, WIN = 8, 64, 64
LAYERS = 2
INNER = LH * LD
HID = int(D * 4 * 2 / 3)
HCH = [(c, min(128, HID - c)) for c in range(0, HID, 128)]
E, I, TOPK = 32, 64, 8
PAIRS = E // 2
VS = 9 * 9
EPS = 1e-5
NEG = -1.0e30

C_ID, C_CAUSAL, C_ONES, C_MEAN, C_ROT = 0, 128, 256, 384, 512
ROTW = TPB * 2 * 2 * LD
C_ALL = C_ROT + ROTW
K_ID, K_MQ, K_MK, K_MAX, K_SEL = 0, 128, 320, 512, 512 + H * 128
K_ALL = K_SEL + PAIRS * 128
V_BG, V_BU = 0, PAIRS
V_LG, V_LB, V_B2 = 2 * PAIRS, 2 * PAIRS + LAYERS, 2 * PAIRS + 2 * LAYERS
V_B1 = V_B2 + LAYERS
V_BO = V_B1 + LAYERS * 2 * len(HCH)
V_BDS, V_BGS, V_BUS, V_ALL = V_BO + 1, V_BO + 2, V_BO + 3, V_BO + 4


def b1_column(layer, half, chunk):
    return V_B1 + chunk * 2 * LAYERS + 2 * layer + half


def shape_constants():
    p = np.arange(128)[:, None]
    f = np.arange(128)[None, :]
    c = np.zeros((128, C_ALL), np.float32)
    c[:, C_ID:C_ID + 128] = p == f
    c[:, C_CAUSAL:C_CAUSAL + 128] = p <= f
    c[:, C_ONES:C_ONES + 128] = 1
    c[:, C_MEAN:C_MEAN + 128] = 1.0 / D
    half = np.arange(0, LD, 2, dtype=np.float32)
    inv = np.float32(1.0) / np.float32(10000.0) ** (half / np.float32(LD))
    t = np.arange(N, dtype=np.float32)
    ang = np.concatenate([t[:, None] * inv[None, :]] * 2, 1).astype(np.float32)
    base = ((half + np.float32(0.4 * LD)) / np.float32(1.4 * LD)).astype(np.float32)
    power = (t - N // 2) / np.float32(WIN // 2)
    sc = np.concatenate([base[None, :] ** power[:, None]] * 2, 1).astype(np.float32)
    sign = np.where(np.arange(LD) < LD // 2, -1.0, 1.0).astype(np.float32)[None, :]
    rot = np.zeros((128, TPB, 2, 2, LD), np.float32)
    for tile in range(TPB):
        r = slice(128 * tile, 128 * tile + 128)
        for qk, s in ((0, sc[r]), (1, 1 / sc[r])):
            rot[:, tile, qk, 0] = np.cos(ang[r]) * s
            rot[:, tile, qk, 1] = np.sin(ang[r]) * s * sign
    c[:, C_ROT:] = rot.reshape(128, -1)

    k = np.zeros((128, K_ALL), np.float32)
    k[:, K_ID:K_ID + 128] = p == f
    key = np.arange(WIN + 128)[None, :] - WIN
    k[:, K_MQ:K_MQ + 192] = np.where((key <= p) & (key >= p - WIN), 0, NEG)
    q = np.arange(128 + WIN)[None, :]
    k[:, K_MK:K_MK + 192] = np.where((p <= q) & (q <= p + WIN), 0, NEG)
    for h in range(H):
        for part in range(3):
            k[part * H + h, K_MAX + h * 128:K_MAX + h * 128 + 128] = -1
    for pr in range(PAIRS):
        for part in range(3):
            for e in range(2):
                at = K_SEL + pr * 128 + e * 64
                k[part * E + 2 * pr + e, at:at + 64] = 1
    return c, k


def flamingo(nc, a, out):
    with ExitStack() as ctx:
        def sb(name, shape, dt=F32):
            return ctx.enter_context(nc.sbuf_tensor(name, shape, dt))

        SET = 3
        turn_sems = []

        def sem(name):
            s = ctx.enter_context(nc.semaphore(name))
            turn_sems.append(s)
            return s

        bank = [ctx.enter_context(nc.psum_tensor(f"bank{i}", [128, 512], F32)) for i in range(8)]

        proj = (3, 4, 5, 6, 7, 2)
        ffb = ((3, 4, 5), (6, 7, 2))

        def cols(b):
            return slice(N * b, N * b + N)

        def bbank(i):
            return bank[i][:, :].bitcast(BF16)

        cf = sb("cf", [128, C_ALL])
        cb = sb("cb", [128, K_ALL], BF16)
        ident, causal = cf[:, C_ID:C_ID + 128], cf[:, C_CAUSAL:C_CAUSAL + 128]
        ones, mean = cf[:, C_ONES:C_ONES + 128], cf[:, C_MEAN:C_MEAN + 128]
        identb = cb[:, K_ID:K_ID + 128]
        rot_c = cf[:, C_ROT:].rearrange("p (t k w d) -> p t k w d", t=TPB, k=2, w=2)
        w_a = sb("w_a", [128, 3, 128])
        w_c = sb("w_c", [128, 4, 128])
        row = sb("row", [1, 3 * 128 + E])
        w_qkv = sb("w_qkv", [128, LAYERS, 3 * INNER])
        w_o = sb("w_o", [128, LAYERS, INNER // 128, D])
        w_1 = sb("w_1", [128, LAYERS, 2 * HID])
        w_2 = sb("w_2", [128, LAYERS, len(HCH), D])
        w_r = sb("w_r", [128, E])
        w_gs = sb("w_gs", [128, 2, I])
        w_ds = sb("w_ds", [I, D])
        w_g = sb("w_g", [128, E, I])
        w_u = sb("w_u", [128, E, I])
        w_d = sb("w_d", [128, PAIRS, D])
        b_d = sb("b_d", [E, D])
        vcol = sb("vcol", [128, V_ALL])
        gate = sb("gate", [128, 4])
        tg = sb("tg", [128, 4])
        qksc = sb("qksc", [128, LAYERS, 2, LD])
        rot = sb("rot", [128, LAYERS, TPB, 2, 2, LD])
        bog = sb("bog", [128, 1])

        x_tok = sb("x_tok", [128, T, D])
        c_tok = sb("c_tok", [128, T, D])
        cT = sb("cT", [128, TOK])
        xT = sb("xT", [128, TOK])
        ln_c, ln_sq, ln_r = (sb(n, [128, TOK]) for n in ("ln_c", "ln_sq", "ln_r"))
        nT = sb("nT", [128, TOK])
        kv_c = sb("kv_c", [128, 2, T, D])
        mx = sb("mx", [128, T, H])
        mx_r = sb("mx_r", [128, T, H])
        mx_p = sb("mx_p", [128, T, 3, H], BF16)
        mxT = sb("mxT", [3 * H, TOK], BF16)
        PT = sb("PT", [128, 4, 2, N])
        oraw = sb("oraw", [128, 2, 512])
        rsum = sb("rsum", [128, T, H])
        att = sb("att", [128, T, D])
        order = nc.dram_tensor("order_dram", (NB, H, N, DH), F32, kind="Internal").ap()
        fT = sb("fT", [128, TOK])
        hT = sb("hT", [128, NB, N])
        lqT = sb("lqT", [128, 2, 4, TOK])
        qS = lqT[:, :, :, :].rearrange("p e a n -> p (e a n)").bitcast(BF16)\
            .rearrange("p (e a n) -> p e a n", e=2, a=H // 2)
        qk_sq = sb("qk_sq", [128, 2, INNER])
        qk_ss = sb("qk_ss", [128, 2 * T, LH])
        qk_lg = sb("qk_lg", [128, 2 * T, LH])
        qk_in = sb("qk_in", [128, 2 * T, LH])
        lv = sb("lv", [128, T, LH, LD + 1])
        r_e, r_1, aff, rep = (sb(n, [128, T, E]) for n in ("r_e", "r_1", "aff", "rep"))
        top = sb("top", [128, T, TOPK])
        tsum, tinv = sb("tsum", [128, T]), sb("tinv", [128, T])
        w_m, w_t, w_res = (sb(n, [128, T, E]) for n in ("w_m", "w_t", "w_res"))
        w_p = sb("w_p", [128, T, 3, E], BF16)
        wS = sb("wS", [3 * E, TOK], BF16)
        wT = sb("wT", [E, TOK])
        o_out = sb("o_out", [128, T, D])

        arena = sb("arena", [128, 3 * 8 * INNER])
        arena2 = sb("arena2", [128, 4 * TOK])

        def part(at, cols, tile=arena):
            return tile[:, at:at + cols]

        w_raw = part(0, 384).rearrange("p (k n) -> p k n", k=3)
        vrow = arena[0:V_ALL, 512:640]
        stack = part(0, 2048).bitcast(BF16).rearrange("p (t h s) -> p t h s", t=T, h=H)
        kS = part(2048, 2048).bitcast(BF16).rearrange("p (a n) -> p a n", a=H // 2)
        part_f = part(4096, TOK)
        part_h, part_m, part_l = (part(4608 + 256 * n, 256).bitcast(BF16) for n in range(3))
        va = part(5376, 2 * T * 8 * VS).rearrange("p (t g x) -> p t g x", t=T, g=2)
        va_one = part(5376, 2 * T * 8 * VS).rearrange("p (t x) -> p t x", x=VS)[:, :, DH:DH + 1]
        qk, qk_c, qk_s = (part(4096 * n, 4096).rearrange("p (m h d) -> p m h d", m=2 * T, h=LH) for n in range(3))
        o_tok = part(8192, 2048).rearrange("p (t h d) -> p t h d", t=T, h=LH)
        oT = part(10240, 2048).rearrange("p (c n) -> p c n", c=4)
        gel, hid = (part(1536 * n, 1536).rearrange("p (c n) -> p c n", c=len(HCH)) for n in range(2))
        lkT = part(0, 2048, arena2).rearrange("p (c n) -> p c n", c=4)
        OUTER = H * DH * DH
        kf_min, kf_exp = part(10560, TOK), part(11072, TOK)
        kf, vc = kv_c[:, 0], kv_c[:, 1]
        outer = part(8192, T * OUTER).rearrange("p (t n) -> p t n", t=T)
        prod = part(4096, 2 * OUTER).rearrange("p (r n) -> p r n", r=2)
        qf, qf_min, qf_exp = (part(512 * n, TOK, arena2) for n in range(3))
        den, rden, nv, nvT, yC = ln_sq, ln_r, att, ln_c, ln_sq
        sg, up, hm = (part(1024 * n, 1024).rearrange("p (r n) -> p r n", r=2) for n in range(3))
        yD = ln_sq

        bias_loads = [(vrow[V_BG:V_BG + PAIRS, :], a["L1_ffn_bg"].rearrange("(p e) i -> p (e i)", e=2)),
                 (vrow[V_BU:V_BU + PAIRS, :], a["L1_ffn_bu"].rearrange("(p e) i -> p (e i)", e=2)),
                 (vrow[V_LG:V_LG + LAYERS, :], a["L0_ffn_ln_g"]),
                 (vrow[V_LB:V_LB + LAYERS, :], a["L0_ffn_ln_b"]),
                 (vrow[V_B2:V_B2 + LAYERS, :], a["L0_ffn_b2"]),
                 (vrow[V_BO:V_BO + 1, :], a["L1_xattn_bo"].rearrange("(a n) -> a n", a=1)),
                 (vrow[V_BDS:V_BDS + 1, :], a["L1_ffn_bd_s"].rearrange("(a n) -> a n", a=1)),
                 (vrow[V_BGS:V_BGS + 1, 0:I], a["L1_ffn_bg_s"].rearrange("(a n) -> a n", a=1)),
                 (vrow[V_BUS:V_BUS + 1, 0:I], a["L1_ffn_bu_s"].rearrange("(a n) -> a n", a=1))]
        halves = a["L0_ffn_b1"].rearrange("l (h n) -> (l h) n", h=2)
        for c, (c0, w) in enumerate(HCH):
            r = b1_column(0, 0, c)
            bias_loads += [(vrow[r:r + 2 * LAYERS, 0:w], halves[:, c0:c0 + w])]
        bias_loads += [(gate[:, 0:2], a["g_xattn"].rearrange("(a n) -> a n", a=1).to_broadcast([128, 2])),
                  (gate[:, 2:4], a["g_ffn"].rearrange("(a n) -> a n", a=1).to_broadcast([128, 2]))]
        for l in range(LAYERS):
            bias_loads += [(qksc[:, l, 0, :], a["L0_ffn_q_scale"][l:l + 1, :].to_broadcast([128, LD])),
                      (qksc[:, l, 1, :], a["L0_ffn_k_scale"][l:l + 1, :].to_broadcast([128, LD]))]
        local_loads = []
        for l in range(LAYERS):
            local_loads += [(w_qkv[:, l, :], a["L0_ffn_wqkv"][l]),
                      (w_o[:, l, :, :], a["L0_ffn_wo"][l].rearrange("(c p) n -> p c n", p=128)),
                      (w_1[:, l, :], a["L0_ffn_w1"][l])]
            local_loads += [(w_2[0:w, l, c, :], a["L0_ffn_w2"][l, c0:c0 + w, :]) for c, (c0, w) in enumerate(HCH)]
        expert_loads = [(w_r[:, :], a["L1_ffn_Wr"]), (w_gs[:, 0, :], a["L1_ffn_Wg_s"]),
                 (w_gs[:, 1, :], a["L1_ffn_Wu_s"]), (w_ds[:, :], a["L1_ffn_Wd_s"]),
                 (w_g[:, :, :], a["L1_ffn_Wg"].rearrange("e h i -> h e i")),
                 (w_u[:, :, :], a["L1_ffn_Wu"].rearrange("e h i -> h e i")),
                 (w_d[:, :, :], a["L1_ffn_Wd"].rearrange("(p e) i h -> (e i) p h", e=2)),
                 (b_d[:, :], a["L1_ffn_bd"])]

        s_const = sem("s_const")
        s_attnW = sem("s_attnW")
        s_biasW = sem("s_biasW")
        s_causalW = sem("s_causalW")
        s_localW = sem("s_localW")
        s_expertW = sem("s_expertW")
        s_zero = sem("s_zero")
        s_setT = sem("s_setT")
        s_set = sem("s_set")
        s_tanh = sem("s_tanh")
        s_out = sem("s_out")
        s_go = sem("s_go")
        turn_sems.clear()
        s_endP, s_endA, s_endD, s_endG = (sem(n) for n in ("s_endP", "s_endA", "s_endD", "s_endG"))
        s_load = sem("s_load")
        s_inT = sem("s_inT")
        s_cT = sem("s_cT")
        s_src = sem("s_src")
        s_mu, s_cen, s_sq, s_var = (sem(n) for n in ("s_mu", "s_cen", "s_sq", "s_var"))
        s_lg, s_rstd, s_norm = (sem(n) for n in ("s_lg", "s_rstd", "s_norm"))
        s_pj = sem("s_pj")
        s_pe = sem("s_pe")
        s_sp = sem("s_sp")
        s_seenP, s_seenA, s_seenD, s_seenG = (sem(n) for n in ("s_seenP", "s_seenA", "s_seenD", "s_seenG"))
        s_pad = sem("s_pad")
        s_st = sem("s_st")
        s_stT = sem("s_stT")
        s_stD = sem("s_stD")
        s_stK = sem("s_stK")
        s_stA = sem("s_stA")
        s_sA = sem("s_sA")
        s_mA = sem("s_mA")
        s_mp = sem("s_mp")
        s_mT = sem("s_mT")
        s_mS = sem("s_mS")
        s_zA = sem("s_zA")
        s_eA = sem("s_eA")
        s_oA = sem("s_oA")
        s_rA = sem("s_rA")
        s_tA = sem("s_tA")
        s_qA = sem("s_qA")
        s_nA = sem("s_nA")
        s_wrA = sem("s_wrA")
        s_rdA0, s_rdA1 = sem("s_rdA0"), sem("s_rdA1")
        s_yA = sem("s_yA")
        s_hh = sem("s_hh")
        s_pB = sem("s_pB")
        s_cB = sem("s_cB")
        s_s2 = sem("s_s2")
        s_ss = sem("s_ss")
        s_sm = sem("s_sm")
        s_sl = sem("s_sl")
        s_si = sem("s_si")
        s_rs = sem("s_rs")
        s_rc = sem("s_rc")
        s_ra = sem("s_ra")
        s_rn = sem("s_rn")
        s_tB = sem("s_tB")
        s_uB = sem("s_uB")
        NSB = NB * (LH // 4 + LH // 2)
        s_sB = sem("s_sB")
        s_mB = sem("s_mB")
        s_zB = sem("s_zB")
        s_eB = sem("s_eB")
        s_oB = sem("s_oB")
        s_rB = sem("s_rB")
        s_vB = sem("s_vB")
        s_qB = sem("s_qB")
        s_nB = sem("s_nB")
        s_wB = sem("s_wB")
        s_xB = sem("s_xB")
        s_yB = sem("s_yB")
        s_zz = sem("s_zz")
        s_af = sem("s_af")
        s_f1 = sem("s_f1")
        s_f2 = sem("s_f2")
        s_f3 = sem("s_f3")
        s_f4 = sem("s_f4")
        s_f5 = sem("s_f5")
        s_cq = sem("s_cq")
        s_km = sem("s_km")
        s_ke = sem("s_ke")
        s_kf = sem("s_kf")
        s_ov = sem("s_ov")
        s_cs = sem("s_cs")
        s_zs = sem("s_zs")
        s_fm = sem("s_fm")
        s_fe = sem("s_fe")
        s_ff = sem("s_ff")
        s_pr = sem("s_pr")
        s_rd = sem("s_rd")
        s_de = sem("s_de")
        s_nn = sem("s_nn")
        s_nt = sem("s_nt")
        s_nc = sem("s_nc")
        s_yc = sem("s_yc")
        s_yd = sem("s_yd")
        s_lo = sem("s_lo")
        s_le = sem("s_le")
        s_la = sem("s_la")
        s_tk = sem("s_tk")
        s_tw = sem("s_tw")
        s_wp = sem("s_wp")
        s_wq = sem("s_wq")
        s_wr = sem("s_wr")
        s_g = sem("s_g")
        s_u = sem("s_u")
        s_rp = sem("s_rp")
        s_sg = sem("s_sg")
        s_up = sem("s_up")
        s_hm = sem("s_hm")
        s_dn = sem("s_dn")
        s_y1 = sem("s_y1")
        s_x4 = sem("s_x4")
        s_xt = sem("s_xt")
        s_xo = sem("s_xo")

        turn_range = range(turn_sems[0].num, turn_sems[-1].num + 1)
        assert len(turn_range) == len(turn_sems)
        block = ctx.enter_context(nc.Block())

        def flat(t):
            return t.rearrange("p t d -> p (t d)")

        @block.sync
        def _(sp):
            sp.dma_start(cf[:, :], a["c_f32"]).then_inc(s_const, 16)
            for n, c in enumerate("qkv"):
                sp.dma_start(w_raw[:, n, :], a[f"L0_xattn_W{c}"]).then_inc(s_attnW, 16)
            sp.dma_start(cb[:, :], a["c_bf16"]).then_inc(s_const, 16)

            def load(turn):
                for src, dst in ((a["x"], x_tok), (a["ctx_1024"], c_tok)):
                    sp.dma_start(dst[:, :, :], src.rearrange("(i b) (t p) d -> i p (b t) d", b=NB, p=128)[turn])\
                      .then_inc(s_load, 16)

            load(0)
            for n, c in enumerate("kvqo"):
                sp.dma_start(w_c[:, "qkvo".index(c), :], a[f"L1_xattn_W{c}"]).then_inc(s_causalW, 16)
            for n, c in enumerate("qkv"):
                sp.dma_start(row[0:1, 128 * n:128 * n + 128], a[f"L1_xattn_b{c}"].rearrange("(a n) -> a n", a=1))\
                  .then_inc(s_causalW, 16)
            sp.dma_start(row[0:1, 384:384 + E], a["L1_ffn_br"].rearrange("(a n) -> a n", a=1)).then_inc(s_causalW, 16)
            sp.wait_ge(s_const, 32)
            sp.wait_ge(s_load, 32)
            sp.sem_clear(s_load)
            sp.sem_inc(s_go, 1)
            with sp.Fori(0, TURNS) as it:
                for bb, s_back in ((0, s_rdA0), (1, s_rdA1)):
                    sp.wait_ge(s_nA, bb + 1)
                    for t in range(TPB):
                        sp.dma_start(order[bb, :, 128 * t:128 * t + 128, :].rearrange("h q d -> q h d"),
                                     att[:, TPB * bb + t, :].rearrange("p (h d) -> p h d", d=DH)).then_inc(s_wrA, 16)
                    sp.wait_ge(s_wrA, 32 * (bb + 1))
                    sp.dma_start(x_tok[:, TPB * bb:TPB * bb + TPB, :],
                                 order[bb].rearrange("h (a b) d -> (h a) (b d)", b=16).rearrange("(t p) c -> p t c", p=128))\
                      .then_inc(s_back, 16)
                sp.wait_ge(s_yA, NB)
                load((it + 1) % TURNS)
                sp.wait_ge(s_xo, 1)
                sp.dma_start(out.rearrange("(i b) (t p) d -> i p (b t) d", b=NB, p=128)[it], o_out[:, :, :])\
                  .then_inc(s_out, 16)
                for s in (s_endP, s_endA, s_endD, s_endG):
                    sp.wait_ge(s, 1)
                sp.wait_ge(s_load, 32)
                sp.sem_clear(turn_range)
                sp.sem_inc(s_go, 1)
                sp.wait_ge(s_out, 16)
                sp.sem_clear(s_out)

        @block.gpsimd
        def _(pool):
            for dst, src in local_loads:
                pool.dma_start(dst, src).then_inc(s_localW, 16)
            for dst, src in expert_loads:
                pool.dma_start(dst, src).then_inc(s_expertW, 16)
            pool.wait_ge(s_set, SET)

            with pool.Fori(0, TURNS) as it:
                pool.wait_ge(s_go, it + 1)

                def wait(s, k):
                    pool.wait_ge(s, k)

                pool.sem_inc(s_seenG, 1)
                wait(s_seenG, 1)
                nc.gpsimd.memset(stack[:, :, :, 48:SLOT], 0.0)
                nc.gpsimd.memset(va[:, :, :, :], 0.0).then_inc(s_pad, 1)
                wait(s_pad, 1)
                nc.gpsimd.memset(va_one, 1.0).then_inc(s_pad, 1)
                wait(s_pe, 2)
                nc.gpsimd.tensor_scalar(kf_min[:, :], flat(kf), 0.0, None, ALU.min).then_inc(s_km, 1)
                for l in range(LAYERS):
                    for m in range(2 * T):
                        wait(s_cB, l * 3 * T + 3 * (m // 2) + m % 2 + 1)
                        tab = rot[:, l, (m // 2) % TPB, m % 2, 1, :].unsqueeze(1)
                        h2 = LD // 2
                        nc.gpsimd.tensor_tensor(qk_s[:, m, :, 0:h2], qk[:, m, :, h2:LD],
                                                tab[:, :, 0:h2].to_broadcast([128, LH, h2]), ALU.mult)
                        nc.gpsimd.tensor_tensor(qk_s[:, m, :, h2:LD], qk[:, m, :, 0:h2],
                                                tab[:, :, h2:LD].to_broadcast([128, LH, h2]), ALU.mult)\
                          .then_inc(s_rs, 1)
                wait(s_yB, NB * LAYERS)
                wait(s_kf, 1)
                for t in range(T):
                    nc.gpsimd.tensor_tensor(
                        outer[:, t, :].rearrange("p (h a d) -> p h a d", h=H, a=DH),
                        kf[:, t, :].rearrange("p (h a) -> p h a", h=H).unsqueeze(3).to_broadcast([128, H, DH, DH]),
                        vc[:, t, :].rearrange("p (h d) -> p h d", h=H).unsqueeze(2).to_broadcast([128, H, DH, DH]),
                        ALU.mult).then_inc(s_ov, 1)
                wait(s_xo, 1)
                pool.drain().then_inc(s_endG, 1)

        @block.tensor
        def _(pe):
            mm, tr = nc.tensor.matmul, nc.tensor.transpose
            pe.wait_ge(s_const, 32)
            pe.wait_ge(s_attnW, 3 * 16)
            for n in range(3):
                tr(bank[0][:, 128 * n:128 * n + 128], w_raw[:, n, :], ident)
            pe.wait_ge(s_biasW, 16 * len(bias_loads))
            tr(bank[1][:, 0:V_ALL], vrow[:, :], ident[0:V_ALL, 0:V_ALL]).then_inc(s_setT, 1)
            pe.wait_ge(s_set, SET)
            with pe.Fori(0, TURNS) as it:
                pe.wait_ge(s_go, it + 1)
                pe.sem_inc(s_seenP, 1)

                def wait(s, k):
                    pe.wait_ge(s, k)

                def mean_pe(src, b, to, ready, count):
                    wait(ready, count)
                    mm(bank[to][:, cols(b)], mean, src[:, cols(b)], start=True, stop=True).then_inc(s_mu, 1)

                def var_pe(stage, b, to):
                    wait(s_sq, NB * stage + b + 1)
                    mm(bank[to][:, cols(b)], mean, ln_sq[:, cols(b)], start=True, stop=True).then_inc(s_var, 1)

                def max_transposed(n, to):
                    wait(s_mp, 4 * n + 4)
                    for t in range(T):
                        last = tr(bbank(to)[0:3 * H, 128 * t:128 * t + 128],
                                  mx_p[:, t, :, :].rearrange("p a h -> p (a h)"), identb)
                    last.then_inc(s_mT, 1)
                    wait(s_mS, n + 1)

                for n, src in enumerate((x_tok, c_tok)):
                    for t in range(T):
                        last = tr(bank[n][:, 128 * t:128 * t + 128], src[:, t, :], ident)
                    last.then_inc(s_inT, 1)

                mean_pe(xT, 0, 0, s_src, NB)
                wait(s_cT, 1)
                mean_pe(xT, 1, 1, s_src, NB)

                def context(n, w):
                    for t in range(T):
                        o = bank[2 + n][:, 128 * t:128 * t + 128]
                        last = mm(o, cT[:, 128 * t:128 * t + 128], w, start=True, stop=n < 2)
                        if n >= 2:
                            last = mm(o, ones[0:1, :], row[0:1, 128 * (n - 1):128 * n], start=False, stop=True)
                    last.then_inc(s_pj, 1)

                context(0, w_a[:, 1, :])
                for b in range(NB):
                    var_pe(0, b, b)
                context(1, w_a[:, 2, :])
                wait(s_causalW, 8 * 16)
                context(2, w_c[:, 1, :])
                context(3, w_c[:, 2, :])

                def stack_transposed(n):
                    wait(s_st, n + 1)
                    for t in range(T):
                        if n == 0 and t == 1:
                            wait(s_pe, 3)
                        if n == 1:
                            wait((s_stD, s_stK)[t % 2], t // 2 + 1)
                        for p in range(H // 2):
                            last = tr(bbank(2 + t)[:, 128 * p:128 * p + 128],
                                      stack[:, t, 2 * p:2 * p + 2, :].rearrange("p h s -> p (h s)"), identb)
                        last.then_inc(s_stT, 1)

                wait(s_pad, 2)
                stack_transposed(0)
                wait(s_norm, NB)
                for t in range(T):
                    last = mm(bank[6][:, 128 * t:128 * t + 128], nT[:, 128 * t:128 * t + 128], w_a[:, 0, :],
                              start=True, stop=True)
                last.then_inc(s_pj, 1)
                stack_transposed(1)
                ring = (0, 1, 6, 7)
                for t in range(T):
                    wait(s_stA, t + 1)
                    for p in range(H // 2):
                        n = t * (H // 2) + p
                        if n >= 4:
                            wait(s_mA, n - 3)
                        for e in range(2):
                            last = mm(bank[ring[n % 4]][:, 256 * e:256 * e + 256],
                                      qS[:, e, p, 128 * t:128 * t + 128],
                                      kS[:, p, N * (t // TPB):N * (t // TPB) + N], start=True, stop=True)
                        last.then_inc(s_sA, 1)
                max_transposed(0, 2)

                def score_A(n):
                    bb, p, kt = n // H, n % H // 2, n % 2
                    if n >= 3:
                        wait(s_eA, n - 2)
                    o = bank[3 + n % 3]
                    k0 = N * bb + 128 * kt
                    for e in range(2):
                        h = 2 * p + e
                        mm(o[:, N * e:N * e + N], cb[0:3 * H, K_MAX + 128 * h:K_MAX + 128 * h + 128],
                           mxT[:, N * bb:N * bb + N], start=(e == 0), stop=False, skip_group_check=True)
                    mm(o[:, :], kS[:, p, k0:k0 + 128], qS[:, :, p, N * bb:N * bb + N], start=False, stop=True,
                       skip_group_check=True).then_inc(s_zA, 1)

                def value_A(n):
                    bb, p, kt = n // H, n % H // 2, n % 2
                    wait(s_eA, n + 1)
                    g = p // 4
                    for e in range(2):
                        h8 = (2 * p + e) % 8
                        last = mm(bank[6 + bb][0:72, N * g:N * g + N],
                                  va[:, TPB * bb + kt, g, 72 * h8:72 * h8 + 72],
                                  PT[:, n % 4, e, 0:N], start=(p % 4 == 0 and kt == 0 and e == 0),
                                  stop=(p % 4 == 3 and kt == 1 and e == 1))
                    last.then_inc(s_oA, 1)

                def back_A(bb):
                    wait(s_rA, bb + 1)
                    for t in range(TPB):
                        for g in range(2):
                            last = tr(bank[1 + bb][:, 72 * (2 * t + g):72 * (2 * t + g) + 72],
                                      oraw[0:72, bb, N * g + 128 * t:N * g + 128 * t + 128], ident[0:72, 0:72])
                    last.then_inc(s_tA, 1)

                def result_A(bb):
                    wait((s_rdA0, s_rdA1)[bb], 16)
                    for t in range(TPB * bb, TPB * bb + TPB):
                        last = tr(bank[bb][:, 128 * t:128 * t + 128], x_tok[:, t, :], ident)
                    last.then_inc(s_yA, 1)

                LAG = 2
                for n in range(NB * H + LAG):
                    if n < NB * H:
                        score_A(n)
                    if n >= LAG:
                        value_A(n - LAG)
                    if n == H + LAG + 2:
                        back_A(0)
                    if n == NB * H - 2:
                        result_A(0)
                    if n == NB * H - 1:
                        mean_pe(xT, 0, 0, s_src, NB + 1)
                var_pe(1, 0, 0)
                back_A(1)

                wait(s_localW, 16 * len(local_loads))

                def project(l, t):
                    wait(s_hh, 2 * NB * l + t // TPB + 1)
                    for part in range(3):
                        n = 3 * t + part
                        if l == 0 and n == 5:
                            wait(s_nA, NB)
                        if n >= 6:
                            wait(s_cB, l * 3 * T + n - 5)
                        mm(bank[proj[n % 6]][:, :], hT[:, :, :].rearrange("p b n -> p (b n)")[:, 128 * t:128 * t + 128],
                           w_qkv[:, l, INNER * part:INNER * part + INNER], start=True, stop=True).then_inc(s_pB, 1)

                for l in range(LAYERS):
                    for t in range(T):
                        if l == 0 and t == TPB:
                            result_A(1)
                            mean_pe(xT, 1, 1, s_src, NB + 2)
                            var_pe(1, 1, 1)
                        project(l, t)
                    for m in range(2 * T):
                        wait(s_rn, l * 2 * T + m + 1)
                        if m < 6:
                            wait(s_cB, l * 3 * T + m + 7)
                        else:
                            wait(s_uB, l * 2 * T + m - 5)
                        for p in range(4):
                            last = tr(bank[proj[m % 6]][:, 128 * p:128 * p + 128],
                                      qk_c[:, m, 2 * p:2 * p + 2, :].rearrange("p h d -> p (h d)"), ident)
                        last.then_inc(s_tB, 1)
                    n = 0
                    for bb in range(NB):
                        wait(s_uB, l * 2 * T + 4 * bb + 4)
                        if bb == 0:
                            wait(s_uB, l * 2 * T + 2 * T)
                        for t, per in ((0, 4), (1, 2)):
                            w = 128 + WIN * t
                            for h0 in range(0, LH, per):
                                if n >= 4:
                                    wait(s_mB, l * NSB + n - 3)
                                for j in range(per):
                                    h = h0 + j
                                    o = bank[n % 4][:, w * j:w * j + w]
                                    q0 = N * bb + 128 * t
                                    mm(o, lqT[:, h % 2, h // 2, q0:q0 + 128],
                                       lkT[:, h // 2, q0 - WIN * t:q0 + 128], start=True, stop=False)
                                    last = mm(o, identb, cb[:, K_MQ + WIN * (1 - t):K_MQ + 192],
                                              start=False, stop=True)
                                last.then_inc(s_sB, 1)
                                n += 1
                    max_transposed(1 + l, 4)

                    def score_B(n):
                        bb, p, kt = n // LH, n % LH // 2, n % 2
                        w, k0 = 192 - 64 * kt, N * bb + 128 * kt
                        if n >= 3:
                            wait(s_eB, l * NB * LH + n - 2)
                        o = bank[5 + n % 3]
                        mm(o[:, 0:2 * w], lkT[:, p, k0:k0 + 128], lqT[:, :, p, k0:k0 + w],
                           start=True, stop=False, skip_group_check=True)
                        mm(o[:, 0:2 * w], identb, cb[:, K_MK:K_MK + w].unsqueeze(1).to_broadcast([128, 2, w]),
                           start=False, stop=False, skip_group_check=True)
                        for e in range(2):
                            h = 2 * p + e
                            last = mm(o[:, w * e:w * e + w], cb[0:3 * H, K_MAX + 128 * h:K_MAX + 128 * h + 128],
                                      mxT[:, k0:k0 + w], start=False, stop=e == 1, skip_group_check=True)
                        last.then_inc(s_zB, 1)

                    def value_B(g):
                        bb, p = g // (LH // 2), g % (LH // 2)
                        wait(s_eB, l * NB * LH + 2 * g + 2)
                        if g >= 2:
                            wait(s_rB, l * NB * LH // 2 + g - 1)
                        P = [PT[:, (2 * g + kt) % 4, :, :].rearrange("p a b -> p (a b)") for kt in range(2)]
                        for e in range(2):
                            o, h = bank[g % 2][0:LD + 1, N * e:N * e + N], 2 * p + e
                            mm(o[:, 0:192], lv[:, TPB * bb, h, :], P[0][:, 192 * e:192 * e + 192], start=True, stop=True)
                            last = mm(o[:, 128:256], lv[:, TPB * bb + 1, h, :], P[1][:, 128 * e:128 * e + 128],
                                      start=False, stop=True, skip_group_check=True)
                        last.then_inc(s_oB, 1)

                    def back_B(g):
                        base = l * NB * LH // 2
                        wait(s_rB, base + g + 1)
                        if g >= 2:
                            wait(s_nB, base + g - 1)
                        for t in range(TPB):
                            for e in range(2):
                                k = 2 * t + e
                                last = tr(bank[2 + g % 2][:, (LD + 1) * k:(LD + 1) * k + LD + 1],
                                          oraw[0:LD + 1, g % 2, N * e + 128 * t:N * e + 128 * t + 128],
                                          ident[0:LD + 1, 0:LD + 1])
                        last.then_inc(s_vB, 1)

                    groups = NB * LH // 2
                    for g in range(groups + 2):
                        if g < groups:
                            score_B(2 * g)
                            score_B(2 * g + 1)
                        if 1 <= g <= groups:
                            value_B(g - 1)
                        if g >= 2:
                            back_B(g - 2)
                    for t in range(T):
                        wait(s_nB, l * groups + (t // TPB + 1) * LH // 2)
                        for p in range(4):
                            last = tr(bank[4 + t][:, 128 * p:128 * p + 128],
                                      o_tok[:, t, 2 * p:2 * p + 2, :].rearrange("p h d -> p (h d)"), ident)
                        last.then_inc(s_wB, 1)
                    for b in range(NB):
                        wait(s_xB, l * T + TPB * (b + 1))
                        for c in range(4):
                            last = mm(bank[2 + b][:, cols(b)], w_o[:, l, c, :], oT[:, c, cols(b)], start=(c == 0), stop=(c == 3))
                        last.then_inc(s_yB, 1)
                    for b in range(NB):
                        mean_pe(hT[:, :, :].rearrange("p b n -> p (b n)"), b, b, s_hh, 2 * NB * l + NB + b + 1)
                    for b in range(NB):
                        var_pe(2 + l, b, b)
                    for b in range(NB):
                        wait(s_af, NB * l + b + 1)
                        for c, (c0, w) in enumerate(HCH):
                            for half in range(2):
                                at = half * HID + c0
                                last = mm(bank[ffb[b][c]][0:w, N * half:N * half + N], w_1[:, l, at:at + w], nT[:, cols(b)],
                                          start=True, stop=True)
                            last.then_inc(s_f1, 1)
                    for b in range(NB):
                        for c, (c0, w) in enumerate(HCH):
                            wait(s_f3, (NB * l + b) * len(HCH) + c + 1)
                            last = mm(bank[b][:, cols(b)], w_2[0:w, l, c, :], hid[0:w, c, cols(b)],
                                      start=(c == 0), stop=(c == len(HCH) - 1))
                        last.then_inc(s_f4, 1)

                def running(t):
                    wait(s_ov, t + 1)
                    if t >= 3:
                        wait(s_pr, 2 * (t - 2))
                    for half in range(2):
                        o = bank[2 + 2 * (t % 3) + half][:, :]
                        at = slice(512 * half, 512 * half + 512)
                        last = mm(o, causal, outer[:, t, at], start=True, stop=t % TPB == 0)
                        if t % TPB:
                            last = mm(o, ones, outer[:, t - 1, at], start=False, stop=True)
                        last.then_inc(s_cs, 1)

                running(0)
                for b in range(NB):
                    mean_pe(xT, b, b, s_src, 2 * NB + b + 1)
                running(1)
                for b in range(NB):
                    var_pe(4, b, b)
                running(2)
                for t in range(T):
                    wait(s_norm, 4 * NB + t // TPB + 1)
                    o = bank[0][:, 128 * t:128 * t + 128]
                    mm(o, nT[:, 128 * t:128 * t + 128], w_c[:, 0, :], start=True, stop=False)
                    last = mm(o, ones[0:1, :], row[0:1, 0:128], start=False, stop=True)
                last.then_inc(s_cq, 1)
                wait(s_kf, 1)
                for t in range(T):
                    o = bank[1][:, 128 * t:128 * t + 128]
                    last = mm(o, causal, kf[:, t, :], start=True, stop=t % TPB == 0)
                    if t % TPB:
                        last = mm(o, ones, kf[:, t - 1, :], start=False, stop=True)
                last.then_inc(s_zs, 1)
                running(3)
                for b in range(NB):
                    for t in range(TPB * b, TPB * b + TPB):
                        wait(s_nn, t + 1)
                        last = tr(bank[6 * b][:, 128 * t:128 * t + 128], nv[:, t, :], ident)
                    last.then_inc(s_nt, 1)
                    wait(s_nc, b + 1)
                    mm(bank[1 + 6 * b][:, cols(b)], w_c[:, 3, :], nvT[:, cols(b)], start=True, stop=True).then_inc(s_yc, 1)

                for b in range(NB):
                    mean_pe(xT, b, 4 + b, s_src, 3 * NB + b + 1)
                for b in range(NB):
                    var_pe(5, b, 4 + b)
                wait(s_expertW, 16 * len(expert_loads))
                for t in range(T):
                    wait(s_norm, 5 * NB + t // TPB + 1)
                    o = bank[1][:, E * t:E * t + E]
                    mm(o, nT[:, 128 * t:128 * t + 128], w_r[:, :], start=True, stop=False)
                    last = mm(o, ones[0:1, :], row[0:1, 384:384 + E], start=False, stop=True)
                last.then_inc(s_lo, 1)

                def gate_up(n):
                    m = 128 if n < PAIRS else I
                    if n < PAIRS:
                        gw = w_g[:, 2 * n:2 * n + 2, :].rearrange("p e i -> p (e i)")
                        uw = w_u[:, 2 * n:2 * n + 2, :].rearrange("p e i -> p (e i)")
                    else:
                        gw, uw = w_gs[:, 0, :], w_gs[:, 1, :]
                    if n >= 2:
                        wait(s_sg, n - 1)
                    mm(bank[2 + 3 * (n % 2)][0:m, :], gw, nT[:, :], start=True, stop=True).then_inc(s_g, 1)
                    if n >= 2:
                        wait(s_hm, n - 1)
                    mm(bank[3 + 3 * (n % 2)][0:m, :], uw, nT[:, :], start=True, stop=True).then_inc(s_u, 1)

                def weights(n):
                    mm(bank[4 + 3 * (n % 2)][:, :], cb[0:3 * E, K_SEL + 128 * n:K_SEL + 128 * n + 128],
                       wS[:, :], start=True, stop=True).then_inc(s_rp, 1)

                def down(n):
                    wait(s_hm, n + 1)
                    if n < PAIRS:
                        mm(bank[0][:, :], w_d[:, n, :], hm[:, n % 2, :], start=False, stop=False).then_inc(s_dn, 1)
                    else:
                        mm(bank[0][:, :], w_ds[:, :], hm[0:I, n % 2, :], start=False, stop=True).then_inc(s_dn, 1)

                gate_up(0)
                gate_up(1)
                wait(s_wp, 4)
                for t in range(T):
                    last = tr(bbank(7)[0:3 * E, 128 * t:128 * t + 128],
                              w_p[:, t, :, :].rearrange("p a e -> p (a e)"), identb)
                last.then_inc(s_wq, 1)
                for t in range(T):
                    last = tr(bank[4][0:E, 128 * t:128 * t + 128], w_t[:, t, :], ident)
                last.then_inc(s_wq, 1)
                wait(s_wr, 2)
                weights(0)
                weights(1)
                mm(bank[0][:, :], b_d[:, :], wT[:, :], start=True, stop=False)
                for n in range(2, PAIRS + 2):
                    if n <= PAIRS:
                        gate_up(n)
                        if n < PAIRS:
                            weights(n)
                    if n == 2:
                        down(0)
                    down(n - 1)
                wait(s_x4, 1)
                for t in range(T):
                    last = tr(bank[1][:, 128 * t:128 * t + 128], xT[:, 128 * t:128 * t + 128], ident)
                last.then_inc(s_xt, 1)
                wait(s_xo, 1)
                pe.drain().then_inc(s_endP, 1)

        @block.scalar
        def _(act):
            A = nc.scalar.activation
            act.wait_ge(s_zero, 1)
            for dst, src in bias_loads:
                act.dma_start(dst, src).then_inc(s_biasW, 16)
            act.wait_ge(s_biasW, 16 * len(bias_loads))
            A(tg[:, :], gate[:, :], ACT.Tanh).then_inc(s_tanh, 1)
            act.wait_ge(s_set, SET)
            with act.Fori(0, TURNS) as it:
                act.wait_ge(s_go, it + 1)
                act.sem_inc(s_seenA, 1)

                def wait(s, k):
                    act.wait_ge(s, k)

                def log_exp():
                    act.preload_act_table_set("natural_log_exp_and_others")

                def norm_act(stage, b, frm):
                    n = NB * stage + b + 1
                    wait(s_var, n)
                    A(ln_r[:, cols(b)], bank[frm][:, cols(b)], ACT.Ln, bias=EPS).then_inc(s_lg, 1)
                    wait(s_lg, n)
                    A(ln_r[:, cols(b)], ln_r[:, cols(b)], ACT.Exp, scale=-0.5).then_inc(s_rstd, 1)

                def max_act(n, frm):
                    wait(s_mT, n + 1)
                    A(mxT[:, :], bbank(frm)[0:3 * H, 0:TOK], ACT.Copy).then_inc(s_mS, 1)

                wait(s_inT, 2)
                A(cT[:, :], bank[1][:, :], ACT.Copy).then_inc(s_cT, 1)
                log_exp()
                for b in range(NB):
                    norm_act(0, b, b)
                wait(s_pj, 2)
                wait(s_pad, 2)
                for g in range(2):
                    last = A(va[:, :, g, :].rearrange("p t (h x) -> p t h x", x=VS)[:, :, :, 0:DH],
                             bank[3][:, :].rearrange("p (t g h d) -> p t g h d", t=T, g=2, h=8)[:, :, g], ACT.Copy)
                last.then_inc(s_pe, 1)
                for n in range(2):
                    wait(s_pj, 3 + n)
                    A(flat(kv_c[:, n]), bank[4 + n][:, :], ACT.Copy).then_inc(s_pe, 1)
                for t in range(1, T, 2):
                    wait(s_stT, t + 1)
                    A(kS[:, :, 128 * t:128 * t + 128], bbank(2 + t).rearrange("p (a n) -> p a n", a=H // 2), ACT.Copy)\
                        .then_inc(s_stK, 1)
                for t in range(T):
                    wait(s_stT, T + t + 1)
                    for e in range(2):
                        last = A(qS[64 * e:64 * e + 64, e, :, 128 * t:128 * t + 128],
                                 bbank(2 + t)[64 * e:64 * e + 64, :].rearrange("p (a n) -> p a n", a=H // 2), ACT.Copy)
                    last.then_inc(s_stA, 1)
                max_act(0, 2)
                for n in range(NB * H):
                    wait(s_zA, n + 1)
                    if n >= 4:
                        wait(s_oA, n - 3)
                    A(PT[:, n % 4, :, 0:N], bank[3 + n % 3][:, :].rearrange("p (e q) -> p e q", e=2), ACT.Exp,
                      scale=float(DH) ** -0.5).then_inc(s_eA, 1)
                    if n == 3:
                        wait(s_km, 1)
                        A(kf_exp[:, :], kf_min[:, :], ACT.Exp).then_inc(s_ke, 1)
                    if n == H + 2:
                        wait(s_oA, H)
                        A(oraw[0:72, 0, :], bank[6][0:72, :], ACT.Copy).then_inc(s_rA, 1)
                norm_act(1, 0, 0)
                wait(s_oA, NB * H)
                A(oraw[0:72, 1, :], bank[7][0:72, :], ACT.Copy).then_inc(s_rA, 1)

                for l in range(LAYERS):
                    def inverse(t):
                        wait(s_sm, l * T + t + 1)
                        A(qk_lg[:, 2 * t:2 * t + 2, :], qk_ss[:, 2 * t:2 * t + 2, :], ACT.Ln, scale=2.0 ** 20)\
                            .then_inc(s_sl, 1)
                        wait(s_sl, l * T + t + 1)
                        A(qk_in[:, 2 * t:2 * t + 2, :], qk_lg[:, 2 * t:2 * t + 2, :], ACT.Exp, scale=-0.5,
                          bias=float(10 * np.log(2.0))).then_inc(s_si, 1)

                    for t in range(T):
                        if l == 0 and t == TPB:
                            norm_act(1, 1, 1)
                        for part in range(3):
                            n = l * 3 * T + 3 * t + part
                            wait(s_pB, n + 1)
                            src = bank[proj[(3 * t + part) % 6]]
                            if part == 2:
                                A(lv[:, t, :, 0:LD], src[:, :].rearrange("p (h d) -> p h d", h=LH), ACT.Copy)\
                                    .then_inc(s_cB, 1)
                                continue
                            m = 2 * t + part
                            A(qk[:, m, :, :].rearrange("p h d -> p (h d)"), src[:, :], ACT.Copy).then_inc(s_cB, 1)
                            wait(s_cB, n + 1)
                            if m >= 2:
                                wait(s_ss, l * 2 * T + m - 1)
                            A(qk_sq[:, m % 2, :], qk[:, m, :, :].rearrange("p h d -> p (h d)"), ACT.Square)\
                                .then_inc(s_s2, 1)
                        if t:
                            inverse(t - 1)
                    inverse(T - 1)
                    for m in range(2 * T):
                        wait(s_tB, l * 2 * T + m + 1)
                        t, src = m // 2, bank[proj[m % 6]]
                        v = src[:, :].rearrange("p (a n) -> p a n", a=4)
                        if m % 2:
                            A(lkT[:, :, 128 * t:128 * t + 128], v, ACT.Copy).then_inc(s_uB, 1)
                        else:
                            for e in range(2):
                                last = A(lqT[64 * e:64 * e + 64, e, :, 128 * t:128 * t + 128],
                                         v[64 * e:64 * e + 64], ACT.Copy)
                            last.then_inc(s_uB, 1)
                    max_act(1 + l, 4)
                    base = l * NB * LH

                    def raw_B(g):
                        wait(s_oB, base // 2 + g + 1)
                        if g >= 2:
                            wait(s_vB, base // 2 + g - 1)
                        A(oraw[0:LD + 1, g % 2, :], bank[g % 2][0:LD + 1, :], ACT.Copy).then_inc(s_rB, 1)

                    for n in range(NB * LH):
                        w = 192 - 64 * (n % 2)
                        wait(s_zB, base + n + 1)
                        if n >= 4:
                            wait(s_oB, base // 2 + (n - 4) // 2 + 1)
                        A(PT[:, n % 4, :, :].rearrange("p a b -> p (a b)")[:, 0:2 * w], bank[5 + n % 3][:, 0:2 * w],
                          ACT.Exp, scale=8.0).then_inc(s_eB, 1)
                        if n >= 3 and n % 2:
                            raw_B((n - 3) // 2)
                    raw_B(NB * LH // 2 - 1)
                    for t in range(T):
                        wait(s_wB, l * T + t + 1)
                        A(oT[:, :, 128 * t:128 * t + 128], bank[4 + t][:, :].rearrange("p (a n) -> p a n", a=4),
                          ACT.Copy).then_inc(s_xB, 1)
                    for b in range(NB):
                        norm_act(2 + l, b, b)
                    for b in range(NB):
                        for c, (c0, w) in enumerate(HCH):
                            v = b1_column(l, 1, c)
                            wait(s_f1, (NB * l + b) * len(HCH) + c + 1)
                            A(gel[0:w, c, cols(b)], bank[ffb[b][c]][0:w, N:2 * N], ACT.Gelu, bias=vcol[0:w, v:v + 1])\
                                .then_inc(s_f2, 1)
                    log_exp()
                for b in range(NB):
                    norm_act(4, b, b)
                wait(s_fm, 1)
                A(qf_exp[:, :], qf_min[:, :], ACT.Exp).then_inc(s_fe, 1)
                for b in range(NB):
                    wait(s_nt, b + 1)
                    A(nvT[:, cols(b)], bank[6 * b][:, cols(b)], ACT.Copy).then_inc(s_nc, 1)
                for b in range(NB):
                    norm_act(5, b, 4 + b)
                wait(s_lo, 1)
                A(flat(r_e), bank[1][:, 0:T * E], ACT.Exp, scale=-1.0).then_inc(s_le, 1)
                for n in range(PAIRS + 1):
                    if n == 2:
                        wait(s_wq, 1)
                        A(wS[:, :], bbank(7)[0:3 * E, 0:TOK], ACT.Copy).then_inc(s_wr, 1)
                        wait(s_wq, 2)
                        A(wT[:, :], bank[4][0:E, :], ACT.Copy).then_inc(s_wr, 1)
                    m = 128 if n < PAIRS else I
                    v = V_BG + n if n < PAIRS else V_BGS
                    wait(s_g, n + 1)
                    if n >= 2:
                        wait(s_up, n - 1)
                    A(sg[0:m, n % 2, :], bank[2 + 3 * (n % 2)][0:m, :], ACT.Silu, bias=vcol[0:m, v:v + 1])\
                        .then_inc(s_sg, 1)
                wait(s_xt, 1)
                A(flat(o_out), bank[1][:, :], ACT.Copy).then_inc(s_xo, 1)
                wait(s_xo, 1)
                act.drain().then_inc(s_endA, 1)

        @block.vector
        def _(dve):
            V = nc.vector
            V.memset(vrow[:, :], 0.0).then_inc(s_zero, 1)
            V.memset(lqT[:, :, :, :], 0.0)
            V.memset(mx[:, :, :], 0.0)
            V.memset(hT[:, :, :], 0.0)
            V.memset(lv[:, :, :, LD:LD + 1], 1.0).then_inc(s_set, 1)
            dve.wait_ge(s_setT, 1)
            V.tensor_copy(flat(w_a), bank[0][:, 0:384])
            V.tensor_copy(vcol[:, :], bank[1][:, 0:V_ALL]).then_inc(s_set, 1)
            dve.wait_ge(s_const, 32)
            dve.wait_ge(s_biasW, 16 * len(bias_loads))
            h2 = LD // 2
            for l in range(LAYERS):
                for t in range(TPB):
                    for k in range(2):
                        V.tensor_tensor(rot[:, l, t, k, 0, :], rot_c[:, t, k, 0, :], qksc[:, l, k, :], ALU.mult)
                        V.tensor_tensor(rot[:, l, t, k, 1, 0:h2], rot_c[:, t, k, 1, 0:h2], qksc[:, l, k, h2:LD], ALU.mult)
                        V.tensor_tensor(rot[:, l, t, k, 1, h2:LD], rot_c[:, t, k, 1, h2:LD], qksc[:, l, k, 0:h2], ALU.mult)
            dve.wait_ge(s_set, 2)
            dve.wait_ge(s_tanh, 1)
            V.tensor_tensor(bog[:, :], vcol[:, V_BO:V_BO + 1], tg[:, 1:2], ALU.mult).then_inc(s_set, 1)
            dve.wait_ge(s_set, SET)
            with dve.Fori(0, TURNS) as it:
                dve.wait_ge(s_go, it + 1)
                dve.sem_inc(s_seenD, 1)

                def wait(s, k):
                    dve.wait_ge(s, k)

                def centred(stage, b, src, frm):
                    wait(s_mu, NB * stage + b + 1)
                    V.tensor_tensor(ln_c[:, cols(b)], src[:, cols(b)], bank[frm][:, cols(b)], ALU.subtract).then_inc(s_cen, 1)
                    wait(s_cen, NB * stage + b + 1)
                    V.tensor_tensor(ln_sq[:, cols(b)], ln_c[:, cols(b)], ln_c[:, cols(b)], ALU.mult).then_inc(s_sq, 1)

                def normal(stage, b, dst):
                    wait(s_rstd, NB * stage + b + 1)
                    V.tensor_tensor(dst[:, cols(b)], ln_c[:, cols(b)], ln_r[:, cols(b)], ALU.mult).then_inc(s_norm, 1)

                def split(n, src, hi, mid, lo, res, s, k0):
                    V.tensor_copy(hi, src).then_inc(s, 1)
                    wait(s, k0 + 1)
                    V.tensor_tensor(res, src, hi, ALU.subtract).then_inc(s, 1)
                    wait(s, k0 + 2)
                    V.tensor_copy(mid, res).then_inc(s, 1)
                    wait(s, k0 + 3)
                    V.tensor_tensor(lo, res, mid, ALU.subtract).then_inc(s, 1)
                    wait(s, k0 + 4)

                def split_stack(n, src):
                    split(n, src, part_h[:, :], part_m[:, :], part_l[:, :], part_f[:, :], s_sp, 4 * n)
                    st = stack[:, :, :, 0:48].rearrange("p t h (s d) -> p (t h) s d", d=DH)
                    parts = [p[:, :].rearrange("p (h d) -> p h d", d=DH) for p in (part_h, part_m, part_l)]
                    if n == 0:
                        order = (0, 1, 2, 0, 1, 0)
                    else:
                        wait(s_stT, T)
                        order = (0, 0, 0, 1, 1, 2)
                    for slot, part in enumerate(order):
                        last = V.tensor_copy(st[:, :, slot, :], parts[part])
                    last.then_inc(s_st, 1)

                def scaled(m, l):
                    wait(s_si, l * T + m // 2 + 1)
                    wait(s_ra, l * 2 * T + m + 1)
                    V.tensor_tensor(qk_c[:, m], qk_c[:, m], qk_in[:, m, :].unsqueeze(2).to_broadcast([128, LH, LD]),
                                    ALU.mult).then_inc(s_rn, 1)

                def max_split(n):
                    split(n, mx[:, :, :], mx_p[:, :, 0, :], mx_p[:, :, 1, :], mx_p[:, :, 2, :], mx_r[:, :, :], s_mp, 4 * n)

                wait(s_inT, 1)
                for b in range(NB):
                    V.tensor_copy(xT[:, cols(b)], bank[0][:, cols(b)]).then_inc(s_src, 1)
                for b in range(NB):
                    centred(0, b, xT, b)
                wait(s_pj, 1)
                split_stack(0, bank[2][:, :])
                for b in range(NB):
                    normal(0, b, nT)
                for t in range(0, T, 2):
                    wait(s_stT, t + 1)
                    V.tensor_copy(kS[:, :, 128 * t:128 * t + 128], bbank(2 + t).rearrange("p (a n) -> p a n", a=H // 2))\
                     .then_inc(s_stD, 1)
                wait(s_pj, 5)
                split_stack(1, bank[6][:, :])
                ring = (0, 1, 6, 7)
                for n in range(T * H // 2):
                    t, p = n // (H // 2), n % (H // 2)
                    wait(s_sA, n + 1)
                    V.tensor_reduce(mx[:, t, 2 * p:2 * p + 2], bank[ring[n % 4]][:, :].rearrange("p (e k) -> p e k", e=2),
                                    AX_X, ALU.max).then_inc(s_mA, 1)
                wait(s_mA, T * H // 2)
                max_split(0)
                wait(s_ke, 1)
                V.scalar_tensor_tensor(out=flat(kf), in0=flat(kf), scalar=0.0, in1=kf_exp[:, :],
                                       op0=ALU.max, op1=ALU.add).then_inc(s_kf, 1)

                def quotient_A(bb):
                    wait(s_tA, bb + 1)
                    src = bank[1 + bb][:, 0:TPB * 144].rearrange("p (a x) -> p a x", x=9)
                    r = rsum[:, TPB * bb:TPB * bb + TPB, :].rearrange("p t h -> p (t h)").unsqueeze(2)
                    V.reciprocal(r, src[:, :, 8:9]).then_inc(s_qA, 1)
                    wait(s_qA, bb + 1)
                    V.tensor_tensor(att[:, TPB * bb:TPB * bb + TPB, :].rearrange("p t (h d) -> p (t h) d", d=DH),
                                    src[:, :, 0:8], r.to_broadcast([128, TPB * H, DH]), ALU.mult).then_inc(s_nA, 1)

                def shifted(b):
                    V.tensor_copy(hT[0:64, b, :], fT[0:64, cols(b)])
                    V.tensor_copy(hT[64:128, b, 1:N], fT[64:128, N * b:N * b + N - 1]).then_inc(s_hh, 1)

                def stream_A(bb):
                    wait(s_yA, bb + 1)
                    V.scalar_tensor_tensor(out=xT[:, cols(bb)], in0=bank[bb][:, cols(bb)], scalar=tg[:, 0:1],
                                           in1=xT[:, cols(bb)], op0=ALU.mult, op1=ALU.add).then_inc(s_src, 1)
                    centred(1, bb, xT, bb)
                    normal(1, bb, fT)
                    wait(s_norm, NB + bb + 1)
                    shifted(bb)

                quotient_A(0)
                stream_A(0)
                quotient_A(1)

                for l in range(LAYERS):
                    b2 = l * 2 * T
                    for m in range(2 * T):
                        if l == 0 and m == 2 * TPB:
                            stream_A(1)
                        t = m // 2
                        wait(s_s2, b2 + m + 1)
                        V.tensor_reduce(qk_ss[:, m, :], qk_sq[:, m % 2, :].rearrange("p (h d) -> p h d", h=LH),
                                        AX_X, ALU.add).then_inc(s_ss, 1)
                        if m % 2:
                            wait(s_ss, b2 + m + 1)
                            V.tensor_scalar(qk_ss[:, m - 1:m + 1, :], qk_ss[:, m - 1:m + 1, :], 1e-24, None, ALU.max)\
                             .then_inc(s_sm, 1)
                        tab = rot[:, l, t % TPB, m % 2, 0, :].unsqueeze(1).to_broadcast([128, LH, LD])
                        V.tensor_tensor(qk_c[:, m], qk[:, m], tab, ALU.mult).then_inc(s_rc, 1)
                        wait(s_rc, b2 + m + 1)
                        wait(s_rs, b2 + m + 1)
                        V.tensor_tensor(qk_c[:, m], qk_c[:, m], qk_s[:, m], ALU.add).then_inc(s_ra, 1)
                        if m >= 2:
                            scaled(m - 2, l)
                    for m in (2 * T - 2, 2 * T - 1):
                        scaled(m, l)
                    n = 0
                    for bb in range(NB):
                        for t, per in ((0, 4), (1, 2)):
                            w = 128 + WIN * t
                            for h0 in range(0, LH, per):
                                wait(s_sB, l * NSB + n + 1)
                                V.tensor_reduce(mx[:, TPB * bb + t, h0:h0 + per],
                                                bank[n % 4][:, 0:w * per].rearrange("p (h k) -> p h k", h=per),
                                                AX_X, ALU.max).then_inc(s_mB, 1)
                                n += 1
                    wait(s_mB, l * NSB + NSB)
                    max_split(1 + l)
                    for g in range(NB * LH // 2):
                        k = l * NB * LH // 2 + g
                        bb, p = g // (LH // 2), g % (LH // 2)
                        wait(s_vB, k + 1)
                        src = bank[2 + g % 2][:, 0:4 * (LD + 1)].rearrange("p (t e x) -> p t e x", t=TPB, e=2)
                        r = rsum[:, TPB * bb:TPB * bb + TPB, 2 * p:2 * p + 2]
                        V.reciprocal(r.unsqueeze(3), src[:, :, :, LD:LD + 1]).then_inc(s_qB, 1)
                        wait(s_qB, k + 1)
                        V.tensor_tensor(o_tok[:, TPB * bb:TPB * bb + TPB, 2 * p:2 * p + 2, :], src[:, :, :, 0:LD],
                                        r.unsqueeze(3).to_broadcast([128, TPB, 2, LD]), ALU.mult).then_inc(s_nB, 1)
                    hflat = hT[:, :, :].rearrange("p b n -> p (b n)")
                    for b in range(NB):
                        wait(s_yB, NB * l + b + 1)
                        V.tensor_tensor(fT[:, cols(b)], fT[:, cols(b)], bank[2 + b][:, cols(b)], ALU.add).then_inc(s_zz, 1)
                        wait(s_zz, NB * l + b + 1)
                        shifted(b)
                    for b in range(NB):
                        centred(2 + l, b, hflat, b)
                    for b in range(NB):
                        normal(2 + l, b, nT)
                        wait(s_norm, NB * (2 + l) + b + 1)
                        V.tensor_scalar(nT[:, cols(b)], nT[:, cols(b)], vcol[:, V_LG + l:V_LG + l + 1],
                                        vcol[:, V_LB + l:V_LB + l + 1], ALU.mult, ALU.add).then_inc(s_af, 1)
                    for b in range(NB):
                        for c, (c0, w) in enumerate(HCH):
                            wait(s_f2, (NB * l + b) * len(HCH) + c + 1)
                            v = b1_column(l, 0, c)
                            V.scalar_tensor_tensor(out=hid[0:w, c, cols(b)], in0=bank[ffb[b][c]][0:w, 0:N],
                                                   scalar=vcol[0:w, v:v + 1], in1=gel[0:w, c, cols(b)],
                                                   op0=ALU.add, op1=ALU.mult).then_inc(s_f3, 1)
                    for b in range(NB):
                        wait(s_f4, NB * l + b + 1)
                        V.scalar_tensor_tensor(out=fT[:, cols(b)], in0=bank[b][:, cols(b)],
                                               scalar=vcol[:, V_B2 + l:V_B2 + l + 1], in1=fT[:, cols(b)],
                                               op0=ALU.add, op1=ALU.add).then_inc(s_f5, 1)
                        wait(s_f5, NB * l + b + 1)
                        if l + 1 < LAYERS:
                            shifted(b)
                        else:
                            V.scalar_tensor_tensor(out=xT[:, cols(b)], in0=fT[:, cols(b)], scalar=tg[:, 2:3],
                                                   in1=xT[:, cols(b)], op0=ALU.mult, op1=ALU.add).then_inc(s_src, 1)
                for b in range(NB):
                    centred(4, b, xT, b)
                for b in range(NB):
                    normal(4, b, nT)
                wait(s_cq, 1)
                V.tensor_scalar(qf_min[:, :], bank[0][:, :], 0.0, None, ALU.min).then_inc(s_fm, 1)
                wait(s_fe, 1)
                V.scalar_tensor_tensor(out=qf[:, :], in0=bank[0][:, :], scalar=0.0, in1=qf_exp[:, :],
                                       op0=ALU.max, op1=ALU.add).then_inc(s_ff, 1)
                wait(s_ff, 1)

                def times_q(t):
                    for half in range(2):
                        wait(s_cs, 2 * t + half + 1)
                        q = qf[:, 128 * t + 64 * half:128 * t + 64 * half + 64].rearrange("p (h d) -> p h d", d=DH)
                        V.tensor_tensor(prod[:, t % 2, 512 * half:512 * half + 512].rearrange("p (h a d) -> p h a d", a=DH, d=DH),
                                        bank[2 + 2 * (t % 3) + half][:, :].rearrange("p (h a d) -> p h a d", a=DH, d=DH),
                                        q.unsqueeze(2).to_broadcast([128, H // 2, DH, DH]), ALU.mult).then_inc(s_pr, 1)

                def quotient(t):
                    wait(s_pr, 2 * t + 2)
                    V.tensor_reduce(nv[:, t, :], prod[:, t % 2, :].rearrange("p (a d) -> p a d", d=DH), AX_X, ALU.add)\
                     .then_inc(s_rd, 1)
                    wait(s_rd, t + 1)
                    V.tensor_tensor(nv[:, t, :], nv[:, t, :], rden[:, 128 * t:128 * t + 128], ALU.mult).then_inc(s_nn, 1)

                times_q(0)
                wait(s_zs, 1)
                V.tensor_tensor(den[:, :], qf[:, :], bank[1][:, :], ALU.mult).then_inc(s_de, 1)
                wait(s_de, 1)
                V.tensor_scalar(den[:, :], den[:, :], 1e-6, None, ALU.add).then_inc(s_de, 1)
                wait(s_de, 2)
                V.reciprocal(rden[:, :], den[:, :]).then_inc(s_de, 1)
                wait(s_de, 3)
                def stream_C(b):
                    wait(s_yc, b + 1)
                    V.tensor_scalar(yC[:, cols(b)], bank[1 + 6 * b][:, cols(b)], tg[:, 1:2], bog[:, :], ALU.mult, ALU.add)\
                     .then_inc(s_yd, 1)
                    wait(s_yd, b + 1)
                    V.tensor_tensor(xT[:, cols(b)], yC[:, cols(b)], xT[:, cols(b)], ALU.add).then_inc(s_src, 1)

                times_q(1)
                quotient(0)
                times_q(2)
                quotient(1)
                times_q(3)
                quotient(2)
                stream_C(0)
                quotient(3)
                stream_C(1)
                for b in range(NB):
                    centred(5, b, xT, 4 + b)
                for b in range(NB):
                    normal(5, b, nT)
                wait(s_le, 1)
                V.tensor_scalar(flat(r_1), flat(r_e), 1.0, None, ALU.add).then_inc(s_la, 1)
                wait(s_la, 1)
                V.reciprocal(flat(aff), flat(r_1)).then_inc(s_la, 1)
                wait(s_la, 2)
                for t in range(T):
                    V.max(top[:, t, :], aff[:, t, :]).then_inc(s_tk, 1)
                for t in range(T):
                    wait(s_tk, t + 1)
                    V.match_replace(rep[:, t, :], top[:, t, :], aff[:, t, :], -1.0).then_inc(s_tk, 1)
                V.tensor_reduce(tsum[:, :], top[:, :, :], AX_X, ALU.add).then_inc(s_tw, 1)
                wait(s_tw, 1)
                V.tensor_scalar(tsum[:, :], tsum[:, :], 1e-9, None, ALU.add).then_inc(s_tw, 1)
                wait(s_tw, 2)
                V.reciprocal(tinv[:, :], tsum[:, :]).then_inc(s_tw, 1)
                wait(s_tk, 2 * T)
                V.scalar_tensor_tensor(out=flat(w_m), in0=flat(rep), scalar=-1.0, in1=flat(aff),
                                       op0=ALU.is_equal, op1=ALU.mult).then_inc(s_tw, 1)
                wait(s_tw, 4)
                V.tensor_tensor(w_t[:, :, :], w_m[:, :, :], tinv[:, :].unsqueeze(2).to_broadcast([128, T, E]), ALU.mult)\
                 .then_inc(s_tw, 1)
                wait(s_tw, 5)
                split(0, w_t[:, :, :], w_p[:, :, 0, :], w_p[:, :, 1, :], w_p[:, :, 2, :], w_res[:, :, :], s_wp, 0)
                for n in range(PAIRS + 1):
                    m = 128 if n < PAIRS else I
                    v = V_BU + n if n < PAIRS else V_BUS
                    wait(s_sg, n + 1)
                    wait(s_u, n + 1)
                    if n >= 2:
                        wait(s_dn, n - 1)
                    dst = up if n < PAIRS else hm
                    last = V.scalar_tensor_tensor(out=dst[0:m, n % 2, :], in0=bank[3 + 3 * (n % 2)][0:m, :],
                                                  scalar=vcol[0:m, v:v + 1], in1=sg[0:m, n % 2, :],
                                                  op0=ALU.add, op1=ALU.mult)
                    last.then_inc(s_up, 1)
                    wait(s_up, n + 1)
                    if n < PAIRS:
                        wait(s_rp, n + 1)
                        V.tensor_tensor(hm[:, n % 2, :], up[:, n % 2, :], bank[4 + 3 * (n % 2)][:, :], ALU.mult)\
                         .then_inc(s_hm, 1)
                    else:
                        V.sem_inc(s_hm, 1)
                wait(s_dn, PAIRS + 1)
                V.tensor_scalar(yD[:, :], bank[0][:, :], vcol[:, V_BDS:V_BDS + 1], tg[:, 3:4], ALU.add, ALU.mult)\
                 .then_inc(s_y1, 1)
                wait(s_y1, 1)
                V.tensor_tensor(xT[:, :], yD[:, :], xT[:, :], ALU.add).then_inc(s_x4, 1)
                wait(s_xo, 1)
                dve.drain().then_inc(s_endD, 1)


_OUT = ((B, N, D), "float32")


def kernel(**inputs):
    import numpy as _np
    import ml_dtypes as _ml
    import concourse.bacc as _bacc
    from concourse import mybir as _mybir
    from concourse.bass_utils import run_bass_kernel_spmd as _run

    nc = _bacc.Bacc("TRN2", target_bir_lowering=False, num_devices=1)
    c_f32, c_bf16 = shape_constants()
    arrays, args = {}, {}
    for name, v in list(inputs.items()) + [("c_f32", c_f32), ("c_bf16", c_bf16.astype(_ml.bfloat16))]:
        v = _np.ascontiguousarray(v)
        arrays[f"in_{name}"] = v
        args[name] = nc.dram_tensor(f"in_{name}", v.shape, _mybir.dt.from_np(v.dtype), kind="ExternalInput").ap()
    shape, dtype = _OUT
    out = nc.dram_tensor("out_0", shape, _mybir.dt.from_np(_np.dtype(dtype)), kind="ExternalOutput").ap()
    flamingo(nc, args, out)
    r = _run(nc, [arrays], core_ids=[0])
    return r.results[0]["out_0"]
```

```python
from contextlib import ExitStack

import numpy as np
import concourse.bass as bass
from concourse import mybir

F32 = mybir.dt.float32
BF16 = mybir.dt.bfloat16
ALU = mybir.AluOpType
ACT = mybir.ActivationFunctionType
AX_X = mybir.AxisListType.X

B, N, D = 8, 256, 128
NB = 2
TURNS = B // NB
TPB = N // 128
T = NB * TPB
TOK = T * 128
H, DH = 16, 8
SLOT = 64
LH, LD, WIN = 8, 64, 64
LAYERS = 2
INNER = LH * LD
HID = int(D * 4 * 2 / 3)
HCH = [(c, min(128, HID - c)) for c in range(0, HID, 128)]
E, I, TOPK = 32, 64, 8
PAIRS = E // 2
VS = 9 * 9
EPS = 1e-5
NEG = -1.0e30

C_ID, C_CAUSAL, C_ONES, C_MEAN, C_ROT = 0, 128, 256, 384, 512
ROTW = TPB * 2 * 2 * LD
C_ALL = C_ROT + ROTW
K_ID, K_MQ, K_MK, K_ONES, K_MAX = 0, 128, 320, 512, 640
K_SEL = K_MAX + H * 128
K_ALL = K_SEL + PAIRS * 128
V_BG, V_BU = 0, PAIRS
V_LG, V_LB, V_B2 = 2 * PAIRS, 2 * PAIRS + LAYERS, 2 * PAIRS + 2 * LAYERS
V_B1 = V_B2 + LAYERS
V_BO = V_B1 + LAYERS * 2 * len(HCH)
V_BDS, V_BGS, V_BUS, V_ALL = V_BO + 1, V_BO + 2, V_BO + 3, V_BO + 4


def b1_column(layer, half, chunk):
    return V_B1 + chunk * 2 * LAYERS + 2 * layer + half


def shape_constants():
    p = np.arange(128)[:, None]
    f = np.arange(128)[None, :]
    c = np.zeros((128, C_ALL), np.float32)
    c[:, C_ID:C_ID + 128] = p == f
    c[:, C_CAUSAL:C_CAUSAL + 128] = p <= f
    c[:, C_ONES:C_ONES + 128] = 1
    c[:, C_MEAN:C_MEAN + 128] = 1.0 / D
    half = np.arange(0, LD, 2, dtype=np.float32)
    inv = np.float32(1.0) / np.float32(10000.0) ** (half / np.float32(LD))
    t = np.arange(N, dtype=np.float32)
    ang = np.concatenate([t[:, None] * inv[None, :]] * 2, 1).astype(np.float32)
    base = ((half + np.float32(0.4 * LD)) / np.float32(1.4 * LD)).astype(np.float32)
    power = (t - N // 2) / np.float32(WIN // 2)
    sc = np.concatenate([base[None, :] ** power[:, None]] * 2, 1).astype(np.float32)
    sign = np.where(np.arange(LD) < LD // 2, -1.0, 1.0).astype(np.float32)[None, :]
    rot = np.zeros((128, TPB, 2, 2, LD), np.float32)
    for tile in range(TPB):
        r = slice(128 * tile, 128 * tile + 128)
        for qk, s in ((0, sc[r]), (1, 1 / sc[r])):
            rot[:, tile, qk, 0] = np.cos(ang[r]) * s
            rot[:, tile, qk, 1] = np.sin(ang[r]) * s * sign
    c[:, C_ROT:] = rot.reshape(128, -1)

    k = np.zeros((128, K_ALL), np.float32)
    k[:, K_ID:K_ID + 128] = p == f
    k[:, K_ONES:K_ONES + 128] = 1
    key = np.arange(WIN + 128)[None, :] - WIN
    k[:, K_MQ:K_MQ + 192] = np.where((key <= p) & (key >= p - WIN), 0, NEG)
    q = np.arange(128 + WIN)[None, :]
    k[:, K_MK:K_MK + 192] = np.where((p <= q) & (q <= p + WIN), 0, NEG)
    for h in range(H):
        for part in range(3):
            k[part * H + h, K_MAX + h * 128:K_MAX + h * 128 + 128] = -1
    for pr in range(PAIRS):
        for part in range(3):
            for e in range(2):
                at = K_SEL + pr * 128 + e * 64
                k[part * E + 2 * pr + e, at:at + 64] = 1
    return c, k


def flamingo(nc, a, out):
    with ExitStack() as ctx:
        def sb(name, shape, dt=F32):
            return ctx.enter_context(nc.sbuf_tensor(name, shape, dt))

        SET = 3
        turn_sems = []

        def sem(name):
            s = ctx.enter_context(nc.semaphore(name))
            turn_sems.append(s)
            return s

        bank = [ctx.enter_context(nc.psum_tensor(f"bank{i}", [128, 512], F32)) for i in range(8)]

        proj = (3, 4, 5, 6, 7, 2)
        ffb = ((5, 4, 3), (6, 7, 2))

        turn = (3, 4, 5, 6, 7, 5, 6, 4)
        ring, UNITS = ((0, 1, 6, 7), (0, 1, 7)), TPB * H // 2
        run = (4, 6, 2)
        mring = (0, 1, 4, 5)

        def cols(b):
            return slice(N * b, N * b + N)

        def bbank(i):
            return bank[i][:, :].bitcast(BF16)

        cf = sb("cf", [128, C_ALL])
        cb = sb("cb", [128, K_ALL], BF16)
        ident, causal = cf[:, C_ID:C_ID + 128], cf[:, C_CAUSAL:C_CAUSAL + 128]
        ones, mean = cf[:, C_ONES:C_ONES + 128], cf[:, C_MEAN:C_MEAN + 128]
        identb = cb[:, K_ID:K_ID + 128]
        rot_c = cf[:, C_ROT:].rearrange("p (t k w d) -> p t k w d", t=TPB, k=2, w=2)
        w_a = sb("w_a", [128, 3, 128])
        w_c = sb("w_c", [128, 4, 128])
        ROW = 3 * 128 + E
        row = sb("row", [3, ROW])
        row_p = sb("row_p", [3, ROW], BF16)
        w_qkv = sb("w_qkv", [128, LAYERS, 3 * INNER])
        w_o = sb("w_o", [128, LAYERS, INNER // 128, D])
        w_1 = sb("w_1", [128, LAYERS, 2 * HID])
        w_2 = sb("w_2", [128, LAYERS, len(HCH), D])
        w_r = sb("w_r", [128, E])
        w_gs = sb("w_gs", [128, 2, I])
        w_ds = sb("w_ds", [I, D])
        w_g = sb("w_g", [128, E, I])
        w_u = sb("w_u", [128, E, I])
        w_d = sb("w_d", [128, PAIRS, D])
        b_d = sb("b_d", [E, D])
        vcol = sb("vcol", [128, V_ALL])
        gate = sb("gate", [128, 4])
        tg = sb("tg", [128, 4])
        qksc = sb("qksc", [128, LAYERS, 2, LD])
        rot = sb("rot", [128, LAYERS, TPB, 2, 2, LD])
        bog, bdg = sb("bog", [128, 1]), sb("bdg", [128, 1])

        x_tok = sb("x_tok", [128, T, D])
        c_tok = sb("c_tok", [128, T, D])
        cT = sb("cT", [128, TOK])
        xT = sb("xT", [128, TOK])
        ln_c, ln_sq, ln_r = (sb(n, [128, TOK]) for n in ("ln_c", "ln_sq", "ln_r"))
        nT = sb("nT", [128, TOK])
        kv_c = sb("kv_c", [128, 2, T, D])
        mx = sb("mx", [128, T, H])
        mx_r = sb("mx_r", [128, T, H])
        mx_p = sb("mx_p", [128, T, 3, H], BF16)
        mxT = sb("mxT", [3 * H, TOK], BF16)
        PT = sb("PT", [128, 4, 2, N])
        oraw = sb("oraw", [128, 2, 512])
        rsum = sb("rsum", [128, T, H])
        att = sb("att", [128, T, D])
        order = nc.dram_tensor("order_dram", (NB, H, N, DH), F32, kind="Internal").ap()
        fT = sb("fT", [128, TOK])
        hT = sb("hT", [128, NB, N])
        lqT = sb("lqT", [128, 2, 4, TOK])
        qS = lqT[:, :, :, :].rearrange("p e a n -> p (e a n)").bitcast(BF16)\
            .rearrange("p (e a n) -> p e a n", e=2, a=H // 2)
        qk_sq = sb("qk_sq", [128, 2, INNER])
        qk_ss = sb("qk_ss", [128, 2 * T, LH])
        qk_lg = sb("qk_lg", [128, 2 * T, LH])
        qk_in = sb("qk_in", [128, 2 * T, LH])
        lv = sb("lv", [128, T, LH, LD + 1])
        top = sb("top", [128, T, TOPK])
        tsum, tinv = sb("tsum", [128, T]), sb("tinv", [128, T])
        w_p = sb("w_p", [128, T, 3, E], BF16)
        wS = sb("wS", [3 * E, TOK], BF16)
        wT = sb("wT", [E, TOK])
        o_out = sb("o_out", [128, T, D])

        arena = sb("arena", [128, 3 * 8 * INNER])
        arena2 = sb("arena2", [128, 4 * TOK])

        def part(at, cols, tile=arena):
            return tile[:, at:at + cols]

        def square(m):
            return qk_sq[:, m % 2, :] if m < 2 * T - 2 else (ln_c, ln_sq)[m % 2][:, :]

        w_raw = part(0, 384).rearrange("p (k n) -> p k n", k=3)
        vrow = arena[0:V_ALL, 512:640]
        stack = part(0, 2048).bitcast(BF16).rearrange("p (t h s) -> p t h s", t=T, h=H)
        kS = part(2048, 2048).bitcast(BF16).rearrange("p (a n) -> p a n", a=H // 2)
        part_f = part(4096, TOK)
        part_h, part_m, part_l = (part(4608 + 256 * n, 256).bitcast(BF16) for n in range(3))
        va = part(5376, 2 * T * 8 * VS).rearrange("p (t g x) -> p t g x", t=T, g=2)
        va_one = part(5376, 2 * T * 8 * VS).rearrange("p (t x) -> p t x", x=VS)[:, :, DH:DH + 1]
        qk, qk_c, qk_s = (part(4096 * n, 4096).rearrange("p (m h d) -> p m h d", m=2 * T, h=LH) for n in range(3))
        o_tok = part(8192, 2048).rearrange("p (t h d) -> p t h d", t=T, h=LH)
        oT = part(10240, 2048).rearrange("p (c n) -> p c n", c=4)
        gel, hid = (part(4608 + 1536 * n, 1536).rearrange("p (c n) -> p c n", c=len(HCH)) for n in range(2))
        lkT = part(0, 2048, arena2).rearrange("p (c n) -> p c n", c=4)
        OUTER = H * DH * DH
        kf_min, kf_exp = part(10560, TOK), part(11072, TOK)
        kf, vc = kv_c[:, 0], kv_c[:, 1]
        outer = part(8192, T * OUTER).rearrange("p (t n) -> p t n", t=T)
        prod = part(4096, 2 * OUTER).rearrange("p (r n) -> p r n", r=2)
        qf, qf_min, qf_exp = (part(512 * n, TOK, arena2) for n in range(3))
        den, rden, nv, nvT = ln_sq, ln_r, att, ln_c
        r_e, r_1, aff, rep, w_m, w_t, w_res = (part(3072 + T * E * n, T * E).rearrange("p (t e) -> p t e", t=T)
                                               for n in range(7))
        sg, up, hm = (part(1024 * n, 1024).rearrange("p (r n) -> p r n", r=2) for n in range(3))

        bias_loads = [(vrow[V_BG:V_BG + PAIRS, :], a["L1_ffn_bg"].rearrange("(p e) i -> p (e i)", e=2)),
                 (vrow[V_BU:V_BU + PAIRS, :], a["L1_ffn_bu"].rearrange("(p e) i -> p (e i)", e=2)),
                 (vrow[V_LG:V_LG + LAYERS, :], a["L0_ffn_ln_g"]),
                 (vrow[V_LB:V_LB + LAYERS, :], a["L0_ffn_ln_b"]),
                 (vrow[V_B2:V_B2 + LAYERS, :], a["L0_ffn_b2"]),
                 (vrow[V_BO:V_BO + 1, :], a["L1_xattn_bo"].rearrange("(a n) -> a n", a=1)),
                 (vrow[V_BDS:V_BDS + 1, :], a["L1_ffn_bd_s"].rearrange("(a n) -> a n", a=1)),
                 (vrow[V_BGS:V_BGS + 1, 0:I], a["L1_ffn_bg_s"].rearrange("(a n) -> a n", a=1)),
                 (vrow[V_BUS:V_BUS + 1, 0:I], a["L1_ffn_bu_s"].rearrange("(a n) -> a n", a=1))]
        halves = a["L0_ffn_b1"].rearrange("l (h n) -> (l h) n", h=2)
        for c, (c0, w) in enumerate(HCH):
            r = b1_column(0, 0, c)
            bias_loads += [(vrow[r:r + 2 * LAYERS, 0:w], halves[:, c0:c0 + w])]
        bias_loads += [(gate[:, 0:2], a["g_xattn"].rearrange("(a n) -> a n", a=1).to_broadcast([128, 2])),
                  (gate[:, 2:4], a["g_ffn"].rearrange("(a n) -> a n", a=1).to_broadcast([128, 2]))]
        for l in range(LAYERS):
            bias_loads += [(qksc[:, l, 0, :], a["L0_ffn_q_scale"][l:l + 1, :].to_broadcast([128, LD])),
                      (qksc[:, l, 1, :], a["L0_ffn_k_scale"][l:l + 1, :].to_broadcast([128, LD]))]
        local_loads = []
        for l in range(LAYERS):
            local_loads += [(w_qkv[:, l, :], a["L0_ffn_wqkv"][l]),
                      (w_o[:, l, :, :], a["L0_ffn_wo"][l].rearrange("(c p) n -> p c n", p=128)),
                      (w_1[:, l, :], a["L0_ffn_w1"][l])]
            local_loads += [(w_2[0:w, l, c, :], a["L0_ffn_w2"][l, c0:c0 + w, :]) for c, (c0, w) in enumerate(HCH)]
        expert_loads = [(w_r[:, :], a["L1_ffn_Wr"]), (w_gs[:, 0, :], a["L1_ffn_Wg_s"]),
                 (w_gs[:, 1, :], a["L1_ffn_Wu_s"]), (w_ds[:, :], a["L1_ffn_Wd_s"]),
                 (w_g[:, :, :], a["L1_ffn_Wg"].rearrange("e h i -> h e i")),
                 (w_u[:, :, :], a["L1_ffn_Wu"].rearrange("e h i -> h e i")),
                 (w_d[:, :, :], a["L1_ffn_Wd"].rearrange("(p e) i h -> (e i) p h", e=2)),
                 (b_d[:, :], a["L1_ffn_bd"])]

        s_constants = sem("s_constants")
        s_constants_bf16 = sem("s_constants_bf16")
        s_first_weights = sem("s_first_weights")
        s_bias_vectors = sem("s_bias_vectors")
        s_second_weights = sem("s_second_weights")
        s_bias_rows = sem("s_bias_rows")
        s_row_parts = sem("s_row_parts")
        s_local_weights = sem("s_local_weights")
        s_expert_weights = sem("s_expert_weights")
        s_vectors_cleared = sem("s_vectors_cleared")
        s_setup_turned = sem("s_setup_turned")
        s_setup = sem("s_setup")
        s_gates = sem("s_gates")
        s_tables = sem("s_tables")
        s_stored = sem("s_stored")
        s_turn_open = sem("s_turn_open")
        turn_sems.clear()
        s_end_pe, s_end_act, s_end_dve, s_end_pool = (sem(n) for n in ("s_end_pe", "s_end_act", "s_end_dve", "s_end_pool"))
        s_loaded = sem("s_loaded")
        s_inputs_turned = sem("s_inputs_turned")
        s_context_out = sem("s_context_out")
        s_stream = sem("s_stream")
        s_mean, s_centred, s_squared, s_variance = (sem(n) for n in ("s_mean", "s_centred", "s_squared", "s_variance"))
        s_variance_log, s_rstd, s_normal = (sem(n) for n in ("s_variance_log", "s_rstd", "s_normal"))
        s_projected = sem("s_projected")
        s_projection_out = sem("s_projection_out")
        s_split = sem("s_split")
        s_seen_pe, s_seen_act, s_seen_dve, s_seen_pool = (sem(n) for n in ("s_seen_pe", "s_seen_act", "s_seen_dve", "s_seen_pool"))
        s_padded = sem("s_padded")
        s_stacked = sem("s_stacked")
        s_stack_turned = sem("s_stack_turned")
        s_k_stack_out = sem("s_k_stack_out")
        s_q_stack_out = sem("s_q_stack_out")
        s_a_scores = sem("s_a_scores")
        s_a_max = sem("s_a_max")
        s_max_parts = sem("s_max_parts")
        s_max_turned = sem("s_max_turned")
        s_max_out = sem("s_max_out")
        s_a_scores_less_max = sem("s_a_scores_less_max")
        s_a_exp = sem("s_a_exp")
        s_a_values = sem("s_a_values")
        s_a_sums_out = sem("s_a_sums_out")
        s_a_sums_turned = sem("s_a_sums_turned")
        s_a_reciprocal = sem("s_a_reciprocal")
        s_a_normalised = sem("s_a_normalised")
        s_order_written = sem("s_order_written")
        s_order_read0, s_order_read1 = sem("s_order_read0"), sem("s_order_read1")
        s_a_result_turned = sem("s_a_result_turned")
        s_shifted = sem("s_shifted")
        s_l_projected = sem("s_l_projected")
        s_l_projection_out = sem("s_l_projection_out")
        s_l_squared = sem("s_l_squared")
        s_l_squared_pool = sem("s_l_squared_pool")
        s_l_sums = sem("s_l_sums")
        s_l_bounded = sem("s_l_bounded")
        s_l_log = sem("s_l_log")
        s_l_inverse_norm = sem("s_l_inverse_norm")
        s_l_sine = sem("s_l_sine")
        s_l_cosine = sem("s_l_cosine")
        s_l_rotated = sem("s_l_rotated")
        s_l_scaled = sem("s_l_scaled")
        s_l_turned = sem("s_l_turned")
        s_l_turned_out = sem("s_l_turned_out")
        NSB = NB * (LH // 4 + LH // 2)
        s_l_scores = sem("s_l_scores")
        s_l_max = sem("s_l_max")
        s_l_scores_less_max = sem("s_l_scores_less_max")
        s_l_exp = sem("s_l_exp")
        s_l_values = sem("s_l_values")
        s_l_values_out = sem("s_l_values_out")
        s_l_values_turned = sem("s_l_values_turned")
        s_l_reciprocal = sem("s_l_reciprocal")
        s_l_normalised = sem("s_l_normalised")
        s_l_heads_turned = sem("s_l_heads_turned")
        s_l_heads_out = sem("s_l_heads_out")
        s_l_output = sem("s_l_output")
        s_l_output_added = sem("s_l_output_added")
        s_l_affine = sem("s_l_affine")
        s_hidden = sem("s_hidden")
        s_gelu = sem("s_gelu")
        s_gated = sem("s_gated")
        s_contracted = sem("s_contracted")
        s_layer_added = sem("s_layer_added")
        s_c_query = sem("s_c_query")
        s_c_k_min = sem("s_c_k_min")
        s_c_k_exp = sem("s_c_k_exp")
        s_c_k_feature = sem("s_c_k_feature")
        s_c_outer = sem("s_c_outer")
        s_c_running = sem("s_c_running")
        s_c_k_running = sem("s_c_k_running")
        s_c_q_min = sem("s_c_q_min")
        s_c_q_exp = sem("s_c_q_exp")
        s_c_q_feature = sem("s_c_q_feature")
        s_c_times_q = sem("s_c_times_q")
        s_c_pool_sum = sem("s_c_pool_sum")
        s_c_summed = sem("s_c_summed")
        s_c_denominator = sem("s_c_denominator")
        s_c_denominator_log = sem("s_c_denominator_log")
        s_c_denominator_inverse = sem("s_c_denominator_inverse")
        s_c_newton = sem("s_c_newton")
        s_c_quotient = sem("s_c_quotient")
        s_c_quotient_turned = sem("s_c_quotient_turned")
        s_c_quotient_out = sem("s_c_quotient_out")
        s_bias_added = sem("s_bias_added")
        s_c_output = sem("s_c_output")
        s_logits = sem("s_logits")
        s_logits_exp = sem("s_logits_exp")
        s_affinity = sem("s_affinity")
        s_top = sem("s_top")
        s_weight = sem("s_weight")
        s_weight_parts = sem("s_weight_parts")
        s_weights_turned = sem("s_weights_turned")
        s_weights_out = sem("s_weights_out")
        s_e_gate = sem("s_e_gate")
        s_e_up = sem("s_e_up")
        s_e_weights = sem("s_e_weights")
        s_e_silu = sem("s_e_silu")
        s_e_gated = sem("s_e_gated")
        s_e_weighted = sem("s_e_weighted")
        s_e_down = sem("s_e_down")
        s_final = sem("s_final")
        s_final_turned = sem("s_final_turned")
        s_final_out = sem("s_final_out")

        turn_range = range(turn_sems[0].num, turn_sems[-1].num + 1)
        assert len(turn_range) == len(turn_sems)
        block = ctx.enter_context(nc.Block())

        def flat(t):
            return t.rearrange("p t d -> p (t d)")

        @block.sync
        def _(sp):
            sp.dma_start(cf[:, :], a["c_f32"]).then_inc(s_constants, 16)
            for n, c in enumerate("qkv"):
                sp.dma_start(w_raw[:, n, :], a[f"L0_xattn_W{c}"]).then_inc(s_first_weights, 16)
            def load(turn):
                for src, dst in ((a["x"], x_tok), (a["ctx_1024"], c_tok)):
                    sp.dma_start(dst[:, :, :], src.rearrange("(i b) (t p) d -> i p (b t) d", b=NB, p=128)[turn])\
                      .then_inc(s_loaded, 16)

            load(0)
            sp.dma_start(cb[:, :], a["c_bf16"]).then_inc(s_constants_bf16, 16)
            for n, c in enumerate("kvqo"):
                sp.dma_start(w_c[:, "qkvo".index(c), :], a[f"L1_xattn_W{c}"]).then_inc(s_second_weights, 16)
            sp.wait_ge(s_loaded, 32)
            sp.sem_clear(s_loaded)
            sp.sem_inc(s_turn_open, 1)
            sp.wait_ge(s_bias_vectors, 16 * len(bias_loads))
            for dst, src in local_loads:
                sp.dma_start(dst, src).then_inc(s_local_weights, 16)
            for dst, src in expert_loads:
                sp.dma_start(dst, src).then_inc(s_expert_weights, 16)
            with sp.Fori(0, TURNS) as it:
                for bb, s_back in ((0, s_order_read0), (1, s_order_read1)):
                    sp.wait_ge(s_a_normalised, bb + 1)
                    for t in range(TPB):
                        sp.dma_start(order[bb, :, 128 * t:128 * t + 128, :].rearrange("h q d -> q h d"),
                                     att[:, TPB * bb + t, :].rearrange("p (h d) -> p h d", d=DH)).then_inc(s_order_written, 16)
                    sp.wait_ge(s_order_written, 32 * (bb + 1))
                    sp.dma_start(x_tok[:, TPB * bb:TPB * bb + TPB, :],
                                 order[bb].rearrange("h (a b) d -> (h a) (b d)", b=16).rearrange("(t p) c -> p t c", p=128))\
                      .then_inc(s_back, 16)
                sp.wait_ge(s_a_result_turned, NB)
                load((it + 1) % TURNS)
                sp.wait_ge(s_final_out, NB)
                sp.dma_start(out.rearrange("(i b) (t p) d -> i p (b t) d", b=NB, p=128)[it], o_out[:, :, :])\
                  .then_inc(s_stored, 16)
                for s in (s_end_pe, s_end_act, s_end_dve, s_end_pool):
                    sp.wait_ge(s, 1)
                sp.wait_ge(s_loaded, 32)
                sp.sem_clear(turn_range)
                sp.sem_inc(s_turn_open, 1)
                sp.wait_ge(s_stored, 16)
                sp.sem_clear(s_stored)

        @block.gpsimd
        def _(pool):
            for n, c in enumerate("qkv"):
                pool.dma_start(row[:, 128 * n:128 * n + 128],
                               a[f"L1_xattn_b{c}"].rearrange("(a n) -> a n", a=1).to_broadcast([3, 128])).then_inc(s_bias_rows, 16)
            pool.dma_start(row[:, 384:384 + E], a["L1_ffn_br"].rearrange("(a n) -> a n", a=1).to_broadcast([3, E]))\
                .then_inc(s_bias_rows, 16)
            pool.wait_ge(s_constants, 16)
            pool.wait_ge(s_bias_vectors, 16 * len(bias_loads))
            h2 = LD // 2
            for l in range(LAYERS):
                for t in range(TPB):
                    for k in range(2):
                        nc.gpsimd.tensor_tensor(rot[:, l, t, k, 0, :], rot_c[:, t, k, 0, :], qksc[:, l, k, :], ALU.mult)
                        nc.gpsimd.tensor_tensor(rot[:, l, t, k, 1, 0:h2], rot_c[:, t, k, 1, 0:h2],
                                                qksc[:, l, k, h2:LD], ALU.mult)
                        last = nc.gpsimd.tensor_tensor(rot[:, l, t, k, 1, h2:LD], rot_c[:, t, k, 1, h2:LD],
                                                       qksc[:, l, k, 0:h2], ALU.mult)
            last.then_inc(s_tables, 1)
            pool.wait_ge(s_tables, 1)
            pool.wait_ge(s_setup, SET)

            with pool.Fori(0, TURNS) as it:
                pool.wait_ge(s_turn_open, it + 1)

                pool.sem_inc(s_seen_pool, 1)
                pool.wait_ge(s_seen_pool, 1)
                nc.gpsimd.memset(stack[:, :, :, 48:SLOT], 0.0)
                nc.gpsimd.memset(va[:, :, :, :], 0.0).then_inc(s_padded, 1)
                pool.wait_ge(s_padded, 1)
                nc.gpsimd.memset(va_one, 1.0).then_inc(s_padded, 1)
                pool.wait_ge(s_projection_out, 2)
                nc.gpsimd.tensor_scalar(kf_min[:, :], flat(kf), 0.0, None, ALU.min).then_inc(s_c_k_min, 1)
                for l in range(LAYERS):
                    for m in range(2 * T):
                        pool.wait_ge(s_l_projection_out, l * 3 * T + 3 * (m // 2) + m % 2 + 1)
                        tab = rot[:, l, (m // 2) % TPB, m % 2, 1, :].unsqueeze(1)
                        h2 = LD // 2
                        nc.gpsimd.tensor_tensor(qk_s[:, m, :, 0:h2], qk[:, m, :, h2:LD],
                                                tab[:, :, 0:h2].to_broadcast([128, LH, h2]), ALU.mult)
                        nc.gpsimd.tensor_tensor(qk_s[:, m, :, h2:LD], qk[:, m, :, 0:h2],
                                                tab[:, :, h2:LD].to_broadcast([128, LH, h2]), ALU.mult)\
                          .then_inc(s_l_sine, 1)
                        if m >= 2 * TPB:
                            if m < 2 * T - 2:
                                pool.wait_ge(s_l_sums, l * 2 * T + m - 1)
                            raw = qk[:, m, :, :].rearrange("p h d -> p (h d)")
                            nc.gpsimd.tensor_tensor(square(m), raw, raw, ALU.mult).then_inc(s_l_squared_pool, 1)
                pool.wait_ge(s_l_output, NB * LAYERS)
                pool.wait_ge(s_c_k_feature, 1)
                for t in range(T):
                    nc.gpsimd.tensor_tensor(
                        outer[:, t, :].rearrange("p (h a d) -> p h a d", h=H, a=DH),
                        kf[:, t, :].rearrange("p (h a) -> p h a", h=H).unsqueeze(3).to_broadcast([128, H, DH, DH]),
                        vc[:, t, :].rearrange("p (h d) -> p h d", h=H).unsqueeze(2).to_broadcast([128, H, DH, DH]),
                        ALU.mult).then_inc(s_c_outer, 1)
                pool.wait_ge(s_c_times_q, 4)
                p4 = prod[:, 1, :].rearrange("p (a d) -> p a d", d=DH)
                nc.gpsimd.tensor_tensor(p4[:, :, 0:4], p4[:, :, 0:4], p4[:, :, 4:8], ALU.add).then_inc(s_c_pool_sum, 1)
                pool.wait_ge(s_c_pool_sum, 1)
                nc.gpsimd.tensor_tensor(p4[:, :, 0:2], p4[:, :, 0:2], p4[:, :, 2:4], ALU.add).then_inc(s_c_pool_sum, 1)
                pool.wait_ge(s_c_pool_sum, 2)
                nc.gpsimd.tensor_tensor(nv[:, 1, :].unsqueeze(2), p4[:, :, 0:1], p4[:, :, 1:2], ALU.add).then_inc(s_c_pool_sum, 1)
                pool.wait_ge(s_normal, 5 * NB)
                nc.gpsimd.tensor_scalar(xT[:, :], xT[:, :], bog[:, :], None, ALU.add).then_inc(s_bias_added, 1)
                pool.wait_ge(s_normal, 6 * NB)
                nc.gpsimd.tensor_scalar(xT[:, :], xT[:, :], bdg[:, :], None, ALU.add).then_inc(s_bias_added, 1)
                pool.wait_ge(s_final_out, NB)
                pool.drain().then_inc(s_end_pool, 1)

        @block.tensor
        def _(pe):
            mm, tr = nc.tensor.matmul, nc.tensor.transpose
            pe.wait_ge(s_constants, 16)
            pe.wait_ge(s_first_weights, 3 * 16)
            for n in range(3):
                last = tr(bank[0][:, 128 * n:128 * n + 128], w_raw[:, n, :], ident)
            last.then_inc(s_setup_turned, 1)
            pe.wait_ge(s_bias_vectors, 16 * len(bias_loads))
            tr(bank[1][:, 0:V_ALL], vrow[:, :], ident[0:V_ALL, 0:V_ALL]).then_inc(s_setup_turned, 1)
            pe.wait_ge(s_setup, SET)
            with pe.Fori(0, TURNS) as it:
                pe.wait_ge(s_turn_open, it + 1)
                pe.sem_inc(s_seen_pe, 1)

                def mean_pe(src, b, to, ready, count):
                    pe.wait_ge(ready, count)
                    mm(bank[to][:, cols(b)], mean, src[:, cols(b)], start=True, stop=True).then_inc(s_mean, 1)

                def var_pe(stage, b, to):
                    pe.wait_ge(s_squared, NB * stage + b + 1)
                    mm(bank[to][:, cols(b)], mean, ln_sq[:, cols(b)], start=True, stop=True).then_inc(s_variance, 1)

                def max_transposed(n, tiles, to):
                    pe.wait_ge(s_max_parts, 4 * n + 4)
                    for t in tiles:
                        last = tr(bbank(to)[0:3 * H, 128 * t:128 * t + 128],
                                  mx_p[:, t, :, :].rearrange("p a h -> p (a h)"), identb)
                    last.then_inc(s_max_turned, 1)
                    pe.wait_ge(s_max_out, n + 1)

                for n, src in enumerate((x_tok, c_tok)):
                    for t in range(T):
                        last = tr(bank[n][:, 128 * t:128 * t + 128], src[:, t, :], ident)
                    last.then_inc(s_inputs_turned, 1)

                mean_pe(xT, 0, 0, s_stream, NB)
                pe.wait_ge(s_context_out, 1)
                mean_pe(xT, 1, 1, s_stream, NB)

                def biased(o, at, w):
                    mm(o, cb[0:3, K_ONES:K_ONES + 128], row_p[:, at:at + w].unsqueeze(1).to_broadcast([3, T, w]),
                       start=True, stop=False, skip_group_check=True)

                def context(n, w):
                    if n >= 2:
                        biased(bank[2 + n][:, :], 128 * (n - 1), 128)
                    for t in range(T):
                        last = mm(bank[2 + n][:, 128 * t:128 * t + 128], cT[:, 128 * t:128 * t + 128], w,
                                  start=n < 2, stop=True, skip_group_check=n >= 2)
                    last.then_inc(s_projected, 1)

                context(0, w_a[:, 1, :])
                for b in range(NB):
                    var_pe(0, b, b)
                context(1, w_a[:, 2, :])
                pe.wait_ge(s_row_parts, 6)
                pe.wait_ge(s_constants_bf16, 16)
                pe.wait_ge(s_second_weights, 4 * 16)
                context(2, w_c[:, 1, :])
                context(3, w_c[:, 2, :])

                def stack_transposed(n):
                    for t in range(T):
                        pe.wait_ge(s_stacked, 1 if n == 0 else 2 + t // TPB)
                        if n == 0 and t == 1:
                            pe.wait_ge(s_projection_out, 3)
                        if n == 1:
                            pe.wait_ge(s_k_stack_out, t + 1)
                        for p in range(H // 2):
                            last = tr(bbank(2 + t)[:, 128 * p:128 * p + 128],
                                      stack[:, t, 2 * p:2 * p + 2, :].rearrange("p h s -> p (h s)"), identb)
                        last.then_inc(s_stack_turned, 1)

                pe.wait_ge(s_constants_bf16, 16)
                pe.wait_ge(s_padded, 2)
                stack_transposed(0)
                pe.wait_ge(s_normal, NB)
                for t in range(T):
                    last = mm(bank[6][:, 128 * t:128 * t + 128], nT[:, 128 * t:128 * t + 128], w_a[:, 0, :],
                              start=True, stop=True)
                last.then_inc(s_projected, 1)
                stack_transposed(1)
                def scores_A(n, to, before):
                    t, p = n // (H // 2), n % (H // 2)
                    pe.wait_ge(s_q_stack_out, t + 1)
                    if before > 0:
                        pe.wait_ge(s_a_max, before)
                    for e in range(2):
                        last = mm(bank[to][:, 256 * e:256 * e + 256],
                                  qS[:, e, p, 128 * t:128 * t + 128],
                                  kS[:, p, N * (t // TPB):N * (t // TPB) + N], start=True, stop=True)
                    last.then_inc(s_a_scores, 1)

                for n in range(UNITS):
                    scores_A(n, ring[0][n % 4], n - 3)
                for n, before in ((UNITS, UNITS - 3), (UNITS + 1, UNITS - 2), (UNITS + 2, UNITS)):
                    scores_A(n, ring[1][n - UNITS], before)
                max_transposed(0, range(0, TPB), 2)

                def score_A(n):
                    bb, p, kt = n // H, n % H // 2, n % 2
                    if n >= 3:
                        pe.wait_ge(s_a_exp, n - 2)
                    o = bank[3 + n % 3]
                    k0 = N * bb + 128 * kt
                    for e in range(2):
                        h = 2 * p + e
                        mm(o[:, N * e:N * e + N], cb[0:3 * H, K_MAX + 128 * h:K_MAX + 128 * h + 128],
                           mxT[:, N * bb:N * bb + N], start=(e == 0), stop=False, skip_group_check=True)
                    mm(o[:, :], kS[:, p, k0:k0 + 128], qS[:, :, p, N * bb:N * bb + N], start=False, stop=True,
                       skip_group_check=True).then_inc(s_a_scores_less_max, 1)

                def value_A(n):
                    bb, p, kt = n // H, n % H // 2, n % 2
                    pe.wait_ge(s_a_exp, n + 1)
                    g = p // 4
                    for e in range(2):
                        h8 = (2 * p + e) % 8
                        last = mm(bank[6 + bb][0:72, N * g:N * g + N],
                                  va[:, TPB * bb + kt, g, 72 * h8:72 * h8 + 72],
                                  PT[:, n % 4, e, 0:N], start=(p % 4 == 0 and kt == 0 and e == 0),
                                  stop=(p % 4 == 3 and kt == 1 and e == 1))
                    last.then_inc(s_a_values, 1)

                def back_A(bb):
                    pe.wait_ge(s_a_sums_out, bb + 1)
                    for t in range(TPB):
                        for g in range(2):
                            last = tr(bank[1 + bb][:, 72 * (2 * t + g):72 * (2 * t + g) + 72],
                                      oraw[0:72, bb, N * g + 128 * t:N * g + 128 * t + 128], ident[0:72, 0:72])
                    last.then_inc(s_a_sums_turned, 1)

                def result_A(bb):
                    pe.wait_ge((s_order_read0, s_order_read1)[bb], 16)
                    for t in range(TPB * bb, TPB * bb + TPB):
                        last = tr(bank[bb][:, 128 * t:128 * t + 128], x_tok[:, t, :], ident)
                    last.then_inc(s_a_result_turned, 1)

                LAG = 2
                for n in range(NB * H + LAG):
                    for k in range(UNITS + 3 + 2 * n, min(UNITS + 5 + 2 * n, 2 * UNITS)):
                        scores_A(k, ring[1][(k - UNITS) % 3], k - 2)
                    if n == UNITS // 2 + 2:
                        max_transposed(1, range(TPB, T), 2)
                    if n < NB * H:
                        score_A(n)
                    if n >= LAG:
                        value_A(n - LAG)
                    if n == H + LAG + 2:
                        back_A(0)
                    if n == NB * H - 2:
                        result_A(0)
                    if n == NB * H - 1:
                        mean_pe(xT, 0, 0, s_stream, NB + 1)
                var_pe(1, 0, 0)
                back_A(1)

                pe.wait_ge(s_local_weights, 16 * len(local_loads))

                def project(l, t):
                    pe.wait_ge(s_shifted, 2 * NB * l + t // TPB + 1)
                    for part in range(3):
                        n = 3 * t + part
                        if l == 0 and n == 5:
                            pe.wait_ge(s_a_normalised, NB)
                        if n >= 6:
                            pe.wait_ge(s_l_projection_out, l * 3 * T + n - 5)
                        mm(bank[proj[n % 6]][:, :], hT[:, :, :].rearrange("p b n -> p (b n)")[:, 128 * t:128 * t + 128],
                           w_qkv[:, l, INNER * part:INNER * part + INNER], start=True, stop=True).then_inc(s_l_projected, 1)

                def running(t):
                    pe.wait_ge(s_c_outer, t + 1)
                    if t >= 3:
                        pe.wait_ge(s_c_times_q, 2 * (t - 2))
                    for half in range(2):
                        o = bank[run[t % 3] + half][:, :]
                        at = slice(512 * half, 512 * half + 512)
                        last = mm(o, causal, outer[:, t, at], start=True, stop=t % TPB == 0)
                        if t % TPB:
                            last = mm(o, ones, outer[:, t - 1, at], start=False, stop=True)
                        last.then_inc(s_c_running, 1)

                hflat = hT[:, :, :].rearrange("p b n -> p (b n)")
                for l in range(LAYERS):
                    for t in range(0 if l == 0 else 1, T - 1):
                        if l == 0 and t == TPB:
                            result_A(1)
                            mean_pe(xT, 1, 1, s_stream, NB + 2)
                            var_pe(1, 1, 1)
                        project(l, t)

                    def turned(m):
                        pe.wait_ge(s_l_scaled, l * 2 * T + m + 1)
                        if m < 3:
                            pe.wait_ge(s_l_projection_out, l * 3 * T + m + 7)
                        for p in range(4):
                            last = tr(bank[turn[m]][:, 128 * p:128 * p + 128],
                                      qk_c[:, m, 2 * p:2 * p + 2, :].rearrange("p h d -> p (h d)"), ident)
                        last.then_inc(s_l_turned, 1)

                    def scores_for_max(bb):
                        pe.wait_ge(s_l_turned_out, l * 2 * T + 4 * bb + 4)
                        n = NSB // NB * bb
                        for t, per in ((0, 4), (1, 2)):
                            w = 128 + WIN * t
                            for h0 in range(0, LH, per):
                                if n >= 4:
                                    pe.wait_ge(s_l_max, l * NSB + n - 3)
                                for j in range(per):
                                    h = h0 + j
                                    o = bank[mring[n % 4]][:, w * j:w * j + w]
                                    q0 = N * bb + 128 * t
                                    mm(o, lqT[:, h % 2, h // 2, q0:q0 + 128],
                                       lkT[:, h // 2, q0 - WIN * t:q0 + 128], start=True, stop=False)
                                    last = mm(o, identb, cb[:, K_MQ + WIN * (1 - t):K_MQ + 192],
                                              start=False, stop=True)
                                last.then_inc(s_l_scores, 1)
                                n += 1

                    def score_B(n):
                        bb, p, kt = n // LH, n % LH // 2, n % 2
                        w, k0 = 192 - 64 * kt, N * bb + 128 * kt
                        if n >= 3:
                            pe.wait_ge(s_l_exp, l * NB * LH + n - 2)
                        o = bank[5 + n % 3]
                        mm(o[:, 0:2 * w], lkT[:, p, k0:k0 + 128], lqT[:, :, p, k0:k0 + w],
                           start=True, stop=False, skip_group_check=True)
                        mm(o[:, 0:2 * w], identb, cb[:, K_MK:K_MK + w].unsqueeze(1).to_broadcast([128, 2, w]),
                           start=False, stop=False, skip_group_check=True)
                        for e in range(2):
                            h = 2 * p + e
                            last = mm(o[:, w * e:w * e + w], cb[0:3 * H, K_MAX + 128 * h:K_MAX + 128 * h + 128],
                                      mxT[:, k0:k0 + w], start=False, stop=e == 1, skip_group_check=True)
                        last.then_inc(s_l_scores_less_max, 1)

                    def value_B(g):
                        bb, p = g // (LH // 2), g % (LH // 2)
                        pe.wait_ge(s_l_exp, l * NB * LH + 2 * g + 2)
                        if g >= 2:
                            pe.wait_ge(s_l_values_out, l * NB * LH // 2 + g - 1)
                        P = [PT[:, (2 * g + kt) % 4, :, :].rearrange("p a b -> p (a b)") for kt in range(2)]
                        for e in range(2):
                            o, h = bank[g % 2][0:LD + 1, N * e:N * e + N], 2 * p + e
                            mm(o[:, 0:192], lv[:, TPB * bb, h, :], P[0][:, 192 * e:192 * e + 192], start=True, stop=True)
                            last = mm(o[:, 128:256], lv[:, TPB * bb + 1, h, :], P[1][:, 128 * e:128 * e + 128],
                                      start=False, stop=True, skip_group_check=True)
                        last.then_inc(s_l_values, 1)

                    def back_B(g):
                        base = l * NB * LH // 2
                        pe.wait_ge(s_l_values_out, base + g + 1)
                        if g >= 2:
                            pe.wait_ge(s_l_normalised, base + g - 1)
                        for t in range(TPB):
                            for e in range(2):
                                k = 2 * t + e
                                last = tr(bank[2 + g % 2][:, (LD + 1) * k:(LD + 1) * k + LD + 1],
                                          oraw[0:LD + 1, g % 2, N * e + 128 * t:N * e + 128 * t + 128],
                                          ident[0:LD + 1, 0:LD + 1])
                        last.then_inc(s_l_values_turned, 1)

                    def o_turned(t):
                        pe.wait_ge(s_l_normalised, l * groups + (t // TPB + 1) * LH // 2)
                        for p in range(4):
                            last = tr(bank[6 + t % 2][:, 128 * p:128 * p + 128],
                                      o_tok[:, t, 2 * p:2 * p + 2, :].rearrange("p h d -> p (h d)"), ident)
                        last.then_inc(s_l_heads_turned, 1)

                    def output(b):
                        pe.wait_ge(s_l_heads_out, l * T + TPB * (b + 1))
                        for c in range(4):
                            last = mm(bank[4 - 2 * b][:, cols(b)], w_o[:, l, c, :], oT[:, c, cols(b)], start=(c == 0), stop=(c == 3))
                        last.then_inc(s_l_output, 1)

                    groups = NB * LH // 2
                    for bb in range(NB):
                        for m in ((0, 1, 2, 3), (6, 7))[bb]:
                            turned(m)
                        scores_for_max(bb)
                        if bb == 0:
                            project(l, T - 1)
                        else:
                            o_turned(0)
                            o_turned(1)
                        max_transposed(NB + NB * l + bb, range(TPB * bb, TPB * bb + TPB), 4)
                        if bb == 1:
                            output(0)
                        g0, g1 = LH // 2 * bb, LH // 2 * (bb + 1)
                        for g in range(g0, g1 + 2):
                            if g < g1:
                                score_B(2 * g)
                                score_B(2 * g + 1)
                            if g0 + 1 <= g <= g1:
                                value_B(g - 1)
                            if bb == 0 and g == g1:
                                turned(4)
                                turned(5)
                            if g >= g0 + 2:
                                back_B(g - 2)
                            if bb == 1 and g == g0 + 2:
                                mean_pe(hflat, 0, 4, s_shifted, 2 * NB * l + NB + 1)
                            if bb == 1 and g == g0 + 3:
                                var_pe(2 + l, 0, 4)
                    def hidden(b, c):
                        c0, w = HCH[c]
                        for half in range(2):
                            at = half * HID + c0
                            last = mm(bank[ffb[b][c]][0:w, N * half:N * half + N], w_1[:, l, at:at + w], nT[:, cols(b)],
                                      start=True, stop=True)
                        last.then_inc(s_hidden, 1)

                    def contracted(b):
                        for c, (c0, w) in enumerate(HCH):
                            pe.wait_ge(s_gated, (NB * l + b) * len(HCH) + c + 1)
                            last = mm(bank[b][:, cols(b)], w_2[0:w, l, c, :], hid[0:w, c, cols(b)],
                                      start=(c == 0), stop=(c == len(HCH) - 1))
                        last.then_inc(s_contracted, 1)

                    pe.wait_ge(s_l_affine, NB * l + 1)
                    hidden(0, 0)
                    o_turned(2)
                    o_turned(3)
                    hidden(0, 1)
                    output(1)
                    hidden(0, 2)
                    mean_pe(hflat, 1, 1, s_shifted, 2 * NB * l + NB + 2)
                    var_pe(2 + l, 1, 1)
                    contracted(0)
                    pe.wait_ge(s_l_affine, NB * l + 2)
                    for c in range(len(HCH)):
                        hidden(1, c)
                    if l + 1 < LAYERS:
                        project(l + 1, 0)
                    else:
                        running(0)
                    contracted(1)
                for b in range(NB):
                    mean_pe(xT, b, b, s_stream, 2 * NB + b + 1)
                running(1)
                for b in range(NB):
                    var_pe(4, b, b)
                running(2)
                pe.wait_ge(s_normal, 4 * NB + 1)
                biased(bank[0][:, :], 0, 128)
                for t in range(T):
                    pe.wait_ge(s_normal, 4 * NB + t // TPB + 1)
                    last = mm(bank[0][:, 128 * t:128 * t + 128], nT[:, 128 * t:128 * t + 128], w_c[:, 0, :],
                              start=False, stop=True, skip_group_check=True)
                last.then_inc(s_c_query, 1)
                pe.wait_ge(s_c_k_feature, 1)
                for t in range(T):
                    o = bank[1][:, 128 * t:128 * t + 128]
                    last = mm(o, causal, kf[:, t, :], start=True, stop=t % TPB == 0)
                    if t % TPB:
                        last = mm(o, ones, kf[:, t - 1, :], start=False, stop=True)
                last.then_inc(s_c_k_running, 1)
                running(3)
                for b in range(NB):
                    for t in range(TPB * b, TPB * b + TPB):
                        pe.wait_ge(s_c_quotient, t + 1)
                        last = tr(bank[6 * b][:, 128 * t:128 * t + 128], nv[:, t, :], ident)
                    last.then_inc(s_c_quotient_turned, 1)
                    pe.wait_ge(s_c_quotient_out, b + 1)
                    mm(bank[1 + 6 * b][:, cols(b)], w_c[:, 3, :], nvT[:, cols(b)], start=True, stop=True).then_inc(s_c_output, 1)

                for b in range(NB):
                    mean_pe(xT, b, 4 + b, s_stream, 3 * NB + b + 1)
                for b in range(NB):
                    var_pe(5, b, 4 + b)
                pe.wait_ge(s_expert_weights, 16 * len(expert_loads))
                biased(bank[1][:, 0:T * E], 384, E)
                for t in range(T):
                    pe.wait_ge(s_normal, 5 * NB + t // TPB + 1)
                    last = mm(bank[1][:, E * t:E * t + E], nT[:, 128 * t:128 * t + 128], w_r[:, :],
                              start=False, stop=True, skip_group_check=True)
                last.then_inc(s_logits, 1)

                def gate_up(n):
                    m = 128 if n < PAIRS else I
                    if n < PAIRS:
                        gw = w_g[:, 2 * n:2 * n + 2, :].rearrange("p e i -> p (e i)")
                        uw = w_u[:, 2 * n:2 * n + 2, :].rearrange("p e i -> p (e i)")
                    else:
                        gw, uw = w_gs[:, 0, :], w_gs[:, 1, :]
                    if n >= 2:
                        pe.wait_ge(s_e_silu, n - 1)
                    mm(bank[2 + 3 * (n % 2)][0:m, :], gw, nT[:, :], start=True, stop=True).then_inc(s_e_gate, 1)
                    if n >= 2:
                        pe.wait_ge(s_e_weighted, n - 1)
                    mm(bank[3 + 3 * (n % 2)][0:m, :], uw, nT[:, :], start=True, stop=True).then_inc(s_e_up, 1)

                def weights(n):
                    mm(bank[4 + 3 * (n % 2)][:, :], cb[0:3 * E, K_SEL + 128 * n:K_SEL + 128 * n + 128],
                       wS[:, :], start=True, stop=True).then_inc(s_e_weights, 1)

                def down(n):
                    pe.wait_ge(s_e_weighted, n + 1)
                    if n < PAIRS:
                        mm(bank[0][:, :], w_d[:, n, :], hm[:, n % 2, :], start=False, stop=False).then_inc(s_e_down, 1)
                    else:
                        mm(bank[0][:, :], w_ds[:, :], hm[0:I, n % 2, :], start=False, stop=True).then_inc(s_e_down, 1)

                gate_up(0)
                gate_up(1)
                pe.wait_ge(s_weight_parts, 4)
                for t in range(T):
                    last = tr(bbank(7)[0:3 * E, 128 * t:128 * t + 128],
                              w_p[:, t, :, :].rearrange("p a e -> p (a e)"), identb)
                last.then_inc(s_weights_turned, 1)
                for t in range(T):
                    last = tr(bank[4][0:E, 128 * t:128 * t + 128], w_t[:, t, :], ident)
                last.then_inc(s_weights_turned, 1)
                pe.wait_ge(s_weights_out, 2)
                weights(0)
                weights(1)
                mm(bank[0][:, :], b_d[:, :], wT[:, :], start=True, stop=False)
                for n in range(2, PAIRS + 2):
                    if n <= PAIRS:
                        gate_up(n)
                        if n < PAIRS:
                            weights(n)
                    if n == 2:
                        down(0)
                    down(n - 1)
                for b in range(NB):
                    pe.wait_ge(s_final, b + 1)
                    for t in range(TPB * b, TPB * b + TPB):
                        last = tr(bank[1 + b][:, 128 * t:128 * t + 128], xT[:, 128 * t:128 * t + 128], ident)
                    last.then_inc(s_final_turned, 1)
                pe.wait_ge(s_final_out, NB)
                pe.drain().then_inc(s_end_pe, 1)

        @block.scalar
        def _(act):
            A = nc.scalar.activation
            act.wait_ge(s_vectors_cleared, 1)
            for dst, src in bias_loads:
                act.dma_start(dst, src).then_inc(s_bias_vectors, 16)
            act.wait_ge(s_bias_vectors, 16 * len(bias_loads))
            A(tg[:, :], gate[:, :], ACT.Tanh).then_inc(s_gates, 1)
            act.wait_ge(s_setup, SET)
            with act.Fori(0, TURNS) as it:
                act.wait_ge(s_turn_open, it + 1)
                act.sem_inc(s_seen_act, 1)

                def log_exp():
                    act.preload_act_table_set("natural_log_exp_and_others")

                def norm_act(stage, b, frm):
                    n = NB * stage + b + 1
                    act.wait_ge(s_variance, n)
                    A(ln_r[:, cols(b)], bank[frm][:, cols(b)], ACT.Ln, bias=EPS).then_inc(s_variance_log, 1)
                    act.wait_ge(s_variance_log, n)
                    A(ln_r[:, cols(b)], ln_r[:, cols(b)], ACT.Exp, scale=-0.5).then_inc(s_rstd, 1)

                def max_act(n, at, frm):
                    act.wait_ge(s_max_turned, n + 1)
                    A(mxT[:, at], bbank(frm)[0:3 * H, at], ACT.Copy).then_inc(s_max_out, 1)

                act.wait_ge(s_inputs_turned, 2)
                A(cT[:, :], bank[1][:, :], ACT.Copy).then_inc(s_context_out, 1)
                log_exp()
                for b in range(NB):
                    norm_act(0, b, b)
                act.wait_ge(s_projected, 2)
                act.wait_ge(s_padded, 2)
                for g in range(2):
                    last = A(va[:, :, g, :].rearrange("p t (h x) -> p t h x", x=VS)[:, :, :, 0:DH],
                             bank[3][:, :].rearrange("p (t g h d) -> p t g h d", t=T, g=2, h=8)[:, :, g], ACT.Copy)
                last.then_inc(s_projection_out, 1)
                for n in range(2):
                    act.wait_ge(s_projected, 3 + n)
                    A(flat(kv_c[:, n]), bank[4 + n][:, :], ACT.Copy).then_inc(s_projection_out, 1)
                for t in range(T):
                    act.wait_ge(s_stack_turned, t + 1)
                    A(kS[:, :, 128 * t:128 * t + 128], bbank(2 + t).rearrange("p (a n) -> p a n", a=H // 2), ACT.Copy)\
                        .then_inc(s_k_stack_out, 1)
                for t in range(T):
                    act.wait_ge(s_stack_turned, T + t + 1)
                    for e in range(2):
                        last = A(qS[64 * e:64 * e + 64, e, :, 128 * t:128 * t + 128],
                                 bbank(2 + t)[64 * e:64 * e + 64, :].rearrange("p (a n) -> p a n", a=H // 2), ACT.Copy)
                    last.then_inc(s_q_stack_out, 1)
                max_act(0, cols(0), 2)
                for n in range(NB * H):
                    if n == UNITS // 2 + 2:
                        max_act(1, cols(1), 2)
                    act.wait_ge(s_a_scores_less_max, n + 1)
                    if n >= 4:
                        act.wait_ge(s_a_values, n - 3)
                    A(PT[:, n % 4, :, 0:N], bank[3 + n % 3][:, :].rearrange("p (e q) -> p e q", e=2), ACT.Exp,
                      scale=float(DH) ** -0.5).then_inc(s_a_exp, 1)
                    if n == 3:
                        act.wait_ge(s_c_k_min, 1)
                        A(kf_exp[:, :], kf_min[:, :], ACT.Exp).then_inc(s_c_k_exp, 1)
                    if n == H + 2:
                        act.wait_ge(s_a_values, H)
                        A(oraw[0:72, 0, :], bank[6][0:72, :], ACT.Copy).then_inc(s_a_sums_out, 1)
                norm_act(1, 0, 0)
                act.wait_ge(s_a_values, NB * H)
                A(oraw[0:72, 1, :], bank[7][0:72, :], ACT.Copy).then_inc(s_a_sums_out, 1)

                for l in range(LAYERS):
                    def inverse(t):
                        act.wait_ge(s_l_bounded, l * T + t + 1)
                        A(qk_lg[:, 2 * t:2 * t + 2, :], qk_ss[:, 2 * t:2 * t + 2, :], ACT.Ln, scale=2.0 ** 20)\
                            .then_inc(s_l_log, 1)
                        act.wait_ge(s_l_log, l * T + t + 1)
                        A(qk_in[:, 2 * t:2 * t + 2, :], qk_lg[:, 2 * t:2 * t + 2, :], ACT.Exp, scale=-0.5,
                          bias=float(10 * np.log(2.0))).then_inc(s_l_inverse_norm, 1)

                    def projected(t):
                        for part in range(3):
                            n = l * 3 * T + 3 * t + part
                            act.wait_ge(s_l_projected, n + 1)
                            src = bank[proj[(3 * t + part) % 6]]
                            if part == 2:
                                A(lv[:, t, :, 0:LD], src[:, :].rearrange("p (h d) -> p h d", h=LH), ACT.Copy)\
                                    .then_inc(s_l_projection_out, 1)
                                continue
                            m = 2 * t + part
                            A(qk[:, m, :, :].rearrange("p h d -> p (h d)"), src[:, :], ACT.Copy).then_inc(s_l_projection_out, 1)
                            if t >= TPB:
                                continue
                            act.wait_ge(s_l_projection_out, n + 1)
                            if m >= 2:
                                act.wait_ge(s_l_sums, l * 2 * T + m - 1)
                            A(square(m), qk[:, m, :, :].rearrange("p h d -> p (h d)"), ACT.Square)\
                                .then_inc(s_l_squared, 1)

                    def out_of_psum(m):
                        act.wait_ge(s_l_turned, l * 2 * T + m + 1)
                        t, src = m // 2, bank[turn[m]]
                        v = src[:, :].rearrange("p (a n) -> p a n", a=4)
                        if m % 2:
                            A(lkT[:, :, 128 * t:128 * t + 128], v, ACT.Copy).then_inc(s_l_turned_out, 1)
                        else:
                            for e in range(2):
                                last = A(lqT[64 * e:64 * e + 64, e, :, 128 * t:128 * t + 128],
                                         v[64 * e:64 * e + 64], ACT.Copy)
                            last.then_inc(s_l_turned_out, 1)

                    base = l * NB * LH

                    def raw_B(g):
                        act.wait_ge(s_l_values, base // 2 + g + 1)
                        if g >= 2:
                            act.wait_ge(s_l_values_turned, base // 2 + g - 1)
                        A(oraw[0:LD + 1, g % 2, :], bank[g % 2][0:LD + 1, :], ACT.Copy).then_inc(s_l_values_out, 1)

                    def turned_out(t):
                        act.wait_ge(s_l_heads_turned, l * T + t + 1)
                        A(oT[:, :, 128 * t:128 * t + 128], bank[6 + t % 2][:, :].rearrange("p (a n) -> p a n", a=4),
                          ACT.Copy).then_inc(s_l_heads_out, 1)

                    projected(0)
                    if l:
                        log_exp()
                    projected(1)
                    inverse(0)
                    if l == 0:
                        norm_act(1, 1, 1)
                    projected(2)
                    inverse(1)
                    for bb in range(NB):
                        for m in range(2 * TPB * bb, 2 * TPB * bb + 2 * TPB):
                            out_of_psum(m)
                        if bb == 0:
                            projected(3)
                        else:
                            turned_out(0)
                            turned_out(1)
                        max_act(NB + NB * l + bb, cols(bb), 4)
                        n0 = LH * bb
                        for n in range(n0, n0 + LH):
                            w = 192 - 64 * (n % 2)
                            act.wait_ge(s_l_scores_less_max, base + n + 1)
                            if n >= 4:
                                act.wait_ge(s_l_values, base // 2 + (n - 4) // 2 + 1)
                            A(PT[:, n % 4, :, :].rearrange("p a b -> p (a b)")[:, 0:2 * w], bank[5 + n % 3][:, 0:2 * w],
                              ACT.Exp, scale=8.0).then_inc(s_l_exp, 1)
                            if n >= n0 + 3 and n % 2:
                                raw_B((n - 3) // 2)
                            if bb == 0 and n in (1, 5):
                                inverse(TPB + n // 4)
                        if bb == 1:
                            norm_act(2 + l, 0, 4)
                        raw_B((n0 + LH) // 2 - 1)
                    def gelu(b, c):
                        w = HCH[c][1]
                        v = b1_column(l, 1, c)
                        act.wait_ge(s_hidden, (NB * l + b) * len(HCH) + c + 1)
                        A(gel[0:w, c, cols(b)], bank[ffb[b][c]][0:w, N:2 * N], ACT.Gelu, bias=vcol[0:w, v:v + 1])\
                            .then_inc(s_gelu, 1)

                    gelu(0, 0)
                    turned_out(2)
                    turned_out(3)
                    gelu(0, 1)
                    gelu(0, 2)
                    log_exp()
                    norm_act(2 + l, 1, 1)
                    for c in range(len(HCH)):
                        gelu(1, c)
                log_exp()
                for b in range(NB):
                    norm_act(4, b, b)
                for b in range(NB):
                    act.wait_ge(s_c_q_min, b + 1)
                    A(qf_exp[:, cols(b)], qf_min[:, cols(b)], ACT.Exp).then_inc(s_c_q_exp, 1)
                act.wait_ge(s_c_denominator, 1)
                A(rden[:, :], den[:, :], ACT.Ln, bias=1e-6).then_inc(s_c_denominator_log, 1)
                act.wait_ge(s_c_denominator_log, 1)
                A(rden[:, :], rden[:, :], ACT.Exp, scale=-1.0).then_inc(s_c_denominator_inverse, 1)
                for b in range(NB):
                    act.wait_ge(s_c_quotient_turned, b + 1)
                    A(nvT[:, cols(b)], bank[6 * b][:, cols(b)], ACT.Copy).then_inc(s_c_quotient_out, 1)
                for b in range(NB):
                    norm_act(5, b, 4 + b)
                act.wait_ge(s_logits, 1)
                A(flat(r_e), bank[1][:, 0:T * E], ACT.Exp, scale=-1.0).then_inc(s_logits_exp, 1)
                for n in range(PAIRS + 1):
                    if n == 2:
                        act.wait_ge(s_weights_turned, 1)
                        A(wS[:, :], bbank(7)[0:3 * E, 0:TOK], ACT.Copy).then_inc(s_weights_out, 1)
                        act.wait_ge(s_weights_turned, 2)
                        A(wT[:, :], bank[4][0:E, :], ACT.Copy).then_inc(s_weights_out, 1)
                    m = 128 if n < PAIRS else I
                    v = V_BG + n if n < PAIRS else V_BGS
                    act.wait_ge(s_e_gate, n + 1)
                    if n >= 2:
                        act.wait_ge(s_e_gated, n - 1)
                    A(sg[0:m, n % 2, :], bank[2 + 3 * (n % 2)][0:m, :], ACT.Silu, bias=vcol[0:m, v:v + 1])\
                        .then_inc(s_e_silu, 1)
                for b in range(NB):
                    act.wait_ge(s_final_turned, b + 1)
                    A(flat(o_out)[:, cols(b)], bank[1 + b][:, cols(b)], ACT.Copy).then_inc(s_final_out, 1)
                act.wait_ge(s_final_out, NB)
                act.drain().then_inc(s_end_act, 1)

        @block.vector
        def _(dve):
            V = nc.vector
            V.memset(vrow[:, :], 0.0).then_inc(s_vectors_cleared, 1)
            V.memset(lqT[:, :, :, :], 0.0)
            V.memset(mx[:, :, :], 0.0)
            V.memset(hT[:, :, :], 0.0)
            V.memset(lv[:, :, :, LD:LD + 1], 1.0).then_inc(s_setup, 1)
            dve.wait_ge(s_setup_turned, 1)
            V.tensor_copy(flat(w_a), bank[0][:, 0:384])
            dve.wait_ge(s_setup_turned, 2)
            V.tensor_copy(vcol[:, :], bank[1][:, 0:V_ALL]).then_inc(s_setup, 1)
            dve.wait_ge(s_constants, 16)
            dve.wait_ge(s_bias_rows, 4 * 16)
            r_h, r_m = (part(768 + 256 * n, 256).bitcast(BF16)[0:3, 0:ROW] for n in range(2))
            r_f = part(1280, ROW)[0:3, :]
            V.tensor_copy(r_h, row[:, :]).then_inc(s_row_parts, 1)
            dve.wait_ge(s_row_parts, 1)
            V.tensor_tensor(r_f, row[:, :], r_h, ALU.subtract).then_inc(s_row_parts, 1)
            dve.wait_ge(s_row_parts, 2)
            V.tensor_copy(r_m, r_f).then_inc(s_row_parts, 1)
            dve.wait_ge(s_row_parts, 3)
            V.tensor_tensor(r_f, r_f, r_m, ALU.subtract)
            V.tensor_scalar(row_p[:, :], r_h, ident[0:3, 0:1], None, ALU.mult).then_inc(s_row_parts, 1)
            dve.wait_ge(s_row_parts, 4)
            V.scalar_tensor_tensor(out=row_p[:, :], in0=r_m, scalar=ident[0:3, 1:2], in1=row_p[:, :],
                                   op0=ALU.mult, op1=ALU.add).then_inc(s_row_parts, 1)
            dve.wait_ge(s_row_parts, 5)
            V.scalar_tensor_tensor(out=row_p[:, :], in0=r_f, scalar=ident[0:3, 2:3], in1=row_p[:, :],
                                   op0=ALU.mult, op1=ALU.add).then_inc(s_row_parts, 1)
            dve.wait_ge(s_row_parts, 6)
            dve.wait_ge(s_setup, 2)
            dve.wait_ge(s_gates, 1)
            V.tensor_tensor(bdg[:, :], vcol[:, V_BDS:V_BDS + 1], tg[:, 3:4], ALU.mult)
            V.tensor_tensor(bog[:, :], vcol[:, V_BO:V_BO + 1], tg[:, 1:2], ALU.mult).then_inc(s_setup, 1)
            dve.wait_ge(s_setup, SET)
            with dve.Fori(0, TURNS) as it:
                dve.wait_ge(s_turn_open, it + 1)
                dve.sem_inc(s_seen_dve, 1)

                def centred(stage, b, src, frm):
                    dve.wait_ge(s_mean, NB * stage + b + 1)
                    V.tensor_tensor(ln_c[:, cols(b)], src[:, cols(b)], bank[frm][:, cols(b)], ALU.subtract).then_inc(s_centred, 1)
                    dve.wait_ge(s_centred, NB * stage + b + 1)
                    V.tensor_tensor(ln_sq[:, cols(b)], ln_c[:, cols(b)], ln_c[:, cols(b)], ALU.mult).then_inc(s_squared, 1)

                def normal(stage, b, dst):
                    dve.wait_ge(s_rstd, NB * stage + b + 1)
                    V.tensor_tensor(dst[:, cols(b)], ln_c[:, cols(b)], ln_r[:, cols(b)], ALU.mult).then_inc(s_normal, 1)

                def split(n, src, hi, mid, lo, res, s, k0):
                    V.tensor_copy(hi, src).then_inc(s, 1)
                    dve.wait_ge(s, k0 + 1)
                    V.tensor_tensor(res, src, hi, ALU.subtract).then_inc(s, 1)
                    dve.wait_ge(s, k0 + 2)
                    V.tensor_copy(mid, res).then_inc(s, 1)
                    dve.wait_ge(s, k0 + 3)
                    V.tensor_tensor(lo, res, mid, ALU.subtract).then_inc(s, 1)
                    dve.wait_ge(s, k0 + 4)

                def split_stack(n, step, src, at, tiles):
                    split(0, src, part_h[:, at], part_m[:, at], part_l[:, at], part_f[:, at], s_split, 4 * step)
                    st = stack[:, tiles, :, 0:48].rearrange("p t h (s d) -> p (t h) s d", d=DH)
                    parts = [p[:, at].rearrange("p (h d) -> p h d", d=DH) for p in (part_h, part_m, part_l)]
                    if n == 0:
                        order = (0, 1, 2, 0, 1, 0)
                    else:
                        dve.wait_ge(s_stack_turned, T)
                        order = (0, 0, 0, 1, 1, 2)
                    for slot, part in enumerate(order):
                        last = V.tensor_copy(st[:, :, slot, :], parts[part])
                    last.then_inc(s_stacked, 1)

                def scaled(m, l):
                    dve.wait_ge(s_l_inverse_norm, l * T + m // 2 + 1)
                    dve.wait_ge(s_l_rotated, l * 2 * T + m + 1)
                    V.tensor_tensor(qk_c[:, m], qk_c[:, m], qk_in[:, m, :].unsqueeze(2).to_broadcast([128, LH, LD]),
                                    ALU.mult).then_inc(s_l_scaled, 1)

                def max_split(n, ts):
                    split(n, mx[:, ts, :], mx_p[:, ts, 0, :], mx_p[:, ts, 1, :], mx_p[:, ts, 2, :], mx_r[:, ts, :],
                          s_max_parts, 4 * n)

                dve.wait_ge(s_inputs_turned, 1)
                for b in range(NB):
                    V.tensor_copy(xT[:, cols(b)], bank[0][:, cols(b)]).then_inc(s_stream, 1)
                for b in range(NB):
                    centred(0, b, xT, b)
                dve.wait_ge(s_projected, 1)
                split_stack(0, 0, bank[2][:, :], slice(0, TOK), slice(0, T))
                for b in range(NB):
                    normal(0, b, nT)
                dve.wait_ge(s_projected, 5)
                for b in range(NB):
                    split_stack(1, 1 + b, bank[6][:, cols(b)], cols(b), slice(TPB * b, TPB * b + TPB))

                def maxima_A(bb):
                    for n in range(UNITS * bb, UNITS * bb + UNITS):
                        t, p = n // (H // 2), n % (H // 2)
                        to = ring[bb][(n - UNITS * bb) % len(ring[bb])]
                        dve.wait_ge(s_a_scores, n + 1)
                        V.tensor_reduce(mx[:, t, 2 * p:2 * p + 2], bank[to][:, :].rearrange("p (e k) -> p e k", e=2),
                                        AX_X, ALU.max).then_inc(s_a_max, 1)
                    dve.wait_ge(s_a_max, UNITS * (bb + 1))
                    max_split(bb, slice(TPB * bb, TPB * bb + TPB))

                maxima_A(0)
                maxima_A(1)
                dve.wait_ge(s_c_k_exp, 1)
                V.scalar_tensor_tensor(out=flat(kf), in0=flat(kf), scalar=0.0, in1=kf_exp[:, :],
                                       op0=ALU.max, op1=ALU.add).then_inc(s_c_k_feature, 1)

                def quotient_A(bb):
                    dve.wait_ge(s_a_sums_turned, bb + 1)
                    src = bank[1 + bb][:, 0:TPB * 144].rearrange("p (a x) -> p a x", x=9)
                    r = rsum[:, TPB * bb:TPB * bb + TPB, :].rearrange("p t h -> p (t h)").unsqueeze(2)
                    V.reciprocal(r, src[:, :, 8:9]).then_inc(s_a_reciprocal, 1)
                    dve.wait_ge(s_a_reciprocal, bb + 1)
                    V.tensor_tensor(att[:, TPB * bb:TPB * bb + TPB, :].rearrange("p t (h d) -> p (t h) d", d=DH),
                                    src[:, :, 0:8], r.to_broadcast([128, TPB * H, DH]), ALU.mult).then_inc(s_a_normalised, 1)

                def shifted(b):
                    V.tensor_copy(hT[0:64, b, :], fT[0:64, cols(b)])
                    V.tensor_copy(hT[64:128, b, 1:N], fT[64:128, N * b:N * b + N - 1]).then_inc(s_shifted, 1)

                def stream_A(bb):
                    dve.wait_ge(s_a_result_turned, bb + 1)
                    V.scalar_tensor_tensor(out=xT[:, cols(bb)], in0=bank[bb][:, cols(bb)], scalar=tg[:, 0:1],
                                           in1=xT[:, cols(bb)], op0=ALU.mult, op1=ALU.add).then_inc(s_stream, 1)

                def normal_A(bb):
                    normal(1, bb, fT)
                    dve.wait_ge(s_normal, NB + bb + 1)
                    shifted(bb)

                hflat = hT[:, :, :].rearrange("p b n -> p (b n)")
                quotient_A(0)
                stream_A(0)
                centred(1, 0, xT, 0)
                normal_A(0)
                quotient_A(1)

                def layer_added(l, b):
                    dve.wait_ge(s_contracted, NB * l + b + 1)
                    V.scalar_tensor_tensor(out=fT[:, cols(b)], in0=bank[b][:, cols(b)],
                                           scalar=vcol[:, V_B2 + l:V_B2 + l + 1], in1=fT[:, cols(b)],
                                           op0=ALU.add, op1=ALU.add).then_inc(s_layer_added, 1)
                    dve.wait_ge(s_layer_added, NB * l + b + 1)
                    if l + 1 < LAYERS:
                        shifted(b)
                    else:
                        V.scalar_tensor_tensor(out=xT[:, cols(b)], in0=fT[:, cols(b)], scalar=tg[:, 2:3],
                                               in1=xT[:, cols(b)], op0=ALU.mult, op1=ALU.add).then_inc(s_stream, 1)

                for l in range(LAYERS):
                    b2 = l * 2 * T

                    dve.wait_ge(s_tables, 1)

                    def rotated(m):
                        t = m // 2
                        dve.wait_ge(s_l_projection_out, l * 3 * T + 3 * t + m % 2 + 1)
                        tab = rot[:, l, t % TPB, m % 2, 0, :].unsqueeze(1).to_broadcast([128, LH, LD])
                        V.tensor_tensor(qk_c[:, m], qk[:, m], tab, ALU.mult).then_inc(s_l_cosine, 1)
                        if m < 2 * TPB:
                            dve.wait_ge(s_l_squared, l * 2 * TPB + m + 1)
                        else:
                            dve.wait_ge(s_l_squared_pool, l * 2 * TPB + m - 2 * TPB + 1)
                        V.tensor_reduce(qk_ss[:, m, :], square(m).rearrange("p (h d) -> p h d", h=LH),
                                        AX_X, ALU.add).then_inc(s_l_sums, 1)
                        if m % 2:
                            dve.wait_ge(s_l_sums, b2 + m + 1)
                            V.tensor_scalar(qk_ss[:, m - 1:m + 1, :], qk_ss[:, m - 1:m + 1, :], 1e-24, None, ALU.max)\
                             .then_inc(s_l_bounded, 1)
                        dve.wait_ge(s_l_cosine, b2 + m + 1)
                        dve.wait_ge(s_l_sine, b2 + m + 1)
                        V.tensor_tensor(qk_c[:, m], qk_c[:, m], qk_s[:, m], ALU.add).then_inc(s_l_rotated, 1)

                    def maxima(bb):
                        n = NSB // NB * bb
                        for t, per in ((0, 4), (1, 2)):
                            w = 128 + WIN * t
                            for h0 in range(0, LH, per):
                                dve.wait_ge(s_l_scores, l * NSB + n + 1)
                                V.tensor_reduce(mx[:, TPB * bb + t, h0:h0 + per],
                                                bank[mring[n % 4]][:, 0:w * per].rearrange("p (h k) -> p h k", h=per),
                                                AX_X, ALU.max).then_inc(s_l_max, 1)
                                n += 1
                        dve.wait_ge(s_l_max, l * NSB + n)
                        max_split(NB + NB * l + bb, slice(TPB * bb, TPB * bb + TPB))

                    def quotient_B(g):
                        k = l * NB * LH // 2 + g
                        bb, p = g // (LH // 2), g % (LH // 2)
                        dve.wait_ge(s_l_values_turned, k + 1)
                        src = bank[2 + g % 2][:, 0:4 * (LD + 1)].rearrange("p (t e x) -> p t e x", t=TPB, e=2)
                        r = rsum[:, TPB * bb:TPB * bb + TPB, 2 * p:2 * p + 2]
                        V.reciprocal(r.unsqueeze(3), src[:, :, :, LD:LD + 1]).then_inc(s_l_reciprocal, 1)
                        dve.wait_ge(s_l_reciprocal, k + 1)
                        V.tensor_tensor(o_tok[:, TPB * bb:TPB * bb + TPB, 2 * p:2 * p + 2, :], src[:, :, :, 0:LD],
                                        r.unsqueeze(3).to_broadcast([128, TPB, 2, LD]), ALU.mult).then_inc(s_l_normalised, 1)

                    rotated(0)
                    if l:
                        layer_added(l - 1, 1)
                    rotated(1)
                    rotated(2)
                    if l == 0:
                        stream_A(1)
                    scaled(0, l)
                    scaled(1, l)
                    if l == 0:
                        centred(1, 1, xT, 1)
                    rotated(3)
                    if l == 0:
                        normal_A(1)
                    scaled(2, l)
                    scaled(3, l)
                    rotated(4)
                    maxima(0)
                    rotated(5)
                    rotated(6)
                    quotient_B(0)
                    rotated(7)
                    scaled(4, l)
                    scaled(5, l)
                    quotient_B(1)
                    scaled(6, l)
                    scaled(7, l)
                    quotient_B(2)
                    quotient_B(3)
                    maxima(1)
                    def normal_B(b):
                        normal(2 + l, b, nT)
                        dve.wait_ge(s_normal, NB * (2 + l) + b + 1)
                        V.tensor_scalar(nT[:, cols(b)], nT[:, cols(b)], vcol[:, V_LG + l:V_LG + l + 1],
                                        vcol[:, V_LB + l:V_LB + l + 1], ALU.mult, ALU.add).then_inc(s_l_affine, 1)

                    def output_added(b):
                        dve.wait_ge(s_l_output, NB * l + b + 1)
                        V.tensor_tensor(fT[:, cols(b)], fT[:, cols(b)], bank[4 - 2 * b][:, cols(b)], ALU.add).then_inc(s_l_output_added, 1)
                        dve.wait_ge(s_l_output_added, NB * l + b + 1)
                        shifted(b)

                    output_added(0)
                    quotient_B(4)
                    centred(2 + l, 0, hflat, 4)
                    quotient_B(5)
                    quotient_B(6)
                    normal_B(0)
                    quotient_B(7)
                    def times_gelu(b, c):
                        w = HCH[c][1]
                        v = b1_column(l, 0, c)
                        dve.wait_ge(s_gelu, (NB * l + b) * len(HCH) + c + 1)
                        V.scalar_tensor_tensor(out=hid[0:w, c, cols(b)], in0=bank[ffb[b][c]][0:w, 0:N],
                                               scalar=vcol[0:w, v:v + 1], in1=gel[0:w, c, cols(b)],
                                               op0=ALU.add, op1=ALU.mult).then_inc(s_gated, 1)

                    times_gelu(0, 0)
                    output_added(1)
                    times_gelu(0, 1)
                    centred(2 + l, 1, hflat, 1)
                    times_gelu(0, 2)
                    normal_B(1)
                    layer_added(l, 0)
                    for c in range(len(HCH)):
                        times_gelu(1, c)
                layer_added(LAYERS - 1, 1)
                for b in range(NB):
                    centred(4, b, xT, b)
                for b in range(NB):
                    normal(4, b, nT)
                dve.wait_ge(s_c_query, 1)
                for b in range(NB):
                    V.tensor_scalar(qf_min[:, cols(b)], bank[0][:, cols(b)], 0.0, None, ALU.min).then_inc(s_c_q_min, 1)

                def feature_q(b):
                    dve.wait_ge(s_c_q_exp, b + 1)
                    V.scalar_tensor_tensor(out=qf[:, cols(b)], in0=bank[0][:, cols(b)], scalar=0.0, in1=qf_exp[:, cols(b)],
                                           op0=ALU.max, op1=ALU.add).then_inc(s_c_q_feature, 1)

                def times_q(t):
                    if t == 3:
                        dve.wait_ge(s_c_pool_sum, 3)
                    for half in range(2):
                        dve.wait_ge(s_c_running, 2 * t + half + 1)
                        q = qf[:, 128 * t + 64 * half:128 * t + 64 * half + 64].rearrange("p (h d) -> p h d", d=DH)
                        V.tensor_tensor(prod[:, t % 2, 512 * half:512 * half + 512].rearrange("p (h a d) -> p h a d", a=DH, d=DH),
                                        bank[run[t % 3] + half][:, :].rearrange("p (h a d) -> p h a d", a=DH, d=DH),
                                        q.unsqueeze(2).to_broadcast([128, H // 2, DH, DH]), ALU.mult).then_inc(s_c_times_q, 1)

                def quotient(t):
                    if t == 1:
                        dve.wait_ge(s_c_pool_sum, 3)
                    else:
                        dve.wait_ge(s_c_times_q, 2 * t + 2)
                        V.tensor_reduce(nv[:, t, :], prod[:, t % 2, :].rearrange("p (a d) -> p a d", d=DH), AX_X, ALU.add)\
                         .then_inc(s_c_summed, 1)
                        dve.wait_ge(s_c_summed, t + 1 if t == 0 else t)
                    if t == 0:
                        dve.wait_ge(s_c_newton, 2)
                    V.scalar_tensor_tensor(out=nv[:, t, :], in0=nv[:, t, :], scalar=-1.0,
                                           in1=rden[:, 128 * t:128 * t + 128], op0=ALU.mult, op1=ALU.mult)\
                     .then_inc(s_c_quotient, 1)

                feature_q(0)
                dve.wait_ge(s_c_q_feature, 1)
                times_q(0)
                feature_q(1)
                dve.wait_ge(s_c_q_feature, 2)
                dve.wait_ge(s_c_k_running, 1)
                V.tensor_tensor(den[:, :], qf[:, :], bank[1][:, :], ALU.mult).then_inc(s_c_denominator, 1)
                def stream_C(b):
                    dve.wait_ge(s_c_output, b + 1)
                    if b == 0:
                        dve.wait_ge(s_bias_added, 1)
                    V.scalar_tensor_tensor(out=xT[:, cols(b)], in0=bank[1 + 6 * b][:, cols(b)], scalar=tg[:, 1:2],
                                           in1=xT[:, cols(b)], op0=ALU.mult, op1=ALU.add).then_inc(s_stream, 1)

                times_q(1)
                dve.wait_ge(s_c_denominator_inverse, 1)
                V.scalar_tensor_tensor(out=den[:, :], in0=den[:, :], scalar=1e-6, in1=rden[:, :],
                                       op0=ALU.add, op1=ALU.mult).then_inc(s_c_newton, 1)
                dve.wait_ge(s_c_newton, 1)
                V.scalar_tensor_tensor(out=rden[:, :], in0=den[:, :], scalar=-2.0, in1=rden[:, :],
                                       op0=ALU.add, op1=ALU.mult).then_inc(s_c_newton, 1)
                quotient(0)
                times_q(2)
                quotient(1)
                times_q(3)
                quotient(2)
                stream_C(0)
                quotient(3)
                stream_C(1)
                for b in range(NB):
                    centred(5, b, xT, 4 + b)
                for b in range(NB):
                    normal(5, b, nT)
                dve.wait_ge(s_logits_exp, 1)
                V.tensor_scalar(flat(r_1), flat(r_e), 1.0, None, ALU.add).then_inc(s_affinity, 1)
                dve.wait_ge(s_affinity, 1)
                V.reciprocal(flat(aff), flat(r_1)).then_inc(s_affinity, 1)
                dve.wait_ge(s_affinity, 2)
                for t in range(T):
                    V.max(top[:, t, :], aff[:, t, :]).then_inc(s_top, 1)
                for t in range(T):
                    dve.wait_ge(s_top, t + 1)
                    V.match_replace(rep[:, t, :], top[:, t, :], aff[:, t, :], -1.0).then_inc(s_top, 1)
                V.tensor_reduce(tsum[:, :], top[:, :, :], AX_X, ALU.add).then_inc(s_weight, 1)
                dve.wait_ge(s_weight, 1)
                V.tensor_scalar(tsum[:, :], tsum[:, :], 1e-9, None, ALU.add).then_inc(s_weight, 1)
                dve.wait_ge(s_weight, 2)
                V.reciprocal(tinv[:, :], tsum[:, :]).then_inc(s_weight, 1)
                dve.wait_ge(s_top, 2 * T)
                V.scalar_tensor_tensor(out=flat(w_m), in0=flat(rep), scalar=-1.0, in1=flat(aff),
                                       op0=ALU.is_equal, op1=ALU.mult).then_inc(s_weight, 1)
                dve.wait_ge(s_weight, 4)
                V.tensor_tensor(w_t[:, :, :], w_m[:, :, :], tinv[:, :].unsqueeze(2).to_broadcast([128, T, E]), ALU.mult)\
                 .then_inc(s_weight, 1)
                dve.wait_ge(s_weight, 5)
                split(0, w_t[:, :, :], w_p[:, :, 0, :], w_p[:, :, 1, :], w_p[:, :, 2, :], w_res[:, :, :], s_weight_parts, 0)
                for n in range(PAIRS + 1):
                    m = 128 if n < PAIRS else I
                    v = V_BU + n if n < PAIRS else V_BUS
                    dve.wait_ge(s_e_silu, n + 1)
                    dve.wait_ge(s_e_up, n + 1)
                    if n >= 2:
                        dve.wait_ge(s_e_down, n - 1)
                    dst = up if n < PAIRS else hm
                    last = V.scalar_tensor_tensor(out=dst[0:m, n % 2, :], in0=bank[3 + 3 * (n % 2)][0:m, :],
                                                  scalar=vcol[0:m, v:v + 1], in1=sg[0:m, n % 2, :],
                                                  op0=ALU.add, op1=ALU.mult)
                    last.then_inc(s_e_gated, 1)
                    dve.wait_ge(s_e_gated, n + 1)
                    if n < PAIRS:
                        dve.wait_ge(s_e_weights, n + 1)
                        V.tensor_tensor(hm[:, n % 2, :], up[:, n % 2, :], bank[4 + 3 * (n % 2)][:, :], ALU.mult)\
                         .then_inc(s_e_weighted, 1)
                    else:
                        V.sem_inc(s_e_weighted, 1)
                dve.wait_ge(s_e_down, PAIRS + 1)
                dve.wait_ge(s_bias_added, 2)
                for b in range(NB):
                    V.scalar_tensor_tensor(out=xT[:, cols(b)], in0=bank[0][:, cols(b)], scalar=tg[:, 3:4],
                                           in1=xT[:, cols(b)], op0=ALU.mult, op1=ALU.add).then_inc(s_final, 1)
                dve.wait_ge(s_final_out, NB)
                dve.drain().then_inc(s_end_dve, 1)


_OUT = ((B, N, D), "float32")


def kernel(**inputs):
    import numpy as _np
    import ml_dtypes as _ml
    import concourse.bacc as _bacc
    from concourse import mybir as _mybir
    from concourse.bass_utils import run_bass_kernel_spmd as _run

    nc = _bacc.Bacc("TRN2", target_bir_lowering=False, num_devices=1)
    c_f32, c_bf16 = shape_constants()
    arrays, args = {}, {}
    for name, v in list(inputs.items()) + [("c_f32", c_f32), ("c_bf16", c_bf16.astype(_ml.bfloat16))]:
        v = _np.ascontiguousarray(v)
        arrays[f"in_{name}"] = v
        args[name] = nc.dram_tensor(f"in_{name}", v.shape, _mybir.dt.from_np(v.dtype), kind="ExternalInput").ap()
    shape, dtype = _OUT
    out = nc.dram_tensor("out_0", shape, _mybir.dt.from_np(_np.dtype(dtype)), kind="ExternalOutput").ap()
    flamingo(nc, args, out)
    r = _run(nc, [arrays], core_ids=[0])
    return r.results[0]["out_0"]
```
